# Optimizing a Trainium2 kernel written in Bass

```python
import numpy as np
import jax
import jax.numpy as jnp

def _softmax(x, axis=-1):
    return jax.nn.softmax(x, axis=axis)

def _gelu(x):
    return jax.nn.gelu(x, approximate=True)

def _silu(x):
    return jax.nn.silu(x)

def _sigmoid(x):
    return jax.nn.sigmoid(x)

def _layernorm(x, axis=-1, eps=1e-05):
    m = jnp.mean(x, axis=axis, keepdims=True)
    v = jnp.var(x, axis=axis, keepdims=True)
    return (x - m) / jnp.sqrt(v + eps)

def _scatter_add(tgt, idx, src, axis=0):
    return tgt.at[idx].add(src)

def _segment_sum(src, seg, n):
    return jax.ops.segment_sum(src, seg, n)
kernel_name = 'mk_conv_seq_d4_conv_nchw128_r2_a26876'

def setup_inputs(seed: int=0):
    np.random.seed(seed)
    _w = jnp.asarray

    def _rec_inputs():
        import jax
        import jax.numpy as jnp
        _gk = jax.random.key(seed)
        x = -0.0005207 + 1.001 * jax.random.normal(jax.random.fold_in(_gk, 1), (4, 64, 32, 32), jnp.float32)
        return x
    x = _rec_inputs()

    def _L0_conv_setup():
        import jax, jax.numpy as jnp
        import numpy as np
        B, C, H, W = (4, 64, 32, 32)

        def conv1x1(x, w, b):
            return jnp.einsum('bchw,oc->bohw', x, w) + b[None, :, None, None]

        def spatial_attention(x, w1, b1, w2, b2, w3, b3, alpha):
            Bb, Cc, Hh, Ww = x.shape
            N = Hh * Ww
            b_ = conv1x1(x, w1, b1).reshape(Bb, Cc, N)
            c_ = conv1x1(x, w2, b2).reshape(Bb, Cc, N)
            d_ = conv1x1(x, w3, b3).reshape(Bb, Cc, N)
            scores = jnp.einsum('bci,bcj->bij', c_, b_)
            A = jax.nn.softmax(scores, axis=1)
            attn = jnp.einsum('bcj,bkj->bck', d_, A)
            return x + alpha * attn.reshape(Bb, Cc, Hh, Ww)
        key = jax.random.key(seed)
        ks = jax.random.split(key, 12)
        s = 1.0 / np.sqrt(C)

        def wb(k1, k2):
            return (jax.random.uniform(k1, (C, C), jnp.float32, -s, s), jax.random.uniform(k2, (C,), jnp.float32, -s, s))
        x = jax.random.normal(ks[0], (B, C, H, W), jnp.float32)
        w1, b1 = wb(ks[1], ks[2])
        w2, b2 = wb(ks[3], ks[4])
        w3, b3 = wb(ks[5], ks[6])
        wd1, bd1 = wb(ks[7], ks[8])
        wd2, bd2 = wb(ks[9], ks[10])
        alpha = jax.random.normal(ks[11], (), jnp.float32) * 0.1
        return {'x': x, 'w1': w1, 'b1': b1, 'w2': w2, 'b2': b2, 'w3': w3, 'b3': b3, 'wd1': wd1, 'bd1': bd1, 'wd2': wd2, 'bd2': bd2, 'alpha': alpha}
    _L0_conv_all = _L0_conv_setup()
    _L0_conv_in = {k: v for k, v in _L0_conv_all.items() if k in ('w1', 'b1', 'w2', 'b2', 'w3', 'b3', 'wd1', 'bd1', 'wd2', 'bd2', 'alpha')}
    del _L0_conv_all

    def _L1_conv_setup():
        import jax, jax.numpy as jnp
        import numpy as np
        NBITS = 3
        BN_EPS = 1e-05

        def lsq_quantize(w, alpha):
            Qn = -2 ** (NBITS - 1)
            Qp = 2 ** (NBITS - 1) - 1
            g = 1.0 / jnp.sqrt(float(w.size) * Qp)
            alpha_s = alpha * g + jax.lax.stop_gradient(alpha - alpha * g)
            wc = jnp.clip(w / alpha_s, Qn, Qp)
            wq = wc + jax.lax.stop_gradient(jnp.round(wc) - wc)
            return wq * alpha_s

        def conv3x3_decomposed(x, wq):
            B, C, H, W = x.shape
            xp = jnp.pad(x, ((0, 0), (0, 0), (1, 1), (1, 1)))
            out = jnp.zeros((B, wq.shape[0], H, W), dtype=x.dtype)
            for kh in range(3):
                for kw in range(3):
                    out = out + jnp.einsum('bchw,oc->bohw', xp[:, :, kh:kh + H, kw:kw + W], wq[:, :, kh, kw])
            return out

        def batchnorm(x, gamma, beta):
            mean = jnp.mean(x, axis=(0, 2, 3), keepdims=True)
            var = jnp.var(x, axis=(0, 2, 3), keepdims=True)
            xhat = (x - mean) * jax.lax.rsqrt(var + BN_EPS)
            return gamma[None, :, None, None] * xhat + beta[None, :, None, None]
        key = jax.random.key(seed)
        ks = jax.random.split(key, 4)
        B, C, H, W = (32, 64, 56, 56)
        x = jax.random.normal(ks[0], (B, C, H, W), dtype=jnp.float32)
        w1 = jax.random.normal(ks[1], (C, C, 3, 3), dtype=jnp.float32) * 0.05
        w2 = jax.random.normal(ks[2], (C, C, 3, 3), dtype=jnp.float32) * 0.05
        alpha1 = jnp.array([0.02], dtype=jnp.float32)
        alpha2 = jnp.array([0.02], dtype=jnp.float32)
        gamma1 = jnp.ones((C,), dtype=jnp.float32)
        beta1 = jnp.zeros((C,), dtype=jnp.float32)
        gamma2 = jnp.ones((C,), dtype=jnp.float32)
        beta2 = jnp.zeros((C,), dtype=jnp.float32)
        return {'x': x, 'w1': w1, 'alpha1': alpha1, 'gamma1': gamma1, 'beta1': beta1, 'w2': w2, 'alpha2': alpha2, 'gamma2': gamma2, 'beta2': beta2}
    _L1_conv_all = _L1_conv_setup()
    _L1_conv_in = {k: v for k, v in _L1_conv_all.items() if k in ('w1', 'alpha1', 'gamma1', 'beta1', 'w2', 'alpha2', 'gamma2', 'beta2')}
    del _L1_conv_all

    def _L2_conv_setup():
        import jax, jax.numpy as jnp
        import numpy as np
        A_BIT = 4
        W_BIT = 4
        EPS = 1e-05
        L_TH = 2

        def _pattern_mask():
            m = np.ones((3, 3), np.float32)
            m[0, 0] = 0.0
            m[2, 2] = 0.0
            return jnp.asarray(m)

        def ste_round(x):
            return x + jax.lax.stop_gradient(jnp.round(x) - x)

        def qfn(x, k):
            n = float(2 ** k - 1)
            return ste_round(x * n) / n

        def act_quant(x, k):
            return qfn(jnp.clip(x, 0.0, 1.0), k)

        def weight_quant(w, k):
            t = jnp.tanh(w)
            t = t / (2.0 * jnp.max(jnp.abs(t))) + 0.5
            return 2.0 * qfn(t, k) - 1.0

        def bn_eval(x, gamma, beta, mean, var):
            inv = gamma / jnp.sqrt(var + EPS)
            return x * inv[None, :, None, None] + (beta - mean * inv)[None, :, None, None]

        def conv3x3(x, w):
            return jax.lax.conv_general_dilated(x, w, window_strides=(1, 1), padding=[(1, 1), (1, 1)], dimension_numbers=('NCHW', 'OIHW', 'NCHW'))
        key = jax.random.key(seed)
        ks = jax.random.split(key, 8)
        B, C, H, W = (64, 64, 32, 32)
        x = jax.random.normal(ks[0], (B, C, H, W), jnp.float32)
        w1 = jax.random.normal(ks[1], (C, C, 3, 3), jnp.float32) * 0.05
        w2 = jax.random.normal(ks[2], (C, C, 3, 3), jnp.float32) * 0.05
        gamma1 = jnp.ones((C,), jnp.float32)
        beta1 = jnp.zeros((C,), jnp.float32)
        mean1 = jax.random.normal(ks[3], (C,), jnp.float32) * 0.1
        var1 = jax.random.uniform(ks[4], (C,), jnp.float32, 0.5, 1.5)
        gamma2 = jnp.ones((C,), jnp.float32)
        beta2 = jnp.zeros((C,), jnp.float32)
        mean2 = jax.random.normal(ks[5], (C,), jnp.float32) * 0.1
        var2 = jax.random.uniform(ks[6], (C,), jnp.float32, 0.5, 1.5)
        return dict(x=x, w1=w1, w2=w2, gamma1=gamma1, beta1=beta1, mean1=mean1, var1=var1, gamma2=gamma2, beta2=beta2, mean2=mean2, var2=var2)
    _L2_conv_all = _L2_conv_setup()
    _L2_conv_in = {k: v for k, v in _L2_conv_all.items() if k in ('w1', 'w2', 'gamma1', 'beta1', 'mean1', 'var1', 'gamma2', 'beta2', 'mean2', 'var2')}
    del _L2_conv_all

    def _L3_conv_setup():
        import jax, jax.numpy as jnp
        import numpy as np
        EPS = 1e-05

        def _bn_train(h, gamma, beta):
            m = h.mean(axis=(0, 2, 3), keepdims=True)
            v = ((h - m) ** 2).mean(axis=(0, 2, 3), keepdims=True)
            return gamma[None, :, None, None] * (h - m) / jnp.sqrt(v + EPS) + beta[None, :, None, None]

        def _box_conv(h, x_min, x_max, y_min, y_max):
            B, Cc, H, W = h.shape
            nb = x_min.shape[1]
            K = Cc * nb
            II = jnp.pad(jnp.cumsum(jnp.cumsum(h, axis=2), axis=3), ((0, 0), (0, 0), (1, 0), (1, 0)))
            cidx = jnp.arange(K) // nb
            IIc = II[:, cidx]
            rows = jnp.arange(H, dtype=h.dtype)
            cols = jnp.arange(W, dtype=h.dtype)
            u_lo = x_min.reshape(-1)
            u_hi = x_max.reshape(-1) + 1.0
            v_lo = y_min.reshape(-1)
            v_hi = y_max.reshape(-1) + 1.0

            def F(u_off, v_off):
                u = jnp.clip(rows[None, :] + u_off[:, None], 0.0, float(H))
                v = jnp.clip(cols[None, :] + v_off[:, None], 0.0, float(W))
                u0f = jnp.floor(u)
                au = u - u0f
                v0f = jnp.floor(v)
                av = v - v0f
                u0 = u0f.astype(jnp.int32)
                u1 = jnp.minimum(u0 + 1, H)
                v0 = v0f.astype(jnp.int32)
                v1 = jnp.minimum(v0 + 1, W)
                R0 = jnp.take_along_axis(IIc, u0[None, :, :, None], axis=2)
                R1 = jnp.take_along_axis(IIc, u1[None, :, :, None], axis=2)
                R = R0 * (1.0 - au)[None, :, :, None] + R1 * au[None, :, :, None]
                C0 = jnp.take_along_axis(R, v0[None, :, None, :], axis=3)
                C1 = jnp.take_along_axis(R, v1[None, :, None, :], axis=3)
                return C0 * (1.0 - av)[None, :, None, :] + C1 * av[None, :, None, :]
            return F(u_hi, v_hi) - F(u_lo, v_hi) - F(u_hi, v_lo) + F(u_lo, v_lo)
        key = jax.random.key(seed)
        ks = jax.random.split(key, 8)
        B, C, H, W = (4, 64, 80, 80)
        nb = 4
        Cbt = C // nb
        x = jax.random.normal(ks[0], (B, C, H, W), dtype=jnp.float32)
        w1 = jax.random.normal(ks[1], (Cbt, C), dtype=jnp.float32) * (1.0 / np.sqrt(C))
        g1 = jnp.ones((Cbt,), jnp.float32)
        b1 = jnp.zeros((Cbt,), jnp.float32)
        x_min = -jax.random.uniform(ks[2], (Cbt, nb), jnp.float32, 1.0, H / 2.0)
        x_max = jax.random.uniform(ks[3], (Cbt, nb), jnp.float32, 1.0, H / 2.0)
        y_min = -jax.random.uniform(ks[4], (Cbt, nb), jnp.float32, 1.0, W / 2.0)
        y_max = jax.random.uniform(ks[5], (Cbt, nb), jnp.float32, 1.0, W / 2.0)
        g2 = jnp.ones((C,), jnp.float32)
        b2 = jnp.zeros((C,), jnp.float32)
        return {'x': x, 'w1': w1, 'g1': g1, 'b1': b1, 'x_min': x_min, 'x_max': x_max, 'y_min': y_min, 'y_max': y_max, 'g2': g2, 'b2': b2}
    _L3_conv_all = _L3_conv_setup()
    _L3_conv_in = {k: v for k, v in _L3_conv_all.items() if k in ('w1', 'g1', 'b1', 'x_min', 'x_max', 'y_min', 'y_max', 'g2', 'b2')}
    del _L3_conv_all
    return {'x': x, 'L0_conv_w1': _L0_conv_in['w1'], 'L0_conv_b1': _L0_conv_in['b1'], 'L0_conv_w2': _L0_conv_in['w2'], 'L0_conv_b2': _L0_conv_in['b2'], 'L0_conv_w3': _L0_conv_in['w3'], 'L0_conv_b3': _L0_conv_in['b3'], 'L0_conv_wd1': _L0_conv_in['wd1'], 'L0_conv_bd1': _L0_conv_in['bd1'], 'L0_conv_wd2': _L0_conv_in['wd2'], 'L0_conv_bd2': _L0_conv_in['bd2'], 'L0_conv_alpha': _L0_conv_in['alpha'], 'L1_conv_w1': _L1_conv_in['w1'], 'L1_conv_alpha1': _L1_conv_in['alpha1'], 'L1_conv_gamma1': _L1_conv_in['gamma1'], 'L1_conv_beta1': _L1_conv_in['beta1'], 'L1_conv_w2': _L1_conv_in['w2'], 'L1_conv_alpha2': _L1_conv_in['alpha2'], 'L1_conv_gamma2': _L1_conv_in['gamma2'], 'L1_conv_beta2': _L1_conv_in['beta2'], 'L2_conv_w1': _L2_conv_in['w1'], 'L2_conv_w2': _L2_conv_in['w2'], 'L2_conv_gamma1': _L2_conv_in['gamma1'], 'L2_conv_beta1': _L2_conv_in['beta1'], 'L2_conv_mean1': _L2_conv_in['mean1'], 'L2_conv_var1': _L2_conv_in['var1'], 'L2_conv_gamma2': _L2_conv_in['gamma2'], 'L2_conv_beta2': _L2_conv_in['beta2'], 'L2_conv_mean2': _L2_conv_in['mean2'], 'L2_conv_var2': _L2_conv_in['var2'], 'L3_conv_w1': _L3_conv_in['w1'], 'L3_conv_g1': _L3_conv_in['g1'], 'L3_conv_b1': _L3_conv_in['b1'], 'L3_conv_x_min': _L3_conv_in['x_min'], 'L3_conv_x_max': _L3_conv_in['x_max'], 'L3_conv_y_min': _L3_conv_in['y_min'], 'L3_conv_y_max': _L3_conv_in['y_max'], 'L3_conv_g2': _L3_conv_in['g2'], 'L3_conv_b2': _L3_conv_in['b2']}

def reference(x, L0_conv_w1, L0_conv_b1, L0_conv_w2, L0_conv_b2, L0_conv_w3, L0_conv_b3, L0_conv_wd1, L0_conv_bd1, L0_conv_wd2, L0_conv_bd2, L0_conv_alpha, L1_conv_w1, L1_conv_alpha1, L1_conv_gamma1, L1_conv_beta1, L1_conv_w2, L1_conv_alpha2, L1_conv_gamma2, L1_conv_beta2, L2_conv_w1, L2_conv_w2, L2_conv_gamma1, L2_conv_beta1, L2_conv_mean1, L2_conv_var1, L2_conv_gamma2, L2_conv_beta2, L2_conv_mean2, L2_conv_var2, L3_conv_w1, L3_conv_g1, L3_conv_b1, L3_conv_x_min, L3_conv_x_max, L3_conv_y_min, L3_conv_y_max, L3_conv_g2, L3_conv_b2):
    import jax
    import jax.numpy as jnp

    def _L0_conv_ref(x, w1, b1, w2, b2, w3, b3, wd1, bd1, wd2, bd2, alpha):
        import jax, jax.numpy as jnp
        import numpy as np
        B, C, H, W = (4, 64, 32, 32)

        def conv1x1(x, w, b):
            return jnp.einsum('bchw,oc->bohw', x, w) + b[None, :, None, None]

        def spatial_attention(x, w1, b1, w2, b2, w3, b3, alpha):
            Bb, Cc, Hh, Ww = x.shape
            N = Hh * Ww
            b_ = conv1x1(x, w1, b1).reshape(Bb, Cc, N)
            c_ = conv1x1(x, w2, b2).reshape(Bb, Cc, N)
            d_ = conv1x1(x, w3, b3).reshape(Bb, Cc, N)
            scores = jnp.einsum('bci,bcj->bij', c_, b_)
            A = jax.nn.softmax(scores, axis=1)
            attn = jnp.einsum('bcj,bkj->bck', d_, A)
            return x + alpha * attn.reshape(Bb, Cc, Hh, Ww)
        e = spatial_attention(x, w1, b1, w2, b2, w3, b3, alpha)
        return conv1x1(e, wd1, bd1) + conv1x1(e, wd2, bd2)

    def _L1_conv_ref(x, w1, alpha1, gamma1, beta1, w2, alpha2, gamma2, beta2):
        import jax, jax.numpy as jnp
        import numpy as np
        NBITS = 3
        BN_EPS = 1e-05

        def lsq_quantize(w, alpha):
            Qn = -2 ** (NBITS - 1)
            Qp = 2 ** (NBITS - 1) - 1
            g = 1.0 / jnp.sqrt(float(w.size) * Qp)
            alpha_s = alpha * g + jax.lax.stop_gradient(alpha - alpha * g)
            wc = jnp.clip(w / alpha_s, Qn, Qp)
            wq = wc + jax.lax.stop_gradient(jnp.round(wc) - wc)
            return wq * alpha_s

        def conv3x3_decomposed(x, wq):
            B, C, H, W = x.shape
            xp = jnp.pad(x, ((0, 0), (0, 0), (1, 1), (1, 1)))
            out = jnp.zeros((B, wq.shape[0], H, W), dtype=x.dtype)
            for kh in range(3):
                for kw in range(3):
                    out = out + jnp.einsum('bchw,oc->bohw', xp[:, :, kh:kh + H, kw:kw + W], wq[:, :, kh, kw])
            return out

        def batchnorm(x, gamma, beta):
            mean = jnp.mean(x, axis=(0, 2, 3), keepdims=True)
            var = jnp.var(x, axis=(0, 2, 3), keepdims=True)
            xhat = (x - mean) * jax.lax.rsqrt(var + BN_EPS)
            return gamma[None, :, None, None] * xhat + beta[None, :, None, None]
        residual = x
        out = conv3x3_decomposed(x, lsq_quantize(w1, alpha1))
        out = jax.nn.relu(batchnorm(out, gamma1, beta1))
        out = conv3x3_decomposed(out, lsq_quantize(w2, alpha2))
        out = batchnorm(out, gamma2, beta2)
        out = jax.nn.relu(out + residual)
        return out

    def _L2_conv_ref(x, w1, w2, gamma1, beta1, mean1, var1, gamma2, beta2, mean2, var2):
        import jax, jax.numpy as jnp
        import numpy as np
        A_BIT = 4
        W_BIT = 4
        EPS = 1e-05
        L_TH = 2

        def _pattern_mask():
            m = np.ones((3, 3), np.float32)
            m[0, 0] = 0.0
            m[2, 2] = 0.0
            return jnp.asarray(m)

        def ste_round(x):
            return x + jax.lax.stop_gradient(jnp.round(x) - x)

        def qfn(x, k):
            n = float(2 ** k - 1)
            return ste_round(x * n) / n

        def act_quant(x, k):
            return qfn(jnp.clip(x, 0.0, 1.0), k)

        def weight_quant(w, k):
            t = jnp.tanh(w)
            t = t / (2.0 * jnp.max(jnp.abs(t))) + 0.5
            return 2.0 * qfn(t, k) - 1.0

        def bn_eval(x, gamma, beta, mean, var):
            inv = gamma / jnp.sqrt(var + EPS)
            return x * inv[None, :, None, None] + (beta - mean * inv)[None, :, None, None]

        def conv3x3(x, w):
            return jax.lax.conv_general_dilated(x, w, window_strides=(1, 1), padding=[(1, 1), (1, 1)], dimension_numbers=('NCHW', 'OIHW', 'NCHW'))
        mask = _pattern_mask()
        wq1 = weight_quant(w1, W_BIT) * mask
        out = act_quant(bn_eval(conv3x3(x, wq1), gamma1, beta1, mean1, var1), A_BIT)
        wq2 = weight_quant(w2, W_BIT) * mask
        out = bn_eval(conv3x3(out, wq2), gamma2, beta2, mean2, var2)
        out = out + x
        return act_quant(out, A_BIT)

    def _L3_conv_ref(x, w1, g1, b1, x_min, x_max, y_min, y_max, g2, b2):
        import jax, jax.numpy as jnp
        import numpy as np
        EPS = 1e-05

        def _bn_train(h, gamma, beta):
            m = h.mean(axis=(0, 2, 3), keepdims=True)
            v = ((h - m) ** 2).mean(axis=(0, 2, 3), keepdims=True)
            return gamma[None, :, None, None] * (h - m) / jnp.sqrt(v + EPS) + beta[None, :, None, None]

        def _box_conv(h, x_min, x_max, y_min, y_max):
            B, Cc, H, W = h.shape
            nb = x_min.shape[1]
            K = Cc * nb
            II = jnp.pad(jnp.cumsum(jnp.cumsum(h, axis=2), axis=3), ((0, 0), (0, 0), (1, 0), (1, 0)))
            cidx = jnp.arange(K) // nb
            IIc = II[:, cidx]
            rows = jnp.arange(H, dtype=h.dtype)
            cols = jnp.arange(W, dtype=h.dtype)
            u_lo = x_min.reshape(-1)
            u_hi = x_max.reshape(-1) + 1.0
            v_lo = y_min.reshape(-1)
            v_hi = y_max.reshape(-1) + 1.0

            def F(u_off, v_off):
                u = jnp.clip(rows[None, :] + u_off[:, None], 0.0, float(H))
                v = jnp.clip(cols[None, :] + v_off[:, None], 0.0, float(W))
                u0f = jnp.floor(u)
                au = u - u0f
                v0f = jnp.floor(v)
                av = v - v0f
                u0 = u0f.astype(jnp.int32)
                u1 = jnp.minimum(u0 + 1, H)
                v0 = v0f.astype(jnp.int32)
                v1 = jnp.minimum(v0 + 1, W)
                R0 = jnp.take_along_axis(IIc, u0[None, :, :, None], axis=2)
                R1 = jnp.take_along_axis(IIc, u1[None, :, :, None], axis=2)
                R = R0 * (1.0 - au)[None, :, :, None] + R1 * au[None, :, :, None]
                C0 = jnp.take_along_axis(R, v0[None, :, None, :], axis=3)
                C1 = jnp.take_along_axis(R, v1[None, :, None, :], axis=3)
                return C0 * (1.0 - av)[None, :, None, :] + C1 * av[None, :, None, :]
            return F(u_hi, v_hi) - F(u_lo, v_hi) - F(u_hi, v_lo) + F(u_lo, v_lo)
        h = jnp.einsum('oc,bchw->bohw', w1, x)
        h = jax.nn.relu(_bn_train(h, g1, b1))
        h = _box_conv(h, x_min, x_max, y_min, y_max)
        h = _bn_train(h, g2, b2)
        return jax.nn.relu(x + h)

    def _gn(v, G=32, eps=1e-05):
        B_, C_, H_, W_ = v.shape
        g = v.reshape(B_, G, C_ // G, H_, W_)
        m = jnp.mean(g, axis=(2, 3, 4), keepdims=True)
        s = jnp.var(g, axis=(2, 3, 4), keepdims=True)
        return ((g - m) / jnp.sqrt(s + eps)).reshape(v.shape)

    def _ln_c(v, eps=1e-06):
        m = jnp.mean(v, axis=1, keepdims=True)
        s = jnp.var(v, axis=1, keepdims=True)
        return (v - m) / jnp.sqrt(s + eps)

    def _ln_t(v, eps=1e-05):
        m = jnp.mean(v, axis=-1, keepdims=True)
        s = jnp.var(v, axis=-1, keepdims=True)
        return (v - m) / jnp.sqrt(s + eps)

    def _to_tokens(v):
        B_, C_, H_, W_ = v.shape
        return v.reshape(B_, C_, H_ * W_).transpose(0, 2, 1)

    def _from_tokens(t, like):
        B_, C_, H_, W_ = like.shape
        return t.transpose(0, 2, 1).reshape(B_, C_, H_, W_)
    x = _L0_conv_ref(x, L0_conv_w1, L0_conv_b1, L0_conv_w2, L0_conv_b2, L0_conv_w3, L0_conv_b3, L0_conv_wd1, L0_conv_bd1, L0_conv_wd2, L0_conv_bd2, L0_conv_alpha)
    x = _L1_conv_ref(x, L1_conv_w1, L1_conv_alpha1, L1_conv_gamma1, L1_conv_beta1, L1_conv_w2, L1_conv_alpha2, L1_conv_gamma2, L1_conv_beta2)
    x = _L2_conv_ref(x, L2_conv_w1, L2_conv_w2, L2_conv_gamma1, L2_conv_beta1, L2_conv_mean1, L2_conv_var1, L2_conv_gamma2, L2_conv_beta2, L2_conv_mean2, L2_conv_var2)
    x = _L3_conv_ref(x, L3_conv_w1, L3_conv_g1, L3_conv_b1, L3_conv_x_min, L3_conv_x_max, L3_conv_y_min, L3_conv_y_max, L3_conv_g2, L3_conv_b2)
    return x

_drawn_inputs = setup_inputs


def setup_inputs(seed=0):
    import zlib

    import numpy as np

    out = dict(_drawn_inputs(seed))
    spreads = {'L1_conv_gamma1': (1.0, 0.2),
     'L1_conv_beta1': (0.0, 0.1),
     'L1_conv_gamma2': (1.0, 0.2),
     'L1_conv_beta2': (0.0, 0.1),
     'L2_conv_gamma1': (1.0, 0.2),
     'L2_conv_beta1': (0.0, 0.1),
     'L2_conv_gamma2': (1.0, 0.2),
     'L2_conv_beta2': (0.0, 0.1),
     'L3_conv_g1': (1.0, 0.6),
     'L3_conv_b1': (0.0, 0.393),
     'L3_conv_g2': (1.0, 0.2),
     'L3_conv_b2': (0.0, 0.1)}
    factors = {'L0_conv_w1': 4.1,
     'L0_conv_b1': 5.16,
     'L0_conv_w2': 4.394,
     'L0_conv_w3': 3.988,
     'L0_conv_b3': 4.636}
    for name, (base, spread) in spreads.items():
        noise = np.random.default_rng([zlib.crc32(name.encode()), seed]).standard_normal(out[name].shape)
        drawn = base * np.exp(spread * noise) if base else spread * noise
        out[name] = jnp.asarray(drawn.astype(out[name].dtype))
    for name, factor in factors.items():
        out[name] = (out[name] * factor).astype(out[name].dtype)
    return out
```

```python
from contextlib import ExitStack

import concourse.bass as bass
from concourse import mybir

F32 = mybir.dt.float32
BF16 = mybir.dt.bfloat16
ALU = mybir.AluOpType
ACT = mybir.ActivationFunctionType
AX = mybir.AxisListType

NB, C, H, W = 4, 64, 32, 32
S2 = W // 2
HW = H * W
HALF = H * S2
JT = HW // 128
RP = H + 2
PAD = RP * S2
OC, BOX = 16, 4
EPS = 1e-5
MAGIC = 12582912.0
QN, QP = -4.0, 3.0
LEVELS = 15.0
LSQ_G = float((C * C * 9 * QP) ** -0.5)
MEAN_N = NB * HW

(P_B1, P_B2, P_B3, P_BD1, P_BD2, P_ALPHA, P_LA, P_L1G, P_L1B, P_L2G, P_L2B, P_L2M, P_L2V, P_G1, P_BT1,
 P_G2, P_BT2, P_XMAX, P_XMIN, P_YMAX, P_YMIN, P_W1) = (
    0, 1, 2, 3, 4, 5, 6, 8, 10, 12, 14, 16, 18, 20, 21, 22, 38, 54, 118, 182, 246, 310)
P_COLS = 326
K_ID, K_AVG2, K_AVG8, K_AVGQ, K_IR, K_IR1, K_JW, K_JW1, K_MASK = 0, 128, 256, 384, 512, 544, 576, 608, 640
K_COLS = 644
WA_COLS = 512
NA, NBW = 384, 192
LAG = 2


def attention_uses():
    uses = [("B", 0), ("C", 0), ("D", 0)]
    for b in range(NB):
        for t in range(JT):
            uses.append(("S", b * JT + t))
            if b + 1 < NB and t in (2, 3, 4):
                uses.append(("BCD"[t - 2], b + 1))
    return uses


def build(nc, x, wa, wconv, par, cst, out):
    uses = attention_uses()
    by_act, by_dve = [], []
    for kind, _ in uses:
        by_act.append((by_act[-1] if by_act else 0) + (kind != "D"))
        by_dve.append((by_dve[-1] if by_dve else 0) + (kind == "D"))
    act_after = {u: by_act[n] for n, u in enumerate(uses)}
    slot_of = {u: n % 3 for n, u in enumerate(uses)}

    with ExitStack() as ctx:
        def sb(name, shape, dt=F32):
            return ctx.enter_context(nc.sbuf_tensor(name, [128] + shape, dt))

        def sem(name):
            return ctx.enter_context(nc.semaphore(name))

        def sems(name, n):
            return [sem(f"{name}{i}") for i in range(n)]

        parm = sb("parm", [P_COLS])
        consts = sb("consts", [K_COLS])
        ident_bf = sb("ident_bf", [128], BF16)
        wq = sb("wq", [4, 6, 128], BF16)
        part = [sb(f"part{i}", [NB, 2, PAD], BF16) for i in range(3)]
        res = sb("res", [2, 2 * PAD])
        y1 = sb("y1", [NB, 2, PAD])
        box_t = sb("box_t", [3, C * H])
        rows_w = sb("rows_w", [OC, BOX * H])
        w1f = sb("w1f", [OC])
        w1p = sb("w1p", [3, OC], BF16)
        wp = sb("wp", [3, 2 * OC], BF16)
        nb2 = sb("nb2", [1])
        bd = sb("bd", [1])
        lsq = sb("lsq", [2])
        lsq_r = sb("lsq_r", [2])
        lsq_t = sb("lsq_t", [2])
        wmax = sb("wmax", [2])
        wmax_all = sb("wmax_all", [2])
        wden = sb("wden", [2])
        ev = [sb(f"ev{i}", [2]) for i in range(8)]
        ev_scale = sb("ev_scale", [2])
        ev_bias = sb("ev_bias", [2])
        st = sb("st", [2, NB, 6])
        mv = sb("mv", [2, 2])
        bn = [sb(f"bn{i}", [2]) for i in range(12)]
        bn_a = sb("bn_a", [2])
        bn_b = sb("bn_b", [2])
        hst = sb("hst", [6])
        hmv = sb("hmv", [2])
        h1 = [sb(f"h1_{i}", [1]) for i in range(12)]
        h_a = sb("h_a", [1])
        h_b = sb("h_b", [1])
        st2 = sb("st2", [OC, 6])
        f1 = [sb(f"f1_{i}", [OC]) for i in range(12)]
        f_avgs = sb("f_avgs", [OC, 6])
        f_vars = sb("f_vars", [OC, 2])
        f_dev = sb("f_dev", [OC, 2])
        f_sq = sb("f_sq", [OC, 2])
        f_a = sb("f_a", [OC])
        f_b = sb("f_b", [OC])

        att = ExitStack()

        def sa(name, shape, dt=F32):
            return att.enter_context(nc.sbuf_tensor(name, [128] + shape, dt))

        wraw = sa("wraw", [4, NA + NBW])
        wtmp = sa("wtmp", [2, NA + NBW])
        xd = sa("xd", [NB, HW])
        x12 = sa("x12", [NB, HW], BF16)
        x13 = sa("x13", [NB, HW], BF16)
        rx = sa("rx", [HW])
        b32 = sa("b32", [HW])
        c32 = sa("c32", [HW])
        rb = sa("rb", [HW])
        rc = sa("rc", [HW])
        b11 = sa("b11", [2, HW], BF16)
        b22 = sa("b22", [2, HW], BF16)
        b31 = sa("b31", [2, HW], BF16)
        c12 = sa("c12", [2, HW], BF16)
        c13 = sa("c13", [2, HW], BF16)
        d32 = sa("d32", [2, JT, C])
        dz = sa("dz", [4, C])
        probs = sa("probs", [3, HW])
        nmax = sa("nmax", [NB * JT])
        zsum = sa("zsum", [NB * JT])
        rz = sa("rz", [NB * JT])
        wsrc = sa("wsrc", [WA_COLS - 256])
        wsp = sa("wsp", [384])
        wr = sa("wr", [384])
        w11 = sa("w11", [384], BF16)
        w22 = sa("w22", [384], BF16)
        w31 = sa("w31", [384], BF16)
        b3b = sa("b3b", [128])
        brow = sa("brow", [C])
        att.close()

        cols_blk = sb("cols_blk", [C, NB, W])
        y2 = sb("y2", [NB, 2, PAD])
        y3 = sb("y3", [NB, 2, PAD])
        tmp = sb("tmp", [2, HALF])
        tmpo = sb("tmpo", [2, HALF])
        x15 = sb("x15", [NB, HALF])
        xi = sb("xi", [NB, HALF], BF16)
        hs = sb("hs", [HALF])
        hblk = sb("hblk", [OC, 128])
        xf, fo, ts = (box_t[:, i, :].rearrange("q (o n) -> q o n", o=OC) for i in range(3))

        ps = ctx.enter_context(nc.psum_tensor("ps", [128, 8, 512], F32))

        def slot(u):
            n = slot_of[u]
            return ps[:, 2 * n:2 * n + 2, :].rearrange("q a n -> q (a n)")

        def blk(y, b, q0=0, q1=128):
            return y[q0:q1, b, 0, S2:S2 + HALF].rearrange("q (r s) -> q r s", s=S2)

        def shadow(y, b, half, skew):
            q0 = 64 * half
            first = 0 if (skew and half) else S2
            v = y[q0:q0 + 64, b, 1, first:first + HALF].rearrange("q (r s) -> q r s", s=S2)
            return (v[:, :, 1:S2], slice(0, S2 - 1)) if half else (v[:, :, 0:S2 - 1], slice(1, S2))

        x_in = sems("x_in", NB)
        x_cast, x_top, x_res, x_mid, x_parts = (sem(n) for n in ("x_cast", "x_top", "x_res", "x_mid", "x_parts"))
        b_hi, b_res, b_mid, b_lo, b_rep = (sem(n) for n in ("b_hi", "b_res", "b_mid", "b_lo", "b_rep"))
        c_hi, c_top, c_res, c_mid, c_lo = (sem(n) for n in ("c_hi", "c_top", "c_res", "c_mid", "c_lo"))
        par_in, wa_in, cst_in, wconv_in = (sem(n) for n in ("par_in", "wa_in", "cst_in", "wconv_in"))
        w_sum, w_fold, w_parts, biases = (sem(n) for n in ("w_sum", "w_fold", "w_parts", "biases"))
        act_step, d_done = sem("act_step"), sem("d_done")
        bc_ready, d_ready, s_ready = sem("bc_ready"), sem("d_ready"), sem("s_ready")
        max_ready, rz_ready, dz_ready, pv_done = sem("max_ready"), sem("rz_ready"), sem("dz_ready"), sem("pv_done")
        gen, p1_done, p2_done, p3_done, r_done = (sems(n, 3) for n in (
            "gen", "p1_done", "p2_done", "p3_done", "r_done"))
        conv_done = sems("conv_done", 4)
        wq_ready = sems("wq_ready", 4)
        wq_zero, y1_zero, y2_zero, y3_zero, hblk_zero = (sem(n) for n in (
            "wq_zero", "y1_zero", "y2_zero", "y3_zero", "hblk_zero"))
        tanh_done, wmax_part, wmax_done = sem("tanh_done"), sem("wmax_part"), sem("wmax_done")
        rows_ready, cols_ready, cols_placed = sem("rows_ready"), sem("cols_ready"), sem("cols_placed")
        wp_ready, id_ready = sem("wp_ready"), sem("id_ready")
        ev_var, ev_sqrt, ev_ready = sem("ev_var"), sem("ev_sqrt"), sem("ev_ready")
        bn_mv, bn_avg, bn_var, bn_sqrt, bn_ready = (sems(n, 2) for n in (
            "bn_mv", "bn_avg", "bn_var", "bn_sqrt", "bn_ready"))
        sum_ready = sem("sum_ready")
        q_relu, q_int, q_ready = sem("q_relu"), sem("q_int"), sem("q_ready")
        x15_ready, o_sum, o_clip, xi_ready = sem("x15_ready"), sem("o_sum"), sem("o_clip"), sem("xi_ready")
        h_raw, h_mv, h_avg, h_var, h_vavg, h_ve, h_sqrt, h_ab, h_ready = (sem(n) for n in (
            "h_raw", "h_mv", "h_avg", "h_var", "h_vavg", "h_ve", "h_sqrt", "h_ab", "h_ready"))
        tr_ready, hblk_act, hblk_dve = sem("tr_ready"), sem("hblk_act"), sem("hblk_dve")
        t_ready, ts_act, ts_dve, f_ready = sem("t_ready"), sem("ts_act"), sem("ts_dve"), sem("f_ready")
        xt_ready, xf_ready = sem("xt_ready"), sem("xf_ready")
        f_stat, f_avg, f_sqr, f_vavg, f_ve, f_sqrt, f_bias, f_xb, f_add, f_out = (sem(n) for n in (
            "f_stat", "f_avg", "f_sqr", "f_vavg", "f_ve", "f_sqrt", "f_bias", "f_xb", "f_add", "f_out"))
        chain = sem("dve_chain")
        pchain = sem("pool_chain")
        stored = sem("stored")

        block = ctx.enter_context(nc.Block())

        @block.sync
        def _(sp):
            sp.dma_start(xd[0:64, 0, :], x[:, 0:HW]).then_inc(x_in[0], 16)
            sp.dma_start(parm[:], par).then_inc(par_in, 16)
            sp.dma_start(consts[:], cst).then_inc(cst_in, 16)
            for b in range(1, NB):
                sp.dma_start(xd[0:64, b, :], x[:, b * HW:(b + 1) * HW]).then_inc(x_in[b], 16)
                sp.dma_start(xd[64:128, b, :], x[:, b * HW:(b + 1) * HW]).then_inc(x_in[b], 16)
            sp.dma_start(wraw[:].rearrange("q k n -> q (k n)"), wconv).then_inc(wconv_in, 16)
            for g in range(4):
                sp.wait_ge(f_out, g + 1)
                sp.dma_start(out[:, 512 * g:512 * (g + 1)],
                             fo[:, 4 * g:4 * g + 4, :].rearrange("q o n -> q (o n)")).then_inc(stored, 16)
            sp.wait_ge(stored, 64)

        @block.tensor
        def _(pe):
            mm = nc.tensor.matmul

            pe.wait_ge(w_sum, 2)
            pe.wait_ge(wa_in, 32)
            mm(ps[:, 7, 0:64], wsrc[0:64, 0:128], wsp[0:64, 256:320], start=True, stop=True)
            mm(ps[:, 7, 64:128], b3b[0:64, :], wsp[0:64, 256:320], start=True, stop=True).then_inc(w_fold, 1)
            pe.wait_ge(w_parts, 4)

            def wait_slot(n):
                if n >= 3:
                    if uses[n - 3][0] == "D":
                        pe.wait_ge(d_done, by_dve[n - 3])
                    else:
                        pe.wait_ge(act_step, by_act[n - 3])

            def project(n, kind, b):
                if kind == "B":
                    pe.wait_ge(x_top, b + 1)
                    pe.wait_ge(x_parts, b + 1)
                wait_slot(n)
                o = slot((kind, b))
                if kind == "D":
                    for t in range(JT):
                        cols = slice(128 * t, 128 * t + 128)
                        mm(o[:, 64 * t:64 * t + 64], x12[:, b, cols], w11[:, 320:384], start=True, stop=False)
                        mm(o[:, 64 * t:64 * t + 64], x12[:, b, cols], w22[:, 320:384], start=False, stop=False)
                        last = mm(o[:, 64 * t:64 * t + 64], x13[:, b, cols], w31[:, 320:384], start=False, stop=True)
                    last.then_inc(d_ready, 1)
                    return
                w0 = 0 if kind == "B" else 128
                for h in range(2):
                    cols = slice(512 * h, 512 * h + 512)
                    mm(o[:, cols], w11[:, w0:w0 + 128], x12[:, b, cols], start=True, stop=False)
                    mm(o[:, cols], w22[:, w0:w0 + 128], x12[:, b, cols], start=False, stop=False)
                    last = mm(o[:, cols], w31[:, w0:w0 + 128], x13[:, b, cols], start=False, stop=True)
                last.then_inc(bc_ready, 1)

            def scores(n, g):
                b, t = divmod(g, JT)
                if t == 0:
                    for s in (b_hi, b_mid, b_lo, b_rep, c_top, c_mid, c_lo):
                        pe.wait_ge(s, b + 1)
                wait_slot(n)
                o = slot(("S", g))
                j = slice(128 * t, 128 * t + 128)
                for w, m in ((b11, c12), (b22, c12), (b31, c13)):
                    for h in range(2):
                        last = mm(o[:, 512 * h:512 * h + 512], w[:, b % 2, j], m[:, b % 2, 512 * h:512 * h + 512],
                                  start=w is b11, stop=w is b31)
                last.then_inc(s_ready, 1)

            def values(g):
                b, t = divmod(g, JT)
                y = ps[:, 6 + b % 2, :]
                if t == 0:
                    if b >= 2:
                        pe.wait_ge(gen[0], 3 * (b - 1))
                    for w, m in ((w11, x12), (w22, x12), (w31, x13)):
                        for p in range(2):
                            mm(y[64 * p:64 * p + 64, :], w[:, 256:320], m[:, b, 512 * p:512 * p + 512],
                               start=w is w11, stop=False)
                pe.wait_ge(dz_ready, g + 1)
                for p in range(2):
                    last = mm(y[64 * p:64 * p + 64, :], dz[:, g % 4, :], probs[:, g % 3, 512 * p:512 * p + 512],
                              start=False, stop=t == JT - 1)
                last.then_inc(pv_done, 1)

            for n, (kind, i) in enumerate(uses):
                if kind == "S":
                    scores(n, i)
                    if i >= LAG:
                        values(i - LAG)
                else:
                    project(n, kind, i)
            for g in range(NB * JT - LAG, NB * JT):
                values(g)

            def convolve(k, b):
                bank = ps[:, 4 * (k % 2) + b, :]
                nbw = 3 if k < 2 else 2
                offs = [S2 * kh for kh in range(3)] + [S2 * kh for kh in range(nbw)]
                if b == 0:
                    pe.wait_ge(wq_ready[k], 5 if k < 2 else 7)
                nparts = 3 if k < 3 else 1
                if k == 3:
                    pe.wait_ge(q_ready, 3 * (b + 1))
                for i in range(nparts):
                    if k < 3:
                        pe.wait_ge((p1_done, p2_done, p3_done)[i][k], b + 1)
                    for j, off in enumerate(offs):
                        last = mm(bank, wq[:, k, j, :], part[i][:, b, int(j >= 3), off:off + HALF],
                                  start=i == 0 and j == 0, stop=i == nparts - 1 and j == len(offs) - 1)
                last.then_inc(conv_done[k], 1)

            for k in range(2):
                for b in range(NB):
                    convolve(k, b)
                pe.wait_ge(bn_mv[k], 1)
                mm(ps[:, 4 * (1 - k), 0:2], consts[:, K_AVG2:K_AVG2 + 128], mv[:, k, :],
                   start=True, stop=True).then_inc(bn_avg[k], 1)
            convolve(2, 0)
            for b in range(1, NB):
                convolve(2, b)
                convolve(3, b - 1)
            convolve(3, NB - 1)

            pe.wait_ge(wp_ready, 1)
            for b in range(NB):
                pe.wait_ge(xi_ready, b + 1)
                for i in range(3):
                    last = mm(ps[32 * b:32 * b + 32, 0, :], wp[:, i, :], xi[:, b, :], start=i == 0, stop=i == 2)
            last.then_inc(h_raw, 1)

            def residual(b, s):
                col = xi[:, b, :].rearrange("q (r s) -> q r s", s=S2)[:, :, s]
                pick = ident_bf[:].rearrange("q (p o x) -> q p o x", p=2, x=BOX)
                for x_ in range(BOX):
                    last = mm(ps[32 * x_:32 * x_ + 32, 4 + b, 32 * s:32 * s + 32], col, pick[:, :, :, x_],
                              start=True, stop=True)
                return last

            pe.wait_ge(h_mv, 1)
            mm(ps[:, 2, 0:2], consts[:, K_AVG8:K_AVG8 + 128], hmv[:], start=True, stop=True).then_inc(h_avg, 1)
            pe.wait_ge(h_var, 1)
            mm(ps[:, 2, 2:3], consts[:, K_AVG8:K_AVG8 + 128], h1[1][:], start=True, stop=True).then_inc(h_vavg, 1)
            pe.wait_ge(h_ready, 1)
            for sq in range(4):
                last = mm(ps[:, 1, 128 * sq:128 * sq + 128], hs[:, 128 * sq:128 * sq + 128], consts[:, K_ID:K_ID + 128], start=True, stop=True)
            last.then_inc(tr_ready, 1)
            pe.wait_ge(hblk_act, 2)
            pe.wait_ge(hblk_dve, 2)
            pe.wait_ge(rows_ready, 1)
            for o in range(OC):
                last = mm(ps[:, 4 + o // 4, 128 * (o % 4):128 * (o % 4) + 128], hblk[:, o, :], rows_w[:, o, :],
                          start=True, stop=True)
                if o % 4 == 3:
                    last.then_inc(t_ready, 1)
            pe.wait_ge(cols_placed, NB)
            for o in range(OC):
                if o % 4 == 0:
                    pe.wait_ge((ts_act, ts_dve)[(o // 4) % 2], o // 8 + 1)
                for x_ in range(BOX):
                    last = mm(ps[32 * x_:32 * x_ + 32, o // 4, 128 * (o % 4):128 * (o % 4) + 128],
                              ts[:, o, 32 * x_:32 * x_ + 32],
                              cols_blk[:, BOX * o + x_].rearrange("q b j -> q (b j)"),
                              start=True, stop=True)
                if o % 4 == 3:
                    last.then_inc(f_ready, 1)
            pe.wait_ge(id_ready, 1)
            pe.wait_ge(ts_act, 2)
            pe.wait_ge(ts_dve, 2)
            for b in range(NB):
                for s in range(S2):
                    last = residual(b, s)
                last.then_inc(xt_ready, 1)
            pe.wait_ge(f_stat, 1)
            pe.wait_ge(xf_ready, 1)
            mm(ps[:, 4, 0:96], consts[:, K_AVGQ:K_AVGQ + 128], st2[:].rearrange("q o n -> q (o n)"),
               start=True, stop=True).then_inc(f_avg, 1)
            pe.wait_ge(f_sqr, 1)
            mm(ps[:, 4, 96:128], consts[:, K_AVGQ:K_AVGQ + 128], f_sq[:].rearrange("q o n -> q (o n)"),
               start=True, stop=True).then_inc(f_vavg, 1)

        @block.scalar
        def _(act):
            act.dma_start(xd[64:128, 0, :], x[:, 0:HW]).then_inc(x_in[0], 16)
            act.dma_start(wsp[:, 0:256], wa[:, 0:256]).then_inc(wa_in, 16)
            act.dma_start(wsrc[:], wa[:, 256:512]).then_inc(wa_in, 16)

            def run(o, i, f, **kw):
                return nc.scalar.activation(o, i, f, **kw)

            def x_first(b):
                act.wait_ge(x_in[b], 32)
                run(x13[:, b, :], xd[:, b, :], ACT.Copy).then_inc(x_cast, 1)

            def project(kind, b):
                act.wait_ge(bc_ready, 2 * b + 1 + (kind == "C"))
                o = slot((kind, b))
                n = act_after[(kind, b)]
                if kind == "B":
                    act.wait_ge(par_in, 16)
                    run(b32[:], o, ACT.Identity, bias=parm[:, P_B1:P_B1 + 1]).then_inc(act_step, 1)
                    act.wait_ge(act_step, n)
                    run(b11[:, b % 2, :], b32[:], ACT.Copy).then_inc(b_hi, 1)
                    run(b31[64:128, b % 2, :], b32[64:128, :], ACT.Copy).then_inc(b_rep, 1)
                else:
                    act.wait_ge(biases, 2)
                    run(c32[:], o, ACT.Identity, bias=nb2[:], scale=-1.0).then_inc(act_step, 1)
                    act.wait_ge(act_step, n)
                    run(c12[0:64, b % 2, :], c32[0:64, :], ACT.Copy).then_inc(c_top, 1)

            def exponentials(g):
                act.wait_ge(max_ready, g + 1)
                if g >= 3:
                    act.wait_ge(pv_done, g - 2)
                run(probs[:, g % 3, :], slot(("S", g)), ACT.Exp, bias=nmax[:, g:g + 1], scale=-1.0,
                    accum_out=zsum[:, g:g + 1]).then_inc(act_step, 1)

            def copies(k, b, y, src, zeroed, skew, func, **kw):
                act.wait_ge(zeroed, 1)
                v = src.rearrange("q (r s) -> q r s", s=S2)
                run(blk(y, b), v, func, **{n: a[:] if hasattr(a, "dtype") else a for n, a in kw.items()})\
                    .then_inc(gen[k], 1)
                for half in range(2):
                    q = slice(64 * half, 64 * half + 64)
                    o, cols = shadow(y, b, half, skew)
                    run(o, v[q, :, cols], func, **{n: a[q] if hasattr(a, "dtype") else a for n, a in kw.items()})\
                        .then_inc(gen[k], 1)
                act.wait_ge(gen[k], 3 * (b + 1))
                run(part[0][:, b].rearrange("q a n -> q (a n)"), y[:, b].rearrange("q a n -> q (a n)"), ACT.Copy)\
                    .then_inc(p1_done[k], 1)

            def block0_out(b):
                act.wait_ge(pv_done, JT * (b + 1))
                copies(0, b, y1, ps[:, 6 + b % 2, :], y1_zero, False, ACT.Identity, bias=bd[:, 0:1])

            x_first(0)
            for kind, i in uses:
                if kind == "S":
                    b, t = divmod(i, JT)
                    if t == 0 and b + 1 < NB:
                        x_first(b + 1)
                    exponentials(i)
                    if t == 2 and b >= 1:
                        block0_out(b - 1)
                    if i == 5:
                        act.wait_ge(wconv_in, 16)
                        run(wraw[:, 2:4, 0:512], wraw[:, 2:4, 0:512], ACT.Tanh).then_inc(tanh_done, 1)
                elif kind != "D":
                    project(kind, i)
            block0_out(NB - 1)
            act.wait_ge(ev_var, 1)
            run(ev[1][:], ev[0][:], ACT.Sqrt).then_inc(ev_sqrt, 1)

            act.wait_ge(bn_var[0], 1)
            run(bn[4][:, 0:1], bn[3][:, 0:1], ACT.Sqrt).then_inc(bn_sqrt[0], 1)
            act.wait_ge(bn_ready[0], 1)
            for b in range(NB):
                copies(1, b, y2, ps[:, b, :], y2_zero, False, ACT.Relu, bias=bn_b[:, 0:1], scale=bn_a[:, 0:1])
            act.wait_ge(cols_ready, 1)
            for b in range(NB):
                run(cols_blk[:, :, b, :], box_t[:, 2, :].rearrange("q (k j) -> q k j", j=W), ACT.Copy,
                    scale=consts[:, K_MASK + b:K_MASK + b + 1]).then_inc(cols_placed, 1)
            act.wait_ge(bn_var[1], 1)
            run(bn[4][:, 1:2], bn[3][:, 1:2], ACT.Sqrt).then_inc(bn_sqrt[1], 1)
            act.wait_ge(bn_ready[1], 1)
            act.wait_ge(ev_ready, 1)

            def inner(b):
                act.wait_ge(conv_done[2], b + 1)
                if b >= 2:
                    act.wait_ge(q_ready, 3 * (b - 1))
                run(tmp[:, b % 2, :], ps[:, b, :], ACT.Relu, bias=ev_bias[:, 0:1], scale=ev_scale[:, 0:1])\
                    .then_inc(q_relu, 1)

            for b in range(NB):
                act.wait_ge(sum_ready, b + 1)
                copies(2, b, y3, tmp[:, b % 2, :], y3_zero, True, ACT.Relu, bias=bn_b[:, 1:2])
                if b == NB - 1:
                    inner(0)
                run(x15[:, b, :].rearrange("q (r s) -> q r s", s=S2), blk(y3, b), ACT.Identity,
                    bias=ev_bias[:, 1:2], scale=LEVELS).then_inc(x15_ready, 1)
            for b in range(1, NB):
                inner(b)

            act.wait_ge(h_ve, 1)
            run(h1[3][:], h1[2][:], ACT.Sqrt).then_inc(h_sqrt, 1)
            act.wait_ge(h_ab, 1)
            run(hs[:].rearrange("q (s r) -> q r s", r=H), ps[:, 0, :].rearrange("q (r s) -> q r s", s=S2), ACT.Relu,
                bias=h_b[:], scale=h_a[:]).then_inc(h_ready, 1)
            act.wait_ge(hblk_zero, 1)
            act.wait_ge(tr_ready, 1)
            for q in range(2):
                rows = slice(32 * q, 32 * q + 32)
                run(hblk[rows, :, rows], ps[rows, 1, :].rearrange("q (m o) -> q o m", o=OC), ACT.Copy)\
                    .then_inc(hblk_act, 1)
            for g in (0, 2):
                act.wait_ge(t_ready, g + 1)
                run(ts[:, 4 * g:4 * g + 4, :].rearrange("q o n -> q (o n)"), ps[:, 4 + g, :], ACT.Copy)\
                    .then_inc(ts_act, 1)
            for b in range(NB):
                act.wait_ge(xt_ready, b + 1)
                run(xf[:, :, 32 * b:32 * b + 32], ps[:, 4 + b, :].rearrange("q (j o) -> q o j", o=OC), ACT.Copy,
                    scale=1.0 / LEVELS).then_inc(xf_ready, 1)
            act.wait_ge(f_ve, 1)
            run(f1[4][:], f1[3][:], ACT.Sqrt).then_inc(f_sqrt, 1)

        @block.vector
        def _(dve):
            V = nc.vector
            links = [0]

            def link(ins):
                links[0] += 1
                ins.then_inc(chain, 1)
                dve.wait_ge(chain, links[0])

            def rstd(ve, s, work, scale_by, o):
                r, t, u = work
                link(V.reciprocal(r, s))
                link(V.tensor_tensor(t, ve, r, ALU.mult))
                link(V.tensor_tensor(t, t, r, ALU.mult))
                link(V.tensor_scalar(t, t, -0.5, 1.5, ALU.mult, ALU.add))
                link(V.tensor_tensor(u, r, t, ALU.mult))
                link(V.tensor_tensor(o, u, scale_by, ALU.mult))

            dve.wait_ge(par_in, 16)
            V.tensor_copy(b3b[:], parm[:, P_B3:P_B3 + 1].to_broadcast([128, 128])).then_inc(w_sum, 1)
            V.tensor_scalar(nb2[:], parm[:, P_B2:P_B2 + 1], -1.0, None, ALU.mult).then_inc(biases, 1)
            V.tensor_tensor(bd[:], parm[:, P_BD1:P_BD1 + 1], parm[:, P_BD2:P_BD2 + 1], ALU.add).then_inc(biases, 1)
            dve.wait_ge(wa_in, 32)
            V.tensor_tensor(wsp[:, 256:320], wsrc[:, 128:192], wsrc[:, 192:256], ALU.add).then_inc(w_sum, 1)

            def x_top_copy(b):
                dve.wait_ge(x_in[b], 32)
                V.tensor_copy(x12[0:64, b, :], xd[0:64, b, :]).then_inc(x_top, 1)

            def x_middle(b):
                dve.wait_ge(x_res, b + 1)
                V.tensor_copy(x12[64:128, b, :], rx[64:128, :]).then_inc(x_mid, 1)

            x_top_copy(0)
            dve.wait_ge(x_cast, 1)
            V.tensor_tensor(rx[64:128, :], xd[64:128, 0, :], x13[64:128, 0, :], ALU.subtract).then_inc(x_res, 1)
            x_middle(0)
            dve.wait_ge(w_fold, 1)
            alpha = parm[:, P_ALPHA:P_ALPHA + 1]
            link(V.tensor_scalar(wsp[:, 320:384], ps[:, 7, 0:64], alpha, None, ALU.mult))
            link(V.tensor_scalar(brow[:], ps[:, 7, 64:128], alpha, None, ALU.mult))
            V.tensor_copy(w11[:], wsp[:]).then_inc(w_parts, 1)
            dve.wait_ge(w_parts, 1)
            link(V.tensor_tensor(wr[:], wsp[:], w11[:], ALU.subtract))
            V.tensor_copy(w22[:], wr[:]).then_inc(w_parts, 1)
            dve.wait_ge(w_parts, 2)
            V.tensor_tensor(w31[0:64, :], wr[0:64, :], w22[0:64, :], ALU.subtract).then_inc(w_parts, 1)
            V.tensor_copy(w31[64:128, :], wsp[64:128, :]).then_inc(w_parts, 1)
            dve.wait_ge(x_mid, 1)
            V.tensor_tensor(x13[64:128, 0, :], rx[64:128, :], x12[64:128, 0, :], ALU.subtract).then_inc(x_parts, 1)

            def b_split(b):
                dve.wait_ge(b_hi, b + 1)
                V.tensor_tensor(rb[:], b32[:], b11[:, b % 2, :], ALU.subtract).then_inc(b_res, 1)
                dve.wait_ge(b_res, b + 1)
                V.tensor_copy(b22[:, b % 2, :], rb[:]).then_inc(b_mid, 1)
                dve.wait_ge(b_mid, b + 1)
                V.tensor_tensor(b31[0:64, b % 2, :], rb[0:64, :], b22[0:64, b % 2, :], ALU.subtract)\
                    .then_inc(b_lo, 1)

            def c_first(b):
                dve.wait_ge(act_step, act_after[("C", b)])
                V.tensor_copy(c13[:, b % 2, :], c32[:]).then_inc(c_hi, 1)

            def c_middle(b):
                dve.wait_ge(c_res, b + 1)
                V.tensor_copy(c12[64:128, b % 2, :], rc[64:128, :]).then_inc(c_mid, 1)

            def d_out(b):
                dve.wait_ge(d_ready, b + 1)
                if b >= 2:
                    dve.wait_ge(dz_ready, JT * (b - 1))
                V.tensor_tensor(d32[:, b % 2], slot(("D", b))[:, 0:512].rearrange("q (t c) -> q t c", c=C),
                                brow[:].unsqueeze(1).to_broadcast([128, JT, C]), ALU.add).then_inc(d_done, 1)

            def normalise(g):
                b, t = divmod(g, JT)
                dve.wait_ge(act_step, act_after[("S", g)])
                V.reciprocal(rz[:, g:g + 1], zsum[:, g:g + 1]).then_inc(rz_ready, 1)
                dve.wait_ge(rz_ready, g + 1)
                if t == 0:
                    dve.wait_ge(d_done, b + 1)
                if g >= 4:
                    dve.wait_ge(pv_done, g - 3)
                V.tensor_scalar(dz[:, g % 4, :], d32[:, b % 2, t, :], rz[:, g:g + 1], None, ALU.mult)\
                    .then_inc(dz_ready, 1)

            def split(k, b, y, last_part=True):
                r = res[:, b % 2, :]
                full = y[:, b].rearrange("q a n -> q (a n)")
                p = [part[i][:, b].rearrange("q a n -> q (a n)") for i in range(3)]
                dve.wait_ge(p1_done[k], b + 1)
                if last_part and b == NB - 1:
                    dve.wait_ge(p3_done[k], b)
                elif b >= 2:
                    dve.wait_ge(p3_done[k], b - 1)
                V.tensor_tensor(r, full, p[0], ALU.subtract).then_inc(r_done[k], 1)
                dve.wait_ge(r_done[k], b + 1)
                V.tensor_copy(p[1], r).then_inc(p2_done[k], 1)
                if last_part:
                    dve.wait_ge(p2_done[k], b + 1)
                    V.tensor_tensor(p[2], r, p[1], ALU.subtract).then_inc(p3_done[k], 1)

            def place_b(k, src, nbw):
                for half in range(2):
                    q = slice(64 * half, 64 * half + 64)
                    o = slice(64 * (1 - half), 64 * (1 - half) + 64)
                    yield wq[q, k, 3:3 + nbw, o], src[q, NA:NA + 64 * nbw].rearrange("q (a n) -> q a n", n=64)

            def lsq_weights():
                la = parm[:, P_LA:P_LA + 2]
                link(V.tensor_scalar(lsq_t[:], la, LSQ_G, None, ALU.mult))
                link(V.tensor_tensor(lsq[:], la, lsq_t[:], ALU.subtract))
                link(V.tensor_tensor(lsq[:], lsq_t[:], lsq[:], ALU.add))
                link(V.reciprocal(lsq_r[:], lsq[:]))
                link(V.tensor_tensor(bn[0][:], lsq[:], lsq[:], ALU.mult))
                link(V.tensor_tensor(bn[1][:], lsq[:], parm[:, P_L1G:P_L1G + 2], ALU.mult))
                dve.wait_ge(wconv_in, 16)
                dve.wait_ge(wq_zero, 1)
                for k in range(2):
                    w = wtmp[:, k, :]
                    link(V.tensor_scalar(w, wraw[:, k, :], lsq_r[:, k:k + 1], QP, ALU.mult, ALU.min))
                    link(V.tensor_scalar(w, w, QN, MAGIC, ALU.max, ALU.add))
                    V.tensor_scalar(wq[:, k, 0:3, :], w[:, 0:NA].rearrange("q (a n) -> q a n", n=128), MAGIC, None,
                                    ALU.subtract).then_inc(wq_ready[k], 3)
                    for o, i in place_b(k, w, 3):
                        V.tensor_scalar(o, i, MAGIC, None, ALU.subtract).then_inc(wq_ready[k], 1)

            def tanh_max():
                dve.wait_ge(tanh_done, 1)
                V.tensor_reduce(wmax[:], wraw[:, 2:4, 0:NA], AX.X, ALU.max, apply_absolute_value=True)\
                    .then_inc(wmax_part, 1)

            def tanh_weights():
                dve.wait_ge(wmax_done, 1)
                link(V.tensor_scalar(wden[:], wmax_all[:], 2.0, None, ALU.mult))
                link(V.reciprocal(wden[:], wden[:]))
                for k in range(2, 4):
                    n = NA + 128
                    w = wtmp[:, k - 2, 0:n]
                    dve.wait_ge(wq_ready[k - 2], 5)
                    link(V.tensor_scalar(w, wraw[:, k, 0:n], wden[:, k - 2:k - 1], 0.5, ALU.mult, ALU.add))
                    link(V.tensor_scalar(w, w, LEVELS, MAGIC, ALU.mult, ALU.add))
                    V.tensor_scalar(wq[:, k, 0:3, :], w[:, 0:NA].rearrange("q (a n) -> q a n", n=128), MAGIC,
                                    LEVELS / 2, ALU.subtract, ALU.subtract).then_inc(wq_ready[k], 3)
                    for o, i in place_b(k, w, 2):
                        V.tensor_scalar(o, i, MAGIC, LEVELS / 2, ALU.subtract, ALU.subtract).then_inc(wq_ready[k], 1)
                    dve.wait_ge(wq_ready[k], 5)
                    V.memset(wq[0:64, k, 0, 64:128], 0.0).then_inc(wq_ready[k], 1)
                    V.memset(wq[64:128, k, 2, 0:64], 0.0).then_inc(wq_ready[k], 1)

            for kind, i in uses:
                if kind == "B":
                    if i == 0:
                        b_split(0)
                elif kind == "C":
                    if i == 0:
                        c_first(0)
                        dve.wait_ge(c_hi, 1)
                        V.tensor_tensor(rc[64:128, :], c32[64:128, :], c13[64:128, 0, :], ALU.subtract)\
                            .then_inc(c_res, 1)
                        c_middle(0)
                        dve.wait_ge(c_mid, 1)
                        V.tensor_tensor(c13[64:128, 0, :], rc[64:128, :], c12[64:128, 0, :], ALU.subtract)\
                            .then_inc(c_lo, 1)
                elif kind == "D":
                    d_out(i)
                else:
                    b, t = divmod(i, JT)
                    dve.wait_ge(s_ready, i + 1)
                    V.tensor_reduce(nmax[:, i:i + 1], slot(("S", i)), AX.X, ALU.min).then_inc(max_ready, 1)
                    if i >= 1:
                        normalise(i - 1)
                    if b + 1 < NB:
                        if t == 1:
                            x_top_copy(b + 1)
                        elif t == 2:
                            x_middle(b + 1)
                        elif t == 3:
                            b_split(b + 1)
                        elif t == 4:
                            c_first(b + 1)
                        elif t == 6:
                            c_middle(b + 1)
                    if t == 5 and b >= 1:
                        split(0, b - 1, y1, last_part=False)
                    if i == 5:
                        tanh_max()
                    if i == 7:
                        lsq_weights()
                    if i == JT + 7:
                        tanh_weights()
            normalise(NB * JT - 1)
            split(0, NB - 1, y1)

            eg, eb, em, evv = (parm[:, p:p + 2] for p in (P_L2G, P_L2B, P_L2M, P_L2V))
            V.tensor_scalar(ev[0][:], evv, EPS, None, ALU.add).then_inc(ev_var, 1)
            dve.wait_ge(ev_sqrt, 1)
            rstd(ev[0][:], ev[1][:], (ev[2][:], ev[3][:], ev[4][:]), eg, ev[5][:])
            link(V.tensor_tensor(ev[6][:], em, ev[5][:], ALU.mult))
            link(V.tensor_tensor(ev[7][:], eb, ev[6][:], ALU.subtract))
            link(V.tensor_scalar(ev_bias[:], ev[7][:], LEVELS, None, ALU.mult))
            link(V.tensor_scalar(ev_scale[:, 0:1], ev[5][:, 0:1], 2.0, None, ALU.mult))
            V.tensor_scalar(ev_scale[:, 1:2], ev[5][:, 1:2], 2.0 / LEVELS, None, ALU.mult).then_inc(ev_ready, 1)
            dve.wait_ge(ev_ready, 1)

            def stats(k, b):
                dve.wait_ge(conv_done[k], b + 1)
                V.bn_stats(st[:, k, b, :], ps[:, 4 * k + b, :])

            def normalisation(k):
                c = slice(k, k + 1)
                avg = ps[:, 4 * (1 - k), 0:2]
                V.bn_aggr(mv[:, k, :], st[:, k].rearrange("q b n -> q (b n)")).then_inc(bn_mv[k], 1)
                dve.wait_ge(bn_avg[k], 1)
                dve.wait_ge(bn_mv[k], 1)
                link(V.tensor_tensor(bn[2][:, c], mv[:, k, 0:1], avg[:, 0:1], ALU.subtract))
                link(V.scalar_tensor_tensor(bn[6][:, c], bn[2][:, c], bn[2][:, c], avg[:, 1:2], ALU.mult, ALU.add))
                V.tensor_scalar(bn[3][:, c], bn[6][:, c], bn[0][:, c], EPS, ALU.mult, ALU.add).then_inc(bn_var[k], 1)
                link(V.tensor_scalar(bn[5][:, c], avg[:, 0:1], -1.0, None, ALU.mult))
                dve.wait_ge(bn_sqrt[k], 1)
                rstd(bn[3][:, c], bn[4][:, c], (bn[7][:, c], bn[8][:, c], bn[9][:, c]), bn[1][:, c], bn_a[:, c])
                V.scalar_tensor_tensor(bn_b[:, c], bn[5][:, c], bn_a[:, c], parm[:, P_L1B + k:P_L1B + k + 1],
                                       ALU.mult, ALU.add).then_inc(bn_ready[k], 1)
                dve.wait_ge(bn_ready[k], 1)

            def link_stats(k, b):
                dve.wait_ge(conv_done[k], b + 1)
                link(V.bn_stats(st[:, k, b, :], ps[:, 4 * k + b, :]))

            for b in range(NB):
                link_stats(0, b)
            normalisation(0)
            for b in range(3):
                split(1, b, y2)
            link_stats(1, 0)
            split(1, 3, y2)
            for b in range(1, NB):
                link_stats(1, b)
            normalisation(1)

            def add_residual(b):
                if b >= 2:
                    dve.wait_ge(gen[2], 3 * (b - 1))
                V.scalar_tensor_tensor(tmp[:, b % 2, :].rearrange("q (r s) -> q r s", s=S2),
                                       ps[:, 4 + b, :].rearrange("q (r s) -> q r s", s=S2), bn_a[:, 1:2],
                                       blk(y1, b), ALU.mult, ALU.add).then_inc(sum_ready, 1)

            def round_inner(b):
                v = tmp[:, b % 2, :]
                dve.wait_ge(q_relu, b + 1)
                V.tensor_scalar(v, v, LEVELS, MAGIC, ALU.min, ALU.add).then_inc(q_int, 1)
                dve.wait_ge(q_int, b + 1)
                v = v.rearrange("q (r s) -> q r s", s=S2)
                V.tensor_scalar(blk(part[0], b), v, MAGIC, None, ALU.subtract).then_inc(q_ready, 1)
                for half in range(2):
                    q = slice(64 * half, 64 * half + 64)
                    o, cols = shadow(part[0], b, half, True)
                    V.tensor_scalar(o, v[q, :, cols], MAGIC, None, ALU.subtract).then_inc(q_ready, 1)

            def outer(b):
                v = tmpo[:, b % 2, :]
                dve.wait_ge(conv_done[3], b + 1)
                dve.wait_ge(x15_ready, b + 1)
                if b >= 2:
                    dve.wait_ge(xi_ready, b - 1)
                V.scalar_tensor_tensor(v, ps[:, 4 + b, :], ev_scale[:, 1:2], x15[:, b, :], ALU.mult, ALU.add)\
                    .then_inc(o_sum, 1)
                dve.wait_ge(o_sum, b + 1)
                V.tensor_scalar(v, v, 0.0, LEVELS, ALU.max, ALU.min).then_inc(o_clip, 1)

            add_residual(0)
            add_residual(1)
            split(2, 0, y3)
            add_residual(2)
            split(2, 1, y3)
            add_residual(3)
            split(2, 2, y3)
            split(2, 3, y3)
            round_inner(0)
            round_inner(1)
            outer(0)
            round_inner(2)
            outer(1)
            round_inner(3)
            outer(2)
            outer(3)

            dve.wait_ge(h_raw, 1)
            link(V.bn_stats(hst[:], ps[:, 0, :]))
            V.bn_aggr(hmv[:], hst[:]).then_inc(h_mv, 1)
            dve.wait_ge(h_avg, 1)
            dve.wait_ge(h_mv, 1)
            link(V.tensor_tensor(h1[0][:], hmv[:, 0:1], ps[:, 2, 0:1], ALU.subtract))
            link(V.tensor_scalar(h1[4][:], ps[:, 2, 0:1], -1.0, None, ALU.mult))
            link(V.tensor_scalar(h1[9][:], parm[:, P_G1:P_G1 + 1], 1.0 / LEVELS, None, ALU.mult))
            V.scalar_tensor_tensor(h1[1][:], h1[0][:], h1[0][:], hmv[:, 1:2], ALU.mult, ALU.add).then_inc(h_var, 1)
            dve.wait_ge(h_vavg, 1)
            V.tensor_scalar(h1[2][:], ps[:, 2, 2:3], LEVELS ** -2, EPS, ALU.mult, ALU.add).then_inc(h_ve, 1)
            dve.wait_ge(h_sqrt, 1)
            rstd(h1[2][:], h1[3][:], (h1[5][:], h1[6][:], h1[7][:]), h1[9][:], h_a[:])
            V.scalar_tensor_tensor(h_b[:], h1[4][:], h_a[:], parm[:, P_BT1:P_BT1 + 1], ALU.mult, ALU.add)\
                .then_inc(h_ab, 1)
            dve.wait_ge(hblk_zero, 1)
            dve.wait_ge(tr_ready, 1)
            for q in range(2, 4):
                rows = slice(32 * q, 32 * q + 32)
                V.tensor_copy(hblk[rows, :, rows], ps[rows, 1, :].rearrange("q (m o) -> q o m", o=OC))\
                    .then_inc(hblk_dve, 1)
            dve.wait_ge(cols_placed, NB)
            for g in (1, 3):
                dve.wait_ge(t_ready, g + 1)
                V.tensor_copy(ts[:, 4 * g:4 * g + 4, :].rearrange("q o n -> q (o n)"), ps[:, 4 + g, :])\
                    .then_inc(ts_dve, 1)
            for o in range(OC):
                if o % 4 == 0:
                    dve.wait_ge(f_ready, o // 4 + 1)
                last = V.bn_stats(st2[:, o, :], ps[:, o // 4, 128 * (o % 4):128 * (o % 4) + 128])
            last.then_inc(f_stat, 1)
            dve.wait_ge(f_avg, 1)
            dve.wait_ge(f_stat, 1)
            link(V.tensor_copy(f_avgs[:], ps[:, 4, 0:96].rearrange("q (o n) -> q o n", n=6)))
            mean = f1[0]
            link(V.tensor_tensor(mean[:], f_avgs[:, :, 1], f_avgs[:, :, 4], ALU.add))
            link(V.tensor_tensor(f1[1][:], f_avgs[:, :, 2], f_avgs[:, :, 5], ALU.add))
            link(V.tensor_tensor(f_dev[:], st2[:, :, 1:5:3], mean[:].unsqueeze(2).to_broadcast([128, OC, 2]),
                                 ALU.subtract))
            V.tensor_tensor(f_sq[:], f_dev[:], f_dev[:], ALU.mult).then_inc(f_sqr, 1)
            dve.wait_ge(f_vavg, 1)
            link(V.tensor_copy(f_vars[:], ps[:, 4, 96:128].rearrange("q (o n) -> q o n", n=2)))
            link(V.tensor_tensor(f1[2][:], f_vars[:, :, 0], f_vars[:, :, 1], ALU.add))
            link(V.scalar_tensor_tensor(f1[5][:], f1[1][:], 1.0 / 64, f1[2][:], ALU.mult, ALU.add))
            V.tensor_scalar(f1[3][:], f1[5][:], EPS, None, ALU.add).then_inc(f_ve, 1)
            dve.wait_ge(f_sqrt, 1)
            rstd(f1[3][:], f1[4][:], (f1[6][:], f1[7][:], f1[8][:]), parm[:, P_G2:P_G2 + OC], f_a[:])
            link(V.tensor_tensor(f1[9][:], mean[:], f_a[:], ALU.mult))
            V.tensor_tensor(f_b[:], parm[:, P_BT2:P_BT2 + OC], f1[9][:], ALU.subtract).then_inc(f_bias, 1)
            for g in range(4):
                o = slice(4 * g, 4 * g + 4)
                link(V.tensor_tensor(fo[:, o, :], ps[:, g, :].rearrange("q (o n) -> q o n", n=128),
                                     f_a[:, o].unsqueeze(2).to_broadcast([128, 4, 128]), ALU.mult))
            for g in range(4):
                o = slice(4 * g, 4 * g + 4)
                dve.wait_ge(f_xb, g + 1)
                link(V.tensor_tensor(fo[:, o, :], fo[:, o, :], xf[:, o, :], ALU.add))
                V.tensor_scalar(fo[:, o, :], fo[:, o, :], 0.0, None, ALU.max).then_inc(f_out, 1)

        @block.gpsimd
        def _(pool):
            G = nc.gpsimd
            links = [0]

            def link(ins):
                links[0] += 1
                ins.then_inc(pchain, 1)
                pool.wait_ge(pchain, links[0])

            G.memset(wq[:], 0.0).then_inc(wq_zero, 1)
            pool.wait_ge(wq_zero, 1)
            G.memset(y1[:], 0.0).then_inc(y1_zero, 1)
            pool.wait_ge(y1_zero, 1)
            pool.wait_ge(cst_in, 16)
            G.tensor_copy(ident_bf[:], consts[:, K_ID:K_ID + 128]).then_inc(id_ready, 1)
            pool.wait_ge(id_ready, 1)

            pool.wait_ge(par_in, 16)
            w1 = parm[:, P_W1:P_W1 + OC]
            link(G.memset(wp[:], 0.0))
            link(G.tensor_copy(w1p[:, 0, :], w1))
            link(G.tensor_tensor(w1f[:], w1, w1p[:, 0, :], ALU.subtract))
            link(G.tensor_copy(w1p[:, 1, :], w1f[:]))
            link(G.tensor_tensor(w1p[:, 2, :], w1f[:], w1p[:, 1, :], ALU.subtract))
            link(G.tensor_copy(wp[0:64, :, 0:OC], w1p[0:64]))
            G.tensor_copy(wp[64:128, :, OC:2 * OC], w1p[64:128]).then_inc(wp_ready, 1)
            pool.wait_ge(wp_ready, 1)

            def x_low(b):
                pool.wait_ge(x_parts, b)
                pool.wait_ge(x_cast, b + 1)
                G.tensor_tensor(rx[64:128, :], xd[64:128, b, :], x13[64:128, b, :], ALU.subtract)\
                    .then_inc(x_res, 1)
                pool.wait_ge(x_mid, b + 1)
                G.tensor_tensor(x13[64:128, b, :], rx[64:128, :], x12[64:128, b, :], ALU.subtract)\
                    .then_inc(x_parts, 1)
                pool.wait_ge(x_parts, b + 1)

            def c_low(b):
                pool.wait_ge(c_hi, b + 1)
                G.tensor_tensor(rc[64:128, :], c32[64:128, :], c13[64:128, b % 2, :], ALU.subtract)\
                    .then_inc(c_res, 1)
                pool.wait_ge(c_mid, b + 1)
                G.tensor_tensor(c13[64:128, b % 2, :], rc[64:128, :], c12[64:128, b % 2, :], ALU.subtract)\
                    .then_inc(c_lo, 1)
                pool.wait_ge(c_lo, b + 1)

            def third_part(b):
                pool.wait_ge(p2_done[0], b + 1)
                G.tensor_tensor(part[2][:, b].rearrange("q a n -> q (a n)"), res[:, b % 2, :],
                                part[1][:, b].rearrange("q a n -> q (a n)"), ALU.subtract)\
                    .then_inc(p3_done[0], 1)
                pool.wait_ge(p3_done[0], b + 1)

            def edge(o, offset, table):
                v = box_t[:, o, :].rearrange("q (k j) -> q k j", j=W)
                link(G.tensor_tensor(v, parm[:, offset:offset + C].unsqueeze(2).to_broadcast([128, C, W]),
                                     consts[:, table:table + W].unsqueeze(1).to_broadcast([128, C, W]), ALU.add))
                link(G.tensor_scalar(v, v, 0.0, 1.0, ALU.max, ALU.min))

            x_low(1)
            edge(0, P_XMAX, K_IR1)
            c_low(1)
            pool.wait_ge(wmax_part, 1)
            G.partition_all_reduce(wmax_all[:], wmax[:], 128, bass.bass_isa.ReduceOp.max).then_inc(wmax_done, 1)
            pool.wait_ge(wmax_done, 1)
            x_low(2)
            edge(1, P_XMIN, K_IR)
            c_low(2)
            third_part(0)
            x_low(3)
            c_low(3)
            third_part(1)
            G.tensor_tensor(rows_w[:].rearrange("q o n -> q (o n)"), box_t[:, 0, :], box_t[:, 1, :], ALU.subtract)\
                .then_inc(rows_ready, 1)
            pool.wait_ge(rows_ready, 1)
            third_part(2)
            edge(0, P_YMAX, K_JW1)
            edge(1, P_YMIN, K_JW)
            G.tensor_tensor(box_t[:, 2, :], box_t[:, 0, :], box_t[:, 1, :], ALU.subtract).then_inc(cols_ready, 1)
            pool.wait_ge(cols_ready, 1)
            pool.wait_ge(pv_done, NB * JT)
            for k in range(4):
                pool.wait_ge(wq_ready[k], 5 if k < 2 else 7)
            G.memset(y2[:], 0.0).then_inc(y2_zero, 1)
            pool.wait_ge(y2_zero, 1)
            G.memset(y3[:], 0.0).then_inc(y3_zero, 1)
            pool.wait_ge(y3_zero, 1)
            G.memset(hblk[:], 0.0).then_inc(hblk_zero, 1)
            pool.wait_ge(hblk_zero, 1)
            for b in range(NB):
                pool.wait_ge(o_clip, b + 1)
                G.tensor_scalar(xi[:, b, :], tmpo[:, b % 2, :], MAGIC, MAGIC, ALU.add, ALU.subtract)\
                    .then_inc(xi_ready, 1)
                pool.wait_ge(xi_ready, b + 1)
            pool.wait_ge(f_bias, 1)
            pool.wait_ge(xf_ready, NB)
            for g in range(4):
                o = slice(4 * g, 4 * g + 4)
                G.tensor_tensor(xf[:, o, :], xf[:, o, :], f_b[:, o].unsqueeze(2).to_broadcast([128, 4, 128]), ALU.add)\
                    .then_inc(f_xb, 1)
                pool.wait_ge(f_xb, g + 1)


def constants():
    import numpy as np

    k = np.zeros((128, K_COLS), np.float32)
    q = np.arange(128)
    k[:, K_ID:K_ID + 128] = np.eye(128)
    k[:, K_AVG2:K_AVG2 + 128] = (q[:, None] % 64 == q[None] % 64) / 2
    k[:, K_AVG8:K_AVG8 + 128] = (q[:, None] % 16 == q[None] % 16) / 8
    k[:, K_AVGQ:K_AVGQ + 128] = (q[:, None] // 32 == q[None] // 32) / 64
    n = np.arange(32)
    r = q % 32
    w = 8 * (q // 8 % 4) + 2 * (q // 32) + q % 2
    k[:, K_IR:K_IR + 32] = n - r[:, None]
    k[:, K_IR1:K_IR1 + 32] = n - r[:, None] + 1
    k[:, K_JW:K_JW + 32] = n - w[:, None]
    k[:, K_JW1:K_JW1 + 32] = n - w[:, None] + 1
    k[:, K_MASK:K_MASK + 4] = (q[:, None] // 2 % 4) == np.arange(4)
    return k


def kernel(**inputs):
    import numpy as np
    import concourse.bacc as bacc
    from concourse.bass_utils import run_bass_kernel_spmd

    a = {n: np.asarray(v) for n, v in inputs.items()}
    x = a["x"].reshape(NB, C, H, S2, 2).transpose(1, 0, 4, 2, 3).reshape(C, NB * HW)

    def twice(m, axis=0):
        return np.concatenate([m, m], axis=axis)

    l0 = {n: a["L0_conv_" + n] for n in ("w1", "w2", "w3", "wd1", "wd2")}
    wa = np.concatenate([twice(twice(l0["w1"].T), 1), twice(twice(l0["w2"].T), 1), twice(twice(l0["w3"]), 1),
                         twice(l0["wd1"].T), twice(l0["wd2"].T)], axis=1)

    def taps(w, picks):
        t = w.transpose(1, 2, 3, 0)
        return np.concatenate([np.concatenate([t[:, kh, kw, :] for kh, kw in picks[p]], axis=1) for p in range(2)])

    col = {(0, 0): 1, (1, 0): 2, (0, 1): 0, (1, 1): 1}
    main = [[(kh, col[i, o]) for kh in range(3) for o in range(2)] for i in range(2)]
    side1 = [[(kh, 2) for kh in range(3)], [(kh, 0) for kh in range(3)]]
    side2 = [[(0, 2), (1, 2), (2, 2)], [(1, 0), (2, 0), (0, 0)]]
    wconv = np.concatenate([taps(a[n], [m + s for m, s in zip(main, side)]) for n, side in (
        ("L1_conv_w1", side1), ("L1_conv_w2", side1), ("L2_conv_w1", side2), ("L2_conv_w2", side2))], axis=1)

    def column(v, n=1):
        return np.tile(np.ravel(v), n)[:, None]

    def everywhere(v):
        return np.broadcast_to(np.ravel(v)[None], (128, np.size(v)))

    cols = [column(a["L0_conv_" + n], 2) for n in ("b1", "b2", "b3", "bd1", "bd2")]
    cols += [column(a[n], 128) for n in ("L0_conv_alpha", "L1_conv_alpha1", "L1_conv_alpha2")]
    cols += [column(a["L1_conv_" + n], 2) for n in ("gamma1", "gamma2", "beta1", "beta2")]
    cols += [column(a["L2_conv_" + n], 2) for n in (
        "gamma1", "gamma2", "beta1", "beta2", "mean1", "mean2", "var1", "var2")]
    cols += [column(a["L3_conv_" + n], 8) for n in ("g1", "b1")]
    cols += [np.repeat(a["L3_conv_" + n].reshape(OC, BOX).T, 32, axis=0) for n in ("g2", "b2")]
    cols += [everywhere(a["L3_conv_" + n]) for n in ("x_max", "x_min", "y_max", "y_min")]
    cols.append(twice(a["L3_conv_w1"].T))
    par = np.concatenate(cols, axis=1)

    sent = {"x": x, "wa": wa, "wconv": wconv, "par": par, "cst": constants()}
    sent = {n: np.ascontiguousarray(v) for n, v in sent.items()}
    nc = bacc.Bacc("TRN2", target_bir_lowering=False, num_devices=1)
    args = [nc.dram_tensor(n, v.shape, mybir.dt.from_np(v.dtype), kind="ExternalInput").ap() for n, v in sent.items()]
    args.append(nc.dram_tensor("out", (128, OC * 128), F32, kind="ExternalOutput").ap())
    build(nc, *args)
    r = run_bass_kernel_spmd(nc, [sent], core_ids=[0])
    got = r.results[0]["out"].reshape(BOX, H, OC, NB, W)
    return np.ascontiguousarray(got.transpose(3, 2, 0, 1, 4)).reshape(NB, C, H, W)
```

```python
from contextlib import ExitStack

import concourse.bass as bass
from concourse import mybir

F32 = mybir.dt.float32
BF16 = mybir.dt.bfloat16
ALU = mybir.AluOpType
ACT = mybir.ActivationFunctionType
AX = mybir.AxisListType

NB, C, H, W = 4, 64, 32, 32
S2 = W // 2
HW = H * W
HALF = H * S2
JT = HW // 128
RP = H + 2
PAD = RP * S2
OC, BOX = 16, 4
EPS = 1e-5
MAGIC = 12582912.0
QN, QP = -4.0, 3.0
LEVELS = 15.0
LSQ_G = float((C * C * 9 * QP) ** -0.5)
MEAN_N = NB * HW

(P_B1, P_B2, P_B3, P_BD1, P_BD2, P_ALPHA, P_LA, P_L1G, P_L1B, P_L2G, P_L2B, P_L2M, P_L2V, P_G1, P_BT1,
 P_G2, P_BT2, P_XMAX, P_XMIN, P_YMAX, P_YMIN, P_W1) = (
    0, 1, 2, 3, 4, 5, 6, 8, 10, 12, 14, 16, 18, 20, 21, 22, 38, 54, 118, 182, 246, 310)
P_COLS = 326
K_ID, K_AVG2, K_AVG8, K_AVGQ, K_IR, K_IR1, K_JW, K_JW1, K_MASK = 0, 128, 256, 384, 512, 544, 576, 608, 640
K_COLS = 644
WA_COLS = 512
NA, NBW = 384, 192
WARM = 10
RELU_ACT = 3
DIRECT = 4
B_AFTER, D_AFTER = 0, 5
PLAIN = 2
H_BANK, HT_BANK, AVG_BANK = 6, 4, 5
BANKS = ((6, 4, 5, 0), (7, 1, 2, 3))
LAG = 2


def c_after(b):
    return DIRECT - 1 if b == 0 else 2


def b_after(b):
    return 1 if b == 0 else B_AFTER


def attention_uses():
    uses = [("C", 0), ("B", 0)]
    for b in range(NB):
        for t in range(JT):
            uses.append(("S", b * JT + t))
            if b == 0 and t == 0:
                uses.append(("D", 0))
            if b + 1 < NB and t in (b_after(b), c_after(b), D_AFTER):
                uses.append(({b_after(b): "B", c_after(b): "C", D_AFTER: "D"}[t], b + 1))
    return uses


def build(nc, x, wa, wconv, par, cst, out):
    uses = attention_uses()
    by_act, by_dve = [], []
    for n, (kind, _) in enumerate(uses):
        by_act.append((by_act[-1] if by_act else 0) + (kind != "D" and n >= 2))
        by_dve.append((by_dve[-1] if by_dve else 0) + (kind == "D"))
    act_after = {u: by_act[n] for n, u in enumerate(uses)}
    slot_of = {u: n % 3 for n, u in enumerate(uses)}

    with ExitStack() as ctx:
        def sb(name, shape, dt=F32):
            return ctx.enter_context(nc.sbuf_tensor(name, [128] + shape, dt))

        def sem(name):
            return ctx.enter_context(nc.semaphore(name))

        def sems(name, n):
            return [sem(f"{name}{i}") for i in range(n)]

        parm = sb("parm", [P_COLS])
        consts = sb("consts", [K_COLS])
        ident_bf = sb("ident_bf", [128], BF16)
        wq = sb("wq", [4, 6, 128], BF16)
        parts = sb("parts", [3, NB, 2, PAD], BF16)
        res = sb("res", [2, HALF])
        y1 = sb("y1", [NB, HALF])
        box_t = sb("box_t", [3, C * H])
        rows_w = sb("rows_w", [OC, BOX * H])
        w1f = sb("w1f", [OC])
        w1p = sb("w1p", [3, OC], BF16)
        wp = sb("wp", [3, 2 * OC], BF16)
        nb2 = sb("nb2", [1])
        bd = sb("bd", [1])
        lsq = sb("lsq", [2])
        lsq_r = sb("lsq_r", [2])
        lsq_t = sb("lsq_t", [2])
        wmax = sb("wmax", [2])
        wmax_all = sb("wmax_all", [2])
        wden = sb("wden", [2])
        ev = [sb(f"ev{i}", [2]) for i in range(8)]
        ev_scale = sb("ev_scale", [2])
        ev_bias = sb("ev_bias", [2])
        st = sb("st", [2, NB, 6])
        mv = sb("mv", [2, 2])
        bn = [sb(f"bn{i}", [2]) for i in range(12)]
        bn_a = sb("bn_a", [2])
        bn_b = sb("bn_b", [2])
        hst = sb("hst", [6])
        hmv = sb("hmv", [2])
        h1 = [sb(f"h1_{i}", [1]) for i in range(12)]
        h_a = sb("h_a", [1])
        h_b = sb("h_b", [1])
        st2 = sb("st2", [OC, 6])
        f1 = [sb(f"f1_{i}", [OC]) for i in range(12)]
        f_avgs = sb("f_avgs", [OC, 6])
        f_vars = sb("f_vars", [OC, 2])
        f_dev = sb("f_dev", [OC, 2])
        f_sq = sb("f_sq", [OC, 2])
        f_a = sb("f_a", [OC])
        f_b = sb("f_b", [OC])

        att = ExitStack()

        def sa(name, shape, dt=F32):
            return att.enter_context(nc.sbuf_tensor(name, [128] + shape, dt))

        wraw = sa("wraw", [4, NA + NBW])
        wtmp = sa("wtmp", [2, NA + NBW])
        xd = sa("xd", [NB, HW])
        x12 = sa("x12", [NB - PLAIN, HW], BF16)
        x13 = sa("x13", [NB - PLAIN, HW], BF16)
        bhalf = sa("bhalf", [128 * DIRECT])
        rx = sa("rx", [HW])
        b32 = sa("b32", [HW])
        c32 = sa("c32", [HW])
        rb = sa("rb", [HW])
        rc = sa("rc", [HW])
        b11 = sa("b11", [2, HW], BF16)
        b22 = sa("b22", [2, HW], BF16)
        b31 = sa("b31", [2, HW], BF16)
        c12 = sa("c12", [2, HW], BF16)
        c13 = sa("c13", [2, HW], BF16)
        d32 = sa("d32", [2, JT, C])
        dz = sa("dz", [4, C])
        probs = sa("probs", [3, HW])
        nmax = sa("nmax", [NB * JT])
        zsum = sa("zsum", [NB * JT])
        rz = sa("rz", [NB * JT])
        wsrc = sa("wsrc", [WA_COLS - 256])
        wsp = sa("wsp", [384])
        wr = sa("wr", [384])
        whalf = sa("whalf", [384])
        w11 = sa("w11", [384], BF16)
        w22 = sa("w22", [384], BF16)
        w31 = sa("w31", [384], BF16)
        b3b = wr[:, 0:128]
        brow = sa("brow", [C])
        att.close()

        cols_blk = sb("cols_blk", [C, NB, W])
        y2 = sb("y2", [NB, HALF])
        y3 = sb("y3", [NB, HALF])
        tmp = sb("tmp", [2, HALF])
        tmpo = sb("tmpo", [2, HALF])
        x15 = sb("x15", [NB, HALF])
        xi = sb("xi", [NB, HALF], BF16)
        hs = sb("hs", [HALF])
        hblk = sb("hblk", [OC, 128])
        edge_buf = [rows_w[:].rearrange("q o n -> q (o n)")] + [box_t[:, i, :] for i in range(3)]
        xf, fo, ts = (box_t[:, i, :].rearrange("q (o n) -> q o n", o=OC) for i in range(3))

        ps = ctx.enter_context(nc.psum_tensor("ps", [128, 8, 512], F32))

        def slot(u):
            n = slot_of[u]
            return ps[:, 2 * n:2 * n + 2, :].rearrange("q a n -> q (a n)")

        y_of = (y1, y2, y3)

        def main(i, b):
            return parts[:, i, b, 0, S2:S2 + HALF]

        def side(i, b, half, skew):
            q = slice(64 * half, 64 * half + 64)
            first = 0 if (skew and half) else S2
            o = parts[q, i, b, 1, first:first + HALF].rearrange("q (r s) -> q r s", s=S2)
            to, of = (slice(1, S2), slice(0, S2 - 1)) if half else (slice(0, S2 - 1), slice(1, S2))

            def moved(t):
                return t[q].rearrange("q (r s) -> q r s", s=S2)[:, :, of]
            return o[:, :, to], moved

        x_in = sems("x_in", NB)
        x_cast, x_top, x_res, x_mid, x_parts = (sem(n) for n in ("x_cast", "x_top", "x_res", "x_mid", "x_parts"))
        b_hi, b_res, b_mid, b_lo, b_rep = (sem(n) for n in ("b_hi", "b_res", "b_mid", "b_lo", "b_rep"))
        c_hi, c_top, c_res, c_mid, c_lo = (sem(n) for n in ("c_hi", "c_top", "c_res", "c_mid", "c_lo"))
        par_in, wa_in, cst_in, wconv_in = (sem(n) for n in ("par_in", "wa_in", "cst_in", "wconv_in"))
        w_sum, w_fold, w_parts, biases = (sem(n) for n in ("w_sum", "w_fold", "w_parts", "biases"))
        warm_zero, w_half, first_ready, first_act, bhalf_ready = (sem(n) for n in (
            "warm_zero", "w_half", "first_ready", "first_act", "bhalf_ready"))
        wsrc_in, edge_sum, edge_clip = sem("wsrc_in"), sem("edge_sum"), sem("edge_clip")
        act_step, d_done = sem("act_step"), sem("d_done")
        bc_ready, d_ready, s_ready = sem("bc_ready"), sem("d_ready"), sem("s_ready")
        max_ready, rz_ready, dz_ready, pv_done = sem("max_ready"), sem("rz_ready"), sem("dz_ready"), sem("pv_done")
        gen = sems("gen", 3)
        main_done, side_done, r_done = sems("main_done", 3), sems("side_done", 3), sem("r_done")
        conv_done = sems("conv_done", 4)
        wq_ready = sems("wq_ready", 4)
        wq_zero, borders_zero, skew_zero, hblk_zero = (sem(n) for n in (
            "wq_zero", "borders_zero", "skew_zero", "hblk_zero"))
        tanh_done, wmax_part, wmax_done = sem("tanh_done"), sem("wmax_part"), sem("wmax_done")
        rows_ready, cols_ready, cols_placed = sem("rows_ready"), sem("cols_ready"), sem("cols_placed")
        wp_ready, id_ready = sem("wp_ready"), sem("id_ready")
        ev_var, ev_sqrt, ev_ready = sem("ev_var"), sem("ev_sqrt"), sem("ev_ready")
        bn_mv, bn_avg, bn_var, bn_sqrt, bn_ready = (sems(n, 2) for n in (
            "bn_mv", "bn_avg", "bn_var", "bn_sqrt", "bn_ready"))
        sum_ready = sem("sum_ready")
        q_relu, q_int, q_ready = sem("q_relu"), sem("q_int"), sem("q_ready")
        x15_ready, o_sum, o_clip, xi_ready = sem("x15_ready"), sem("o_sum"), sem("o_clip"), sem("xi_ready")
        h_raw, h_mv, h_avg, h_var, h_vavg, h_ve, h_sqrt, h_ab, h_ready = (sem(n) for n in (
            "h_raw", "h_mv", "h_avg", "h_var", "h_vavg", "h_ve", "h_sqrt", "h_ab", "h_ready"))
        tr_ready, hblk_act, hblk_dve = sem("tr_ready"), sem("hblk_act"), sem("hblk_dve")
        t_ready, ts_act, ts_dve, f_ready = sem("t_ready"), sem("ts_act"), sem("ts_dve"), sem("f_ready")
        xt_ready, xf_ready = sem("xt_ready"), sem("xf_ready")
        f_stat, f_avg, f_sqr, f_vavg, f_ve, f_sqrt, f_bias, f_xb, f_add, f_out = (sem(n) for n in (
            "f_stat", "f_avg", "f_sqr", "f_vavg", "f_ve", "f_sqrt", "f_bias", "f_xb", "f_add", "f_out"))
        chain = sem("dve_chain")
        pchain = sem("pool_chain")
        stored, f_out_dve = sem("stored"), sem("f_out_dve")

        warm = main(0, 0)

        block = ctx.enter_context(nc.Block())

        @block.sync
        def _(sp):
            sp.dma_start(xd[0:64, 0, :], x[:, 0:HW]).then_inc(x_in[0], 16)
            sp.dma_start(xd[64:128, 0, :], x[:, 0:HW]).then_inc(x_in[0], 16)
            sp.dma_start(consts[:], cst).then_inc(cst_in, 16)
            for b in range(1, NB):
                sp.dma_start(xd[0:64, b, :], x[:, b * HW:(b + 1) * HW]).then_inc(x_in[b], 16)
                sp.dma_start(xd[64:128, b, :], x[:, b * HW:(b + 1) * HW]).then_inc(x_in[b], 16)
            sp.dma_start(wraw[:].rearrange("q k n -> q (k n)"), wconv).then_inc(wconv_in, 16)
            for g in range(4):
                sp.wait_ge(f_out, RELU_ACT * (g + 1))
                sp.wait_ge(f_out_dve, (4 - RELU_ACT) * (g + 1))
                sp.dma_start(out[:, 512 * g:512 * (g + 1)],
                             fo[:, 4 * g:4 * g + 4, :].rearrange("q o n -> q (o n)")).then_inc(stored, 16)
            sp.wait_ge(stored, 64)

        @block.tensor
        def _(pe):
            mm = nc.tensor.matmul

            pe.wait_ge(warm_zero, 1)
            for _ in range(WARM):
                mm(ps[:, 6, :], warm[:, 0:128], warm, start=True, stop=True)

            def project_first(kind):
                o = slot((kind, 0))
                w0 = 0 if kind == "B" else 128
                for h in range(2):
                    cols = slice(512 * h, 512 * h + 512)
                    mm(o[:, cols], whalf[:, w0:w0 + 128], xd[:, 0, cols], start=True, stop=True).then_inc(first_ready, 1)

            def wait_slot(n):
                if n >= 3:
                    if n < 5:
                        pe.wait_ge(first_act, 2 * (n - 2))
                    elif uses[n - 3][0] == "D":
                        pe.wait_ge(d_done, by_dve[n - 3])
                    else:
                        pe.wait_ge(act_step, by_act[n - 3])

            def project(n, kind, b):
                if kind == "B" and b >= PLAIN:
                    pe.wait_ge(x_top, b - PLAIN + 1)
                    pe.wait_ge(x_parts, b - PLAIN + 1)
                    pe.wait_ge(w_parts, 4)
                elif b == 1:
                    pe.wait_ge(x_in[1], 32)
                wait_slot(n)
                o = slot((kind, b))
                if kind == "D":
                    if b == 0:
                        pe.wait_ge(w_half, 3)
                    for t in range(JT):
                        cols = slice(128 * t, 128 * t + 128)
                        v = o[:, 64 * t:64 * t + 64]
                        if b < PLAIN:
                            last = mm(v, xd[:, b, cols], whalf[:, 320:384], start=True, stop=True)
                            continue
                        mm(v, x12[:, b - PLAIN, cols], w11[:, 320:384], start=True, stop=False)
                        mm(v, x12[:, b - PLAIN, cols], w22[:, 320:384], start=False, stop=False)
                        last = mm(v, x13[:, b - PLAIN, cols], w31[:, 320:384], start=False, stop=True)
                    last.then_inc(d_ready, 1)
                    return
                w0 = 0 if kind == "B" else 128
                for h in range(2):
                    cols = slice(512 * h, 512 * h + 512)
                    if b < PLAIN:
                        last = mm(o[:, cols], whalf[:, w0:w0 + 128], xd[:, b, cols], start=True, stop=True)
                        continue
                    mm(o[:, cols], w11[:, w0:w0 + 128], x12[:, b - PLAIN, cols], start=True, stop=False)
                    mm(o[:, cols], w22[:, w0:w0 + 128], x12[:, b - PLAIN, cols], start=False, stop=False)
                    last = mm(o[:, cols], w31[:, w0:w0 + 128], x13[:, b - PLAIN, cols], start=False, stop=True)
                last.then_inc(bc_ready, 1)

            def scores(n, g):
                b, t = divmod(g, JT)
                if g == 0:
                    pe.wait_ge(first_act, 2)
                    pe.wait_ge(bhalf_ready, 1)
                elif g == DIRECT or t == 0:
                    for s in (b_hi, b_mid, b_lo, b_rep, c_top, c_hi, c_mid, c_lo):
                        pe.wait_ge(s, b + 1)
                wait_slot(n)
                if g < DIRECT:
                    for h in range(2):
                        cols = slice(512 * h, 512 * h + 512)
                        last = mm(slot(("S", g))[:, cols], bhalf[:, 128 * g:128 * g + 128], c32[:, cols],
                                  start=True, stop=True)
                    last.then_inc(s_ready, 1)
                    return
                o = slot(("S", g))
                j = slice(128 * t, 128 * t + 128)
                for w, m in ((b11, c12), (b22, c12), (b31, c13)):
                    for h in range(2):
                        last = mm(o[:, 512 * h:512 * h + 512], w[:, b % 2, j], m[:, b % 2, 512 * h:512 * h + 512],
                                  start=w is b11, stop=w is b31)
                last.then_inc(s_ready, 1)

            def values(g):
                b, t = divmod(g, JT)
                y = ps[:, 6 + b % 2, :]
                if t == 0:
                    if b >= 2:
                        pe.wait_ge(gen[0], b - 1)
                    terms = [(whalf, xd[:, b, :])] if b < PLAIN else \
                        [(w, m[:, b - PLAIN, :]) for w, m in ((w11, x12), (w22, x12), (w31, x13))]
                    for n, (w, m) in enumerate(terms):
                        for p in range(2):
                            mm(y[64 * p:64 * p + 64, :], w[:, 256:320], m[:, 512 * p:512 * p + 512],
                               start=n == 0, stop=False)
                pe.wait_ge(dz_ready, g + 1)
                for p in range(2):
                    last = mm(y[64 * p:64 * p + 64, :], dz[:, g % 4, :], probs[:, g % 3, 512 * p:512 * p + 512],
                              start=False, stop=t == JT - 1)
                last.then_inc(pv_done, 1)

            pe.wait_ge(x_in[0], 32)
            pe.wait_ge(w_half, 1)
            project_first("C")
            project_first("B")
            pe.wait_ge(w_sum, 2)
            mm(ps[:, 7, 0:64], wsrc[0:64, 0:128], wsp[0:64, 256:320], start=True, stop=True)
            mm(ps[:, 7, 64:128], b3b[0:64, :], wsp[0:64, 256:320], start=True, stop=True).then_inc(w_fold, 1)
            for n, (kind, i) in enumerate(uses):
                if n < 2:
                    continue
                if kind == "S":
                    scores(n, i)
                    if i >= LAG:
                        values(i - LAG)
                else:
                    project(n, kind, i)

            def convolve(k, b, i):
                bank = ps[:, BANKS[k % 2][b], :]
                nbw = 3 if k < 2 else 2
                last_part = 2 if k < 3 else 0
                n = NB * k + b
                if k == 3:
                    pe.wait_ge(q_ready, 3 * (b + 1))
                else:
                    pe.wait_ge(main_done[i], n + 1)
                for kh in range(3):
                    mm(bank, wq[:, k, kh, :], parts[:, i, b, 0, S2 * kh:S2 * kh + HALF],
                       start=i == 0 and kh == 0, stop=False)
                if k < 3:
                    pe.wait_ge(side_done[i], 2 * (n + 1))
                for kh in range(nbw):
                    last = mm(bank, wq[:, k, 3 + kh, :], parts[:, i, b, 1, S2 * kh:S2 * kh + HALF],
                              start=False, stop=i == last_part and kh == nbw - 1)
                if i == last_part:
                    last.then_inc(conv_done[k], 1)

            def average(k):
                pe.wait_ge(bn_mv[k], 1)
                mm(ps[:, BANKS[1 - k][0], 0:2], consts[:, K_AVG2:K_AVG2 + 128], mv[:, k, :],
                   start=True, stop=True).then_inc(bn_avg[k], 1)

            pe.wait_ge(wq_ready[0], 5)
            pe.wait_ge(borders_zero, 1)
            pe.wait_ge(gen[0], NB - 1)
            convolve(0, 0, 0)
            convolve(0, 0, 1)
            values(NB * JT - 2)
            convolve(0, 0, 2)
            values(NB * JT - 1)
            pe.wait_ge(act_step, act_after[("S", NB * JT - 1)])
            for b in range(1, NB):
                for i in range(3):
                    convolve(0, b, i)
            average(0)
            turns = ((0, 0), (0, 1), (1, 0), (0, 2), (1, 1), (2, 0), (1, 2), (2, 1), (3, 0), (2, 2), (3, 1), (3, 2))
            pe.wait_ge(wq_ready[1], 5)
            for b, i in turns:
                convolve(1, b, i)
            average(1)
            for k in range(2, 4):
                pe.wait_ge(wq_ready[k], 7)
            pe.wait_ge(skew_zero, 1)
            for b, i in turns:
                convolve(2, b, i)
                if (b, i) in ((3, 0), (3, 2)):
                    convolve(3, b - 3 + (i == 2), 0)
            convolve(3, 2, 0)
            convolve(3, 3, 0)

            pe.wait_ge(wp_ready, 1)
            pe.wait_ge(id_ready, 1)

            def residual(b, s):
                col = xi[:, b, :].rearrange("q (r s) -> q r s", s=S2)[:, :, s]
                pick = ident_bf[:].rearrange("q (p o x) -> q p o x", p=2, x=BOX)
                for x_ in range(BOX):
                    last = mm(ps[32 * x_:32 * x_ + 32, BANKS[1][b], 32 * s:32 * s + 32], col, pick[:, :, :, x_],
                              start=True, stop=True)
                return last

            for b in range(NB):
                pe.wait_ge(xi_ready, b + 1)
                for i in range(3):
                    last = mm(ps[32 * b:32 * b + 32, H_BANK, :], wp[:, i, :], xi[:, b, :], start=i == 0, stop=i == 2)
                if b == NB - 1:
                    last.then_inc(h_raw, 1)
                for s in range(S2):
                    last = residual(b, s)
                last.then_inc(xt_ready, 1)
            pe.wait_ge(h_mv, 1)
            mm(ps[:, AVG_BANK, 0:2], consts[:, K_AVG8:K_AVG8 + 128], hmv[:], start=True, stop=True).then_inc(h_avg, 1)
            pe.wait_ge(h_var, 1)
            mm(ps[:, AVG_BANK, 2:3], consts[:, K_AVG8:K_AVG8 + 128], h1[1][:], start=True, stop=True).then_inc(h_vavg, 1)
            pe.wait_ge(h_ready, 1)
            for sq in range(4):
                last = mm(ps[:, HT_BANK, 128 * sq:128 * sq + 128], hs[:, 128 * sq:128 * sq + 128], consts[:, K_ID:K_ID + 128], start=True, stop=True)
            last.then_inc(tr_ready, 1)
            pe.wait_ge(hblk_act, 2)
            pe.wait_ge(hblk_dve, 2)
            pe.wait_ge(rows_ready, 1)
            pe.wait_ge(xf_ready, NB)
            pe.wait_ge(cols_placed, NB)

            def box_rows(g):
                for o in range(4 * g, 4 * g + 4):
                    last = mm(ps[:, BANKS[1][g], 128 * (o % 4):128 * (o % 4) + 128], hblk[:, o, :], rows_w[:, o, :],
                              start=True, stop=True)
                last.then_inc(t_ready, 1)

            def box_columns(g):
                pe.wait_ge(ts_act, g + 1)
                for o in range(4 * g, 4 * g + 4):
                    for x_ in range(BOX):
                        last = mm(ps[32 * x_:32 * x_ + 32, BANKS[0][g], 128 * (o % 4):128 * (o % 4) + 128],
                                  ts[:, o, 32 * x_:32 * x_ + 32],
                                  cols_blk[:, BOX * o + x_].rearrange("q b j -> q (b j)"), start=True, stop=True)
                last.then_inc(f_ready, 1)

            box_rows(0)
            box_rows(1)
            box_columns(0)
            box_rows(2)
            box_columns(1)
            box_rows(3)
            box_columns(2)
            box_columns(3)
            pe.wait_ge(f_stat, 1)
            mm(ps[:, BANKS[1][0], 0:96], consts[:, K_AVGQ:K_AVGQ + 128], st2[:].rearrange("q o n -> q (o n)"),
               start=True, stop=True).then_inc(f_avg, 1)
            pe.wait_ge(f_sqr, 1)
            mm(ps[:, BANKS[1][0], 96:128], consts[:, K_AVGQ:K_AVGQ + 128], f_sq[:].rearrange("q o n -> q (o n)"),
               start=True, stop=True).then_inc(f_vavg, 1)

        @block.scalar
        def _(act):
            act.dma_start(wsp[:, 0:256], wa[:, 0:256]).then_inc(wa_in, 16)
            act.dma_start(parm[:], par).then_inc(par_in, 16)
            act.dma_start(wsrc[:], wa[:, 256:512]).then_inc(wsrc_in, 16)

            def run(o, i, f, **kw):
                return nc.scalar.activation(o, i, f, **kw)

            def x_first(b):
                act.wait_ge(x_in[b], 32)
                run(x13[:, b - PLAIN, :], xd[:, b, :], ACT.Copy).then_inc(x_cast, 1)

            def first_out(kind, h):
                cols = slice(512 * h, 512 * h + 512)
                act.wait_ge(first_ready, 1 + h + 2 * (kind == "B"))
                o = slot((kind, 0))[:, cols]
                if kind == "C":
                    act.wait_ge(biases, 2)
                    run(c32[:, cols], o, ACT.Identity, bias=nb2[:], scale=-1.0).then_inc(first_act, 1)
                else:
                    run(b32[:, cols], o, ACT.Identity, bias=parm[:, P_B1:P_B1 + 1]).then_inc(first_act, 1)

            def b_out(b):
                act.wait_ge(b_res, b)
                act.wait_ge(bc_ready, 2 * b - 1)
                run(b32[:], slot(("B", b)), ACT.Identity, bias=parm[:, P_B1:P_B1 + 1]).then_inc(act_step, 1)
                act.wait_ge(act_step, act_after[("B", b)])
                run(b11[:, b % 2, :], b32[:], ACT.Copy).then_inc(b_hi, 1)

            def b_repeat(b):
                run(b31[64:128, b % 2, :], b32[64:128, :], ACT.Copy).then_inc(b_rep, 1)

            def c_out(b):
                act.wait_ge(c_res, b)
                act.wait_ge(bc_ready, 2 * b)
                run(c32[:], slot(("C", b)), ACT.Identity, bias=nb2[:], scale=-1.0).then_inc(act_step, 1)

            def c_repeat(b):
                act.wait_ge(act_step, act_after[("C", b)])
                run(c12[0:64, b % 2, :], c32[0:64, :], ACT.Copy).then_inc(c_top, 1)

            def exponentials(g):
                act.wait_ge(max_ready, g + 1)
                if g >= 3:
                    act.wait_ge(pv_done, g - 2)
                run(probs[:, g % 3, :], slot(("S", g)), ACT.Exp, bias=nmax[:, g:g + 1], scale=-1.0,
                    accum_out=zsum[:, g:g + 1]).then_inc(act_step, 1)

            def image_out(k, b, src, func, **kw):
                run(main(0, b), src, func, **kw).then_inc(main_done[0], 1)
                run(y_of[k][:, b, :], src, func, **kw).then_inc(gen[k], 1)

            def block0_out(b):
                act.wait_ge(pv_done, JT * (b + 1))
                image_out(0, b, ps[:, 6 + b % 2, :], ACT.Identity, bias=bd[:])

            act.wait_ge(warm_zero, 1)
            run(zsum[:, 0:1], warm[:, 0:1], ACT.Exp)
            act.wait_ge(par_in, 16)
            first_out("C", 0)
            first_out("C", 1)
            first_out("B", 0)
            first_out("B", 1)
            act.wait_ge(first_act, 4)
            run(c12[0:64, 0, :], c32[0:64, :], ACT.Copy).then_inc(c_top, 1)
            run(b11[:, 0, :], b32[:], ACT.Copy).then_inc(b_hi, 1)
            run(b31[64:128, 0, :], b32[64:128, :], ACT.Copy).then_inc(b_rep, 1)
            for kind, i in uses:
                if kind != "S":
                    continue
                b, t = divmod(i, JT)
                if t == (3 if b == 0 else 0) and b + 2 < NB:
                    x_first(b + 2)
                exponentials(i)
                if b + 1 < NB:
                    if t == b_after(b):
                        b_out(b + 1)
                    if t == c_after(b):
                        c_out(b + 1)
                        b_repeat(b + 1)
                    if t == c_after(b) + 1:
                        c_repeat(b + 1)
                if t == 4 and b >= 1:
                    block0_out(b - 1)
                if i == NB * JT - 3:
                    act.wait_ge(wconv_in, 16)
                    run(wraw[:, 2:4, 0:512], wraw[:, 2:4, 0:512], ACT.Tanh).then_inc(tanh_done, 1)
            block0_out(NB - 1)
            act.wait_ge(ev_var, 1)
            run(ev[1][:], ev[0][:], ACT.Sqrt).then_inc(ev_sqrt, 1)

            act.wait_ge(bn_var[0], 1)
            run(bn[4][:, 0:1], bn[3][:, 0:1], ACT.Sqrt).then_inc(bn_sqrt[0], 1)
            act.wait_ge(bn_ready[0], 1)
            for b in range(NB):
                image_out(1, b, ps[:, BANKS[0][b], :], ACT.Relu, bias=bn_b[:, 0:1], scale=bn_a[:, 0:1])
            act.wait_ge(cols_ready, 1)
            act.wait_ge(wq_ready[3], 7)
            for b in range(NB):
                run(cols_blk[:, :, b, :], box_t[:, 2, :].rearrange("q (k j) -> q k j", j=W), ACT.Copy,
                    scale=consts[:, K_MASK + b:K_MASK + b + 1]).then_inc(cols_placed, 1)
            act.wait_ge(bn_var[1], 1)
            run(bn[4][:, 1:2], bn[3][:, 1:2], ACT.Sqrt).then_inc(bn_sqrt[1], 1)
            act.wait_ge(bn_ready[1], 1)
            act.wait_ge(ev_ready, 1)

            def inner(b):
                act.wait_ge(conv_done[2], b + 1)
                if b >= 2:
                    act.wait_ge(q_ready, 3 * (b - 1))
                run(tmp[:, b % 2, :], ps[:, BANKS[0][b], :], ACT.Relu, bias=ev_bias[:, 0:1], scale=ev_scale[:, 0:1])\
                    .then_inc(q_relu, 1)

            for b in range(NB):
                act.wait_ge(sum_ready, b + 1)
                image_out(2, b, tmp[:, b % 2, :], ACT.Relu, bias=bn_b[:, 1:2])
                act.wait_ge(main_done[0], 2 * NB + b + 1)
                for half in range(2):
                    o, moved = side(0, b, half, True)
                    run(o, moved(main(0, b)), ACT.Copy).then_inc(side_done[0], 1)
                if b == NB - 1:
                    inner(0)
                act.wait_ge(gen[2], b + 1)
                run(x15[:, b, :], y3[:, b, :], ACT.Identity, bias=ev_bias[:, 1:2], scale=LEVELS)\
                    .then_inc(x15_ready, 1)
            for b in range(1, NB):
                inner(b)

            for b in range(NB):
                act.wait_ge(xt_ready, b + 1)
                run(xf[:, :, 32 * b:32 * b + 32], ps[:, BANKS[1][b], :].rearrange("q (j o) -> q o j", o=OC), ACT.Copy,
                    scale=1.0 / LEVELS).then_inc(xf_ready, 1)
                if b == 2:
                    act.wait_ge(h_ve, 1)
                    run(h1[3][:], h1[2][:], ACT.Sqrt).then_inc(h_sqrt, 1)
            act.wait_ge(h_ab, 1)
            run(hs[:].rearrange("q (s r) -> q r s", r=H), ps[:, H_BANK, :].rearrange("q (r s) -> q r s", s=S2), ACT.Relu,
                bias=h_b[:], scale=h_a[:]).then_inc(h_ready, 1)
            act.wait_ge(hblk_zero, 1)
            act.wait_ge(tr_ready, 1)
            for q in range(2):
                rows = slice(32 * q, 32 * q + 32)
                run(hblk[rows, :, rows], ps[rows, HT_BANK, :].rearrange("q (m o) -> q o m", o=OC), ACT.Copy)\
                    .then_inc(hblk_act, 1)
            for g in range(4):
                act.wait_ge(t_ready, g + 1)
                run(ts[:, 4 * g:4 * g + 4, :].rearrange("q o n -> q (o n)"), ps[:, BANKS[1][g], :], ACT.Copy)\
                    .then_inc(ts_act, 1)
            act.wait_ge(f_ve, 1)
            run(f1[4][:], f1[3][:], ACT.Sqrt).then_inc(f_sqrt, 1)
            act.wait_ge(f_bias, 1)
            for o in range(OC):
                if o % 4 < RELU_ACT:
                    act.wait_ge(f_add, o + 1)
                    run(fo[:, o, :], fo[:, o, :], ACT.Relu, bias=f_b[:, o:o + 1]).then_inc(f_out, 1)

        @block.vector
        def _(dve):
            V = nc.vector
            links = [0]

            def link(ins):
                links[0] += 1
                ins.then_inc(chain, 1)
                dve.wait_ge(chain, links[0])

            def rstd(ve, s, work, scale_by, o):
                r, t, u = work
                link(V.reciprocal(r, s))
                link(V.tensor_tensor(t, ve, r, ALU.mult))
                link(V.tensor_tensor(t, t, s, ALU.add))
                link(V.reciprocal(u, t))
                link(V.scalar_tensor_tensor(o, u, 2.0, scale_by, ALU.mult, ALU.mult))

            V.memset(warm, 0.0).then_inc(warm_zero, 1)
            images = parts[:].rearrange("q i b a n -> q (i b a) n")
            shadows = parts[:, :, :, 1, :].rearrange("q i b (r s) -> q (i b) r s", s=S2)
            dve.wait_ge(warm_zero, 1)
            link(V.memset(images[:, :, 0:S2], 0.0))
            link(V.memset(images[:, :, PAD - S2:PAD], 0.0))
            link(V.memset(shadows[0:64, :, :, S2 - 1], 0.0))
            V.memset(shadows[64:128, :, :, 0], 0.0).then_inc(borders_zero, 1)
            dve.wait_ge(wa_in, 16)
            V.tensor_scalar(whalf[:, 0:256], wsp[:, 0:256], 0.5, None, ALU.mult).then_inc(w_half, 1)
            dve.wait_ge(par_in, 16)
            V.tensor_scalar(nb2[:], parm[:, P_B2:P_B2 + 1], -1.0, None, ALU.mult).then_inc(biases, 1)
            V.tensor_tensor(bd[:], parm[:, P_BD1:P_BD1 + 1], parm[:, P_BD2:P_BD2 + 1], ALU.add).then_inc(biases, 1)
            V.tensor_copy(b3b, parm[:, P_B3:P_B3 + 1].to_broadcast([128, 128])).then_inc(w_sum, 1)
            dve.wait_ge(wsrc_in, 16)
            V.tensor_tensor(wsp[:, 256:320], wsrc[:, 128:192], wsrc[:, 192:256], ALU.add).then_inc(w_sum, 1)
            dve.wait_ge(w_sum, 2)
            V.tensor_scalar(whalf[:, 256:320], wsp[:, 256:320], 0.5, None, ALU.mult).then_inc(w_half, 1)

            def x_top_copy(b):
                dve.wait_ge(x_in[b], 32)
                V.tensor_copy(x12[0:64, b - PLAIN, :], xd[0:64, b, :]).then_inc(x_top, 1)

            def x_middle(b):
                dve.wait_ge(x_res, b - PLAIN + 1)
                V.tensor_copy(x12[64:128, b - PLAIN, :], rx[64:128, :]).then_inc(x_mid, 1)

            def weight_parts():
                dve.wait_ge(w_fold, 1)
                alpha = parm[:, P_ALPHA:P_ALPHA + 1]
                link(V.tensor_scalar(wsp[:, 320:384], ps[:, 7, 0:64], alpha, None, ALU.mult))
                link(V.tensor_scalar(brow[:], ps[:, 7, 64:128], alpha, None, ALU.mult))
                V.tensor_scalar(whalf[:, 320:384], wsp[:, 320:384], 0.5, None, ALU.mult).then_inc(w_half, 1)
                V.tensor_copy(w11[:], wsp[:]).then_inc(w_parts, 1)
                dve.wait_ge(w_parts, 1)
                link(V.tensor_tensor(wr[:], wsp[:], w11[:], ALU.subtract))
                V.tensor_copy(w22[:], wr[:]).then_inc(w_parts, 1)
                dve.wait_ge(w_parts, 2)
                V.tensor_tensor(w31[0:64, :], wr[0:64, :], w22[0:64, :], ALU.subtract).then_inc(w_parts, 1)
                V.tensor_copy(w31[64:128, :], wsp[64:128, :]).then_inc(w_parts, 1)

            def b_middle(b):
                dve.wait_ge(b_res, b + 1)
                V.tensor_copy(b22[:, b % 2, :], rb[:]).then_inc(b_mid, 1)

            def c_first(b):
                if b:
                    dve.wait_ge(act_step, act_after[("C", b)])
                else:
                    dve.wait_ge(first_act, 2)
                V.tensor_copy(c13[:, b % 2, :], c32[:]).then_inc(c_hi, 1)

            def c_middle(b):
                dve.wait_ge(c_res, b + 1)
                V.tensor_copy(c12[64:128, b % 2, :], rc[64:128, :]).then_inc(c_mid, 1)

            def d_out(b):
                dve.wait_ge(d_ready, b + 1)
                if b >= 2:
                    dve.wait_ge(dz_ready, JT * (b - 1))
                V.tensor_tensor(d32[:, b % 2], slot(("D", b))[:, 0:512].rearrange("q (t c) -> q t c", c=C),
                                brow[:].unsqueeze(1).to_broadcast([128, JT, C]), ALU.add).then_inc(d_done, 1)

            def normalise(g):
                b, t = divmod(g, JT)
                dve.wait_ge(act_step, act_after[("S", g)])
                V.reciprocal(rz[:, g:g + 1], zsum[:, g:g + 1]).then_inc(rz_ready, 1)
                dve.wait_ge(rz_ready, g + 1)
                if t == 0:
                    dve.wait_ge(d_done, b + 1)
                if g >= 4:
                    dve.wait_ge(pv_done, g - 3)
                V.tensor_scalar(dz[:, g % 4, :], d32[:, b % 2, t, :], rz[:, g:g + 1], None, ALU.mult)\
                    .then_inc(dz_ready, 1)

            def side_copies(k, b, i):
                dve.wait_ge(main_done[i], NB * k + b + 1)
                for half in range(2):
                    o, moved = side(i, b, half, k == 2)
                    V.tensor_copy(o, moved(main(i, b))).then_inc(side_done[i], 1)

            def split_residual(k, b):
                n = NB * k + b
                dve.wait_ge(main_done[0], n + 1)
                dve.wait_ge(gen[k], b + 1)
                if n >= 2:
                    dve.wait_ge(side_done[2], 2 * (n - 1))
                V.tensor_tensor(res[:, b % 2, :], y_of[k][:, b, :], main(0, b), ALU.subtract).then_inc(r_done, 1)

            def split_second(k, b):
                dve.wait_ge(r_done, NB * k + b + 1)
                V.tensor_copy(main(1, b), res[:, b % 2, :]).then_inc(main_done[1], 1)
                side_copies(k, b, 1)

            def place_b(k, src, nbw):
                for half in range(2):
                    q = slice(64 * half, 64 * half + 64)
                    o = slice(64 * (1 - half), 64 * (1 - half) + 64)
                    yield wq[q, k, 3:3 + nbw, o], src[q, NA:NA + 64 * nbw].rearrange("q (a n) -> q a n", n=64)

            def lsq_scales():
                la = parm[:, P_LA:P_LA + 2]
                link(V.tensor_scalar(lsq_t[:], la, LSQ_G, None, ALU.mult))
                link(V.tensor_tensor(lsq[:], la, lsq_t[:], ALU.subtract))
                link(V.tensor_tensor(lsq[:], lsq_t[:], lsq[:], ALU.add))
                link(V.reciprocal(lsq_r[:], lsq[:]))
                link(V.tensor_tensor(bn[0][:], lsq[:], lsq[:], ALU.mult))
                link(V.tensor_tensor(bn[1][:], lsq[:], parm[:, P_L1G:P_L1G + 2], ALU.mult))
                V.tensor_scalar(ev[0][:], parm[:, P_L2V:P_L2V + 2], EPS, None, ALU.add).then_inc(ev_var, 1)

            def lsq_weights(k):
                dve.wait_ge(wconv_in, 16)
                dve.wait_ge(wq_zero, 1)
                w = wtmp[:, k, :]
                link(V.tensor_scalar(w, wraw[:, k, :], lsq_r[:, k:k + 1], QP, ALU.mult, ALU.min))
                link(V.tensor_scalar(w, w, QN, MAGIC, ALU.max, ALU.add))
                V.tensor_scalar(wq[:, k, 0:3, :], w[:, 0:NA].rearrange("q (a n) -> q a n", n=128), MAGIC, None,
                                ALU.subtract).then_inc(wq_ready[k], 3)
                for o, i in place_b(k, w, 3):
                    V.tensor_scalar(o, i, MAGIC, None, ALU.subtract).then_inc(wq_ready[k], 1)

            def tanh_max():
                dve.wait_ge(tanh_done, 1)
                V.tensor_reduce(wmax[:], wraw[:, 2:4, 0:NA], AX.X, ALU.max, apply_absolute_value=True)\
                    .then_inc(wmax_part, 1)

            def tanh_scale():
                dve.wait_ge(wmax_done, 1)
                link(V.tensor_scalar(wden[:], wmax_all[:], 2.0, None, ALU.mult))
                link(V.reciprocal(wden[:], wden[:]))

            def tanh_weights(k):
                n = NA + 128
                w = wtmp[:, k - 2, 0:n]
                dve.wait_ge(wq_ready[k - 2], 5)
                link(V.tensor_scalar(w, wraw[:, k, 0:n], wden[:, k - 2:k - 1], 0.5, ALU.mult, ALU.add))
                link(V.tensor_scalar(w, w, LEVELS, MAGIC, ALU.mult, ALU.add))
                V.tensor_scalar(wq[:, k, 0:3, :], w[:, 0:NA].rearrange("q (a n) -> q a n", n=128), MAGIC,
                                LEVELS / 2, ALU.subtract, ALU.subtract).then_inc(wq_ready[k], 3)
                for o, i in place_b(k, w, 2):
                    V.tensor_scalar(o, i, MAGIC, LEVELS / 2, ALU.subtract, ALU.subtract).then_inc(wq_ready[k], 1)
                dve.wait_ge(wq_ready[k], 5)
                V.memset(wq[0:64, k, 0, 64:128], 0.0).then_inc(wq_ready[k], 1)
                V.memset(wq[64:128, k, 2, 0:64], 0.0).then_inc(wq_ready[k], 1)

            def clip_edges(i):
                v = edge_buf[i]
                dve.wait_ge(edge_sum, i + 1)
                V.tensor_scalar(v, v, 0.0, 1.0, ALU.max, ALU.min).then_inc(edge_clip, 1)

            def half_of_b():
                dve.wait_ge(first_act, 3)
                V.tensor_scalar(bhalf[:], b32[:, 0:128 * DIRECT], 0.5, None, ALU.mult).then_inc(bhalf_ready, 1)

            half_of_b()
            c_first(0)
            weight_parts()
            for kind, i in uses:
                if kind == "D":
                    d_out(i)
                if kind != "S":
                    continue
                b, t = divmod(i, JT)
                dve.wait_ge(s_ready, i + 1)
                V.tensor_reduce(nmax[:, i:i + 1], slot(("S", i)), AX.X, ALU.min).then_inc(max_ready, 1)
                if i >= 1:
                    normalise(i - 1)
                if i == 0:
                    c_middle(0)
                if i == 1:
                    b_middle(0)
                if b + 1 < NB:
                    if t == c_after(b) + 1:
                        c_first(b + 1)
                    if t == (3 if b == 0 else 2):
                        b_middle(b + 1)
                    if t == c_after(b) + 3:
                        c_middle(b + 1)
                if b + 2 < NB:
                    if t == (5 if b == 0 else 0):
                        x_top_copy(b + 2)
                    elif t == (6 if b == 0 else 1):
                        x_middle(b + 2)
                if b >= 1:
                    if t == 5:
                        side_copies(0, b - 1, 0)
                    elif t == 6:
                        split_residual(0, b - 1)
                    elif t == 7:
                        split_second(0, b - 1)
                if i == JT:
                    lsq_scales()
                if i == 2 * JT:
                    lsq_weights(0)
                if i >= NB * JT - 4:
                    clip_edges(i - (NB * JT - 4))
            normalise(NB * JT - 1)
            side_copies(0, NB - 1, 0)
            split_residual(0, NB - 1)
            split_second(0, NB - 1)
            lsq_weights(1)
            tanh_max()

            def normalisation(k):
                c = slice(k, k + 1)
                avg = ps[:, BANKS[1 - k][0], 0:2]
                V.bn_aggr(mv[:, k, :], st[:, k].rearrange("q b n -> q (b n)")).then_inc(bn_mv[k], 1)
                dve.wait_ge(bn_avg[k], 1)
                dve.wait_ge(bn_mv[k], 1)
                link(V.tensor_tensor(bn[2][:, c], mv[:, k, 0:1], avg[:, 0:1], ALU.subtract))
                link(V.scalar_tensor_tensor(bn[6][:, c], bn[2][:, c], bn[2][:, c], avg[:, 1:2], ALU.mult, ALU.add))
                V.tensor_scalar(bn[3][:, c], bn[6][:, c], bn[0][:, c], EPS, ALU.mult, ALU.add).then_inc(bn_var[k], 1)
                link(V.tensor_scalar(bn[5][:, c], avg[:, 0:1], -1.0, None, ALU.mult))
                dve.wait_ge(bn_sqrt[k], 1)
                rstd(bn[3][:, c], bn[4][:, c], (bn[7][:, c], bn[8][:, c], bn[9][:, c]), bn[1][:, c], bn_a[:, c])
                V.scalar_tensor_tensor(bn_b[:, c], bn[5][:, c], bn_a[:, c], parm[:, P_L1B + k:P_L1B + k + 1],
                                       ALU.mult, ALU.add).then_inc(bn_ready[k], 1)
                dve.wait_ge(bn_ready[k], 1)

            def inner_normalisation():
                eg, eb, em = (parm[:, p:p + 2] for p in (P_L2G, P_L2B, P_L2M))
                dve.wait_ge(ev_sqrt, 1)
                rstd(ev[0][:], ev[1][:], (ev[2][:], ev[3][:], ev[4][:]), eg, ev[5][:])
                link(V.tensor_tensor(ev[6][:], em, ev[5][:], ALU.mult))
                link(V.tensor_tensor(ev[7][:], eb, ev[6][:], ALU.subtract))
                link(V.tensor_scalar(ev_bias[:], ev[7][:], LEVELS, None, ALU.mult))
                link(V.tensor_scalar(ev_scale[:, 0:1], ev[5][:, 0:1], 2.0, None, ALU.mult))
                V.tensor_scalar(ev_scale[:, 1:2], ev[5][:, 1:2], 2.0 / LEVELS, None, ALU.mult).then_inc(ev_ready, 1)
                dve.wait_ge(ev_ready, 1)

            def link_stats(k, b):
                dve.wait_ge(conv_done[k], b + 1)
                link(V.bn_stats(st[:, k, b, :], ps[:, BANKS[k][b], :]))

            for b in range(NB):
                link_stats(0, b)
            normalisation(0)
            for b in range(NB):
                side_copies(1, b, 0)
                split_residual(1, b)
                split_second(1, b)
                if b == 0:
                    tanh_scale()
                elif b < 3:
                    tanh_weights(b + 1)
                else:
                    inner_normalisation()
            for b in range(NB):
                link_stats(1, b)
            V.memset(shadows[64:128, :, RP - 2, :], 0.0).then_inc(skew_zero, 1)
            normalisation(1)

            def add_residual(b):
                if b >= 2:
                    dve.wait_ge(gen[2], b - 1)
                V.scalar_tensor_tensor(tmp[:, b % 2, :], ps[:, BANKS[1][b], :], bn_a[:, 1:2], y1[:, b, :],
                                       ALU.mult, ALU.add).then_inc(sum_ready, 1)

            def round_inner(b):
                v = tmp[:, b % 2, :]
                dve.wait_ge(q_relu, b + 1)
                V.tensor_scalar(v, v, LEVELS, MAGIC, ALU.min, ALU.add).then_inc(q_int, 1)
                dve.wait_ge(q_int, b + 1)
                V.tensor_scalar(main(0, b), v, MAGIC, None, ALU.subtract).then_inc(q_ready, 1)
                dve.wait_ge(q_ready, 3 * b + 1)
                for half in range(2):
                    o, moved = side(0, b, half, True)
                    V.tensor_copy(o, moved(main(0, b))).then_inc(q_ready, 1)

            def outer(b):
                v = tmpo[:, b % 2, :]
                dve.wait_ge(conv_done[3], b + 1)
                dve.wait_ge(x15_ready, b + 1)
                link(V.scalar_tensor_tensor(v, ps[:, BANKS[1][b], :], ev_scale[:, 1:2], x15[:, b, :], ALU.mult, ALU.add))
                link(V.tensor_scalar(v, v, 0.0, LEVELS, ALU.max, ALU.min))
                V.tensor_scalar(xi[:, b, :], v, MAGIC, MAGIC, ALU.add, ALU.subtract).then_inc(xi_ready, 1)

            def split_two(b):
                split_residual(2, b)
                split_second(2, b)

            add_residual(0)
            add_residual(1)
            split_two(0)
            add_residual(2)
            split_two(1)
            add_residual(3)
            split_two(2)
            round_inner(0)
            split_two(3)
            round_inner(1)
            outer(0)
            round_inner(2)
            outer(1)
            round_inner(3)
            outer(2)
            outer(3)

            dve.wait_ge(h_raw, 1)
            link(V.bn_stats(hst[:], ps[:, H_BANK, :]))
            V.bn_aggr(hmv[:], hst[:]).then_inc(h_mv, 1)
            dve.wait_ge(h_avg, 1)
            dve.wait_ge(h_mv, 1)
            link(V.tensor_tensor(h1[0][:], hmv[:, 0:1], ps[:, AVG_BANK, 0:1], ALU.subtract))
            link(V.tensor_scalar(h1[4][:], ps[:, AVG_BANK, 0:1], -1.0, None, ALU.mult))
            link(V.tensor_scalar(h1[9][:], parm[:, P_G1:P_G1 + 1], 1.0 / LEVELS, None, ALU.mult))
            V.scalar_tensor_tensor(h1[1][:], h1[0][:], h1[0][:], hmv[:, 1:2], ALU.mult, ALU.add).then_inc(h_var, 1)
            dve.wait_ge(h_vavg, 1)
            V.tensor_scalar(h1[2][:], ps[:, AVG_BANK, 2:3], LEVELS ** -2, EPS, ALU.mult, ALU.add).then_inc(h_ve, 1)
            dve.wait_ge(h_sqrt, 1)
            rstd(h1[2][:], h1[3][:], (h1[5][:], h1[6][:], h1[7][:]), h1[9][:], h_a[:])
            V.scalar_tensor_tensor(h_b[:], h1[4][:], h_a[:], parm[:, P_BT1:P_BT1 + 1], ALU.mult, ALU.add)\
                .then_inc(h_ab, 1)
            dve.wait_ge(hblk_zero, 1)
            dve.wait_ge(tr_ready, 1)
            for q in range(2, 4):
                rows = slice(32 * q, 32 * q + 32)
                V.tensor_copy(hblk[rows, :, rows], ps[rows, HT_BANK, :].rearrange("q (m o) -> q o m", o=OC))\
                    .then_inc(hblk_dve, 1)
            for o in range(OC):
                if o % 4 == 0:
                    dve.wait_ge(f_ready, o // 4 + 1)
                last = V.bn_stats(st2[:, o, :], ps[:, BANKS[0][o // 4], 128 * (o % 4):128 * (o % 4) + 128])
            last.then_inc(f_stat, 1)
            dve.wait_ge(f_avg, 1)
            dve.wait_ge(f_stat, 1)
            link(V.tensor_copy(f_avgs[:], ps[:, BANKS[1][0], 0:96].rearrange("q (o n) -> q o n", n=6)))
            mean = f1[0]
            link(V.tensor_tensor(mean[:], f_avgs[:, :, 1], f_avgs[:, :, 4], ALU.add))
            link(V.tensor_tensor(f1[1][:], f_avgs[:, :, 2], f_avgs[:, :, 5], ALU.add))
            link(V.tensor_tensor(f_dev[:], st2[:, :, 1:5:3], mean[:].unsqueeze(2).to_broadcast([128, OC, 2]),
                                 ALU.subtract))
            V.tensor_tensor(f_sq[:], f_dev[:], f_dev[:], ALU.mult).then_inc(f_sqr, 1)
            dve.wait_ge(f_vavg, 1)
            link(V.tensor_copy(f_vars[:], ps[:, BANKS[1][0], 96:128].rearrange("q (o n) -> q o n", n=2)))
            link(V.tensor_tensor(f1[2][:], f_vars[:, :, 0], f_vars[:, :, 1], ALU.add))
            link(V.scalar_tensor_tensor(f1[5][:], f1[1][:], 1.0 / 64, f1[2][:], ALU.mult, ALU.add))
            V.tensor_scalar(f1[3][:], f1[5][:], EPS, None, ALU.add).then_inc(f_ve, 1)
            dve.wait_ge(f_sqrt, 1)
            rstd(f1[3][:], f1[4][:], (f1[6][:], f1[7][:], f1[8][:]), parm[:, P_G2:P_G2 + OC], f_a[:])
            link(V.tensor_tensor(f1[9][:], mean[:], f_a[:], ALU.mult))
            V.tensor_tensor(f_b[:], parm[:, P_BT2:P_BT2 + OC], f1[9][:], ALU.subtract).then_inc(f_bias, 1)
            dve.wait_ge(f_bias, 1)
            for o in range(OC):
                V.scalar_tensor_tensor(fo[:, o, :], ps[:, BANKS[0][o // 4], 128 * (o % 4):128 * (o % 4) + 128], f_a[:, o:o + 1],
                                       xf[:, o, :], ALU.mult, ALU.add).then_inc(f_add, 1)
                if o % 4 >= RELU_ACT:
                    dve.wait_ge(f_add, o + 1)
                    V.tensor_scalar(fo[:, o, :], fo[:, o, :], f_b[:, o:o + 1], 0.0, ALU.add, ALU.max)\
                        .then_inc(f_out_dve, 1)

        @block.gpsimd
        def _(pool):
            G = nc.gpsimd
            links = [0]

            def link(ins):
                links[0] += 1
                ins.then_inc(pchain, 1)
                pool.wait_ge(pchain, links[0])

            G.memset(wq[:], 0.0).then_inc(wq_zero, 1)
            pool.wait_ge(wq_zero, 1)
            pool.wait_ge(cst_in, 16)
            G.tensor_copy(ident_bf[:], consts[:, K_ID:K_ID + 128]).then_inc(id_ready, 1)
            pool.wait_ge(id_ready, 1)

            def x_residual(b):
                pool.wait_ge(x_cast, b - PLAIN + 1)
                G.tensor_tensor(rx[64:128, :], xd[64:128, b, :], x13[64:128, b - PLAIN, :], ALU.subtract)\
                    .then_inc(x_res, 1)
                pool.wait_ge(x_res, b - PLAIN + 1)

            def x_third(b):
                pool.wait_ge(x_mid, b - PLAIN + 1)
                G.tensor_tensor(x13[64:128, b - PLAIN, :], rx[64:128, :], x12[64:128, b - PLAIN, :], ALU.subtract)\
                    .then_inc(x_parts, 1)
                pool.wait_ge(x_parts, b - PLAIN + 1)

            def b_residual(b):
                pool.wait_ge(b_hi, b + 1)
                G.tensor_tensor(rb[:], b32[:], b11[:, b % 2, :], ALU.subtract).then_inc(b_res, 1)
                pool.wait_ge(b_res, b + 1)

            def b_third(b):
                pool.wait_ge(b_mid, b + 1)
                G.tensor_tensor(b31[0:64, b % 2, :], rb[0:64, :], b22[0:64, b % 2, :], ALU.subtract)\
                    .then_inc(b_lo, 1)
                pool.wait_ge(b_lo, b + 1)

            def c_residual(b):
                pool.wait_ge(c_hi, b + 1)
                G.tensor_tensor(rc[64:128, :], c32[64:128, :], c13[64:128, b % 2, :], ALU.subtract)\
                    .then_inc(c_res, 1)
                pool.wait_ge(c_res, b + 1)

            def c_third(b):
                pool.wait_ge(c_mid, b + 1)
                G.tensor_tensor(c13[64:128, b % 2, :], rc[64:128, :], c12[64:128, b % 2, :], ALU.subtract)\
                    .then_inc(c_lo, 1)
                pool.wait_ge(c_lo, b + 1)

            def third_part(k, b):
                n = NB * k + b
                pool.wait_ge(main_done[1], n + 1)
                G.tensor_tensor(main(2, b), res[:, b % 2, :], main(1, b), ALU.subtract).then_inc(main_done[2], 1)
                pool.wait_ge(main_done[2], n + 1)
                for half in range(2):
                    o, moved = side(2, b, half, k == 2)
                    G.tensor_tensor(o, moved(res[:, b % 2, :]), moved(main(1, b)), ALU.subtract)\
                        .then_inc(side_done[2], 1)
                    pool.wait_ge(side_done[2], 2 * n + 1 + half)

            def edge(i, offset, table):
                G.tensor_tensor(edge_buf[i].rearrange("q (k j) -> q k j", j=W),
                                parm[:, offset:offset + C].unsqueeze(2).to_broadcast([128, C, W]),
                                consts[:, table:table + W].unsqueeze(1).to_broadcast([128, C, W]), ALU.add)\
                    .then_inc(edge_sum, 1)
                pool.wait_ge(edge_sum, i + 1)

            c_residual(0)
            b_residual(0)
            c_third(0)
            b_third(0)
            pool.wait_ge(par_in, 16)
            w1 = parm[:, P_W1:P_W1 + OC]
            link(G.memset(wp[:], 0.0))
            link(G.tensor_copy(w1p[:, 0, :], w1))
            link(G.tensor_tensor(w1f[:], w1, w1p[:, 0, :], ALU.subtract))
            link(G.tensor_copy(w1p[:, 1, :], w1f[:]))
            link(G.tensor_tensor(w1p[:, 2, :], w1f[:], w1p[:, 1, :], ALU.subtract))
            link(G.tensor_copy(wp[0:64, :, 0:OC], w1p[0:64]))
            G.tensor_copy(wp[64:128, :, OC:2 * OC], w1p[64:128]).then_inc(wp_ready, 1)
            pool.wait_ge(wp_ready, 1)

            b_residual(1)
            b_third(1)
            x_residual(2)
            c_residual(1)
            c_third(1)
            x_third(2)
            x_residual(3)
            b_residual(2)
            x_third(3)
            b_third(2)
            c_residual(2)
            c_third(2)
            third_part(0, 0)
            b_residual(3)
            b_third(3)
            c_residual(3)
            c_third(3)
            third_part(0, 1)
            edge(0, P_XMAX, K_IR1)
            edge(1, P_XMIN, K_IR)
            edge(2, P_YMAX, K_JW1)
            edge(3, P_YMIN, K_JW)
            third_part(0, 2)
            third_part(0, 3)
            pool.wait_ge(edge_clip, 2)
            G.tensor_tensor(edge_buf[0], edge_buf[0], edge_buf[1], ALU.subtract).then_inc(rows_ready, 1)
            pool.wait_ge(rows_ready, 1)
            pool.wait_ge(wmax_part, 1)
            G.partition_all_reduce(wmax_all[:], wmax[:], 128, bass.bass_isa.ReduceOp.max).then_inc(wmax_done, 1)
            pool.wait_ge(wmax_done, 1)
            pool.wait_ge(edge_clip, 4)
            G.tensor_tensor(edge_buf[3], edge_buf[2], edge_buf[3], ALU.subtract).then_inc(cols_ready, 1)
            pool.wait_ge(cols_ready, 1)
            pool.wait_ge(pv_done, NB * JT)
            G.memset(hblk[:], 0.0).then_inc(hblk_zero, 1)
            pool.wait_ge(hblk_zero, 1)
            for k in (1, 2):
                for b in range(NB):
                    third_part(k, b)


def constants():
    import numpy as np

    k = np.zeros((128, K_COLS), np.float32)
    q = np.arange(128)
    k[:, K_ID:K_ID + 128] = np.eye(128)
    k[:, K_AVG2:K_AVG2 + 128] = (q[:, None] % 64 == q[None] % 64) / 2
    k[:, K_AVG8:K_AVG8 + 128] = (q[:, None] % 16 == q[None] % 16) / 8
    k[:, K_AVGQ:K_AVGQ + 128] = (q[:, None] // 32 == q[None] // 32) / 64
    n = np.arange(32)
    r = q % 32
    w = 8 * (q // 8 % 4) + 2 * (q // 32) + q % 2
    k[:, K_IR:K_IR + 32] = n - r[:, None]
    k[:, K_IR1:K_IR1 + 32] = n - r[:, None] + 1
    k[:, K_JW:K_JW + 32] = n - w[:, None]
    k[:, K_JW1:K_JW1 + 32] = n - w[:, None] + 1
    k[:, K_MASK:K_MASK + 4] = (q[:, None] // 2 % 4) == np.arange(4)
    return k


def kernel(**inputs):
    import numpy as np
    import concourse.bacc as bacc
    from concourse.bass_utils import run_bass_kernel_spmd

    a = {n: np.asarray(v) for n, v in inputs.items()}
    x = a["x"].reshape(NB, C, H, S2, 2).transpose(1, 0, 4, 2, 3).reshape(C, NB * HW)

    def twice(m, axis=0):
        return np.concatenate([m, m], axis=axis)

    l0 = {n: a["L0_conv_" + n] for n in ("w1", "w2", "w3", "wd1", "wd2")}
    wa = np.concatenate([twice(twice(l0["w1"].T), 1), twice(twice(l0["w2"].T), 1), twice(twice(l0["w3"]), 1),
                         twice(l0["wd1"].T), twice(l0["wd2"].T)], axis=1)

    def taps(w, picks):
        t = w.transpose(1, 2, 3, 0)
        return np.concatenate([np.concatenate([t[:, kh, kw, :] for kh, kw in picks[p]], axis=1) for p in range(2)])

    col = {(0, 0): 1, (1, 0): 2, (0, 1): 0, (1, 1): 1}
    main = [[(kh, col[i, o]) for kh in range(3) for o in range(2)] for i in range(2)]
    side1 = [[(kh, 2) for kh in range(3)], [(kh, 0) for kh in range(3)]]
    side2 = [[(0, 2), (1, 2), (2, 2)], [(1, 0), (2, 0), (0, 0)]]
    wconv = np.concatenate([taps(a[n], [m + s for m, s in zip(main, side)]) for n, side in (
        ("L1_conv_w1", side1), ("L1_conv_w2", side1), ("L2_conv_w1", side2), ("L2_conv_w2", side2))], axis=1)

    def column(v, n=1):
        return np.tile(np.ravel(v), n)[:, None]

    def everywhere(v):
        return np.broadcast_to(np.ravel(v)[None], (128, np.size(v)))

    cols = [column(a["L0_conv_" + n], 2) for n in ("b1", "b2", "b3", "bd1", "bd2")]
    cols += [column(a[n], 128) for n in ("L0_conv_alpha", "L1_conv_alpha1", "L1_conv_alpha2")]
    cols += [column(a["L1_conv_" + n], 2) for n in ("gamma1", "gamma2", "beta1", "beta2")]
    cols += [column(a["L2_conv_" + n], 2) for n in (
        "gamma1", "gamma2", "beta1", "beta2", "mean1", "mean2", "var1", "var2")]
    cols += [column(a["L3_conv_" + n], 8) for n in ("g1", "b1")]
    cols += [np.repeat(a["L3_conv_" + n].reshape(OC, BOX).T, 32, axis=0) for n in ("g2", "b2")]
    cols += [everywhere(a["L3_conv_" + n]) for n in ("x_max", "x_min", "y_max", "y_min")]
    cols.append(twice(a["L3_conv_w1"].T))
    par = np.concatenate(cols, axis=1)

    sent = {"x": x, "wa": wa, "wconv": wconv, "par": par, "cst": constants()}
    sent = {n: np.ascontiguousarray(v) for n, v in sent.items()}
    nc = bacc.Bacc("TRN2", target_bir_lowering=False, num_devices=1)
    args = [nc.dram_tensor(n, v.shape, mybir.dt.from_np(v.dtype), kind="ExternalInput").ap() for n, v in sent.items()]
    args.append(nc.dram_tensor("out", (128, OC * 128), F32, kind="ExternalOutput").ap())
    build(nc, *args)
    r = run_bass_kernel_spmd(nc, [sent], core_ids=[0])
    got = r.results[0]["out"].reshape(BOX, H, OC, NB, W)
    return np.ascontiguousarray(got.transpose(3, 2, 0, 1, 4)).reshape(NB, C, H, W)
```

```python
from contextlib import ExitStack

import concourse.bass as bass
from concourse import mybir

F32 = mybir.dt.float32
BF16 = mybir.dt.bfloat16
ALU = mybir.AluOpType
ACT = mybir.ActivationFunctionType
AX = mybir.AxisListType

NB, C, H, W = 4, 64, 32, 32
S2 = W // 2
HW = H * W
HALF = H * S2
JT = HW // 128
RP = H + 2
PAD = RP * S2
OC, BOX = 16, 4
EPS = 1e-5
MAGIC = 12582912.0
QN, QP = -4.0, 3.0
LEVELS = 15.0
LSQ_G = float((C * C * 9 * QP) ** -0.5)

(P_B1, P_B2, P_B3, P_BD1, P_BD2, P_ALPHA, P_LA, P_L1G, P_L1B, P_L2G, P_L2B, P_L2M, P_L2V, P_G1, P_BT1,
 P_G2, P_BT2, P_XMAX, P_XMIN, P_YMAX, P_YMIN, P_W1) = (
    0, 1, 2, 3, 4, 5, 6, 8, 10, 12, 14, 16, 18, 20, 21, 22, 38, 54, 118, 182, 246, 310)
P_COLS = 326
K_ID, K_AVG2, K_AVG8, K_AVGQ, K_IR, K_IR1, K_JW, K_JW1, K_MASK = 0, 128, 256, 384, 512, 544, 576, 608, 640
K_COLS = 644
WA_COLS = 512
NA, NBW = 384, 192
WARM = 10
RELU_DVE = (0, 8)
DIRECT = 3
D_AFTER = 5
PLAIN = 2
H_BANK, HT_BANK, AVG_BANK = 6, 4, 5
BANKS = ((6, 4, 5, 0), (7, 1, 2, 3))
ORDER_1 = ((0, 0), (1, 0), (0, 1), (1, 1), (0, 2), (2, 0), (2, 1), (1, 2), (3, 0), (3, 1), (2, 2), (3, 2))
ORDER_2 = ((2, 0, 0), (2, 0, 1), (2, 1, 0), (2, 0, 2), (2, 1, 1), (2, 2, 0), (2, 2, 1), (2, 1, 2), (2, 3, 0),
           (3, 0, 0), (2, 2, 2), (2, 3, 1), (3, 1, 0), (2, 3, 2))
LAG = 2


def c_after(b):
    return DIRECT if b == 0 else 2


def gpsimd_sides(k, b):
    return (k == 0 and b < NB - 1) or (k == 2 and b < 2)


def b_after(b):
    return 1 if b == 0 else 0


def attention_uses():
    uses = [("C", 0), ("B", 0)]
    for b in range(NB):
        for t in range(JT):
            uses.append(("S", b * JT + t))
            if b == 0 and t == 0:
                uses.append(("D", 0))
            if b + 1 < NB and t in (b_after(b), c_after(b), D_AFTER):
                uses.append(({b_after(b): "B", c_after(b): "C", D_AFTER: "D"}[t], b + 1))
    return uses


def build(nc, x, wa, wconv, par, cst, out):
    uses = attention_uses()
    by_act, by_dve = [], []
    for n, (kind, _) in enumerate(uses):
        by_act.append((by_act[-1] if by_act else 0) + (kind != "D" and n >= 2))
        by_dve.append((by_dve[-1] if by_dve else 0) + (kind == "D"))
    act_after = {u: by_act[n] for n, u in enumerate(uses)}
    slot_of = {u: n % 3 for n, u in enumerate(uses)}

    with ExitStack() as ctx:
        def sb(name, shape, dt=F32):
            return ctx.enter_context(nc.sbuf_tensor(name, [128] + shape, dt))

        def sem(name):
            return ctx.enter_context(nc.semaphore(name))

        def sems(name, n):
            return [sem(f"{name}{i}") for i in range(n)]

        parm = sb("parm", [P_COLS])
        consts = sb("consts", [K_COLS])
        ident_bf = sb("ident_bf", [128], BF16)
        wq = sb("wq", [4, 6, 128], BF16)
        parts = sb("parts", [3, NB, 2, PAD], BF16)
        wside = sb("wside", [3, 3, 2, 64], BF16)
        res = sb("res", [2, HALF])
        y1 = sb("y1", [NB, HALF])
        box_t = sb("box_t", [3, C * H])
        rows_w = sb("rows_w", [OC, BOX * H])
        wraw = sb("wraw", [4, NA + NBW])
        wtmp = sb("wtmp", [2, NA + NBW])
        w1f = sb("w1f", [OC])
        w1p = sb("w1p", [3, OC], BF16)
        wp = sb("wp", [3, 2 * OC], BF16)
        nb2 = sb("nb2", [1])
        bd = sb("bd", [1])
        lsq = sb("lsq", [2])
        lsq_r = sb("lsq_r", [2])
        lsq_t = sb("lsq_t", [2])
        wmax = sb("wmax", [2])
        wmax_all = sb("wmax_all", [2])
        wden = sb("wden", [2])
        ev_var_r, ev_rstd, ev_gain, ev_shift, ev_add = (sb(n, [2]) for n in (
            "ev_var_r", "ev_rstd", "ev_gain", "ev_shift", "ev_add"))
        ev_scale = sb("ev_scale", [2])
        ev_bias = sb("ev_bias", [2])
        st = sb("st", [2, NB, 6])
        mv = sb("mv", [2, 2])
        lsq_sq, lsq_gain, bn_dev, bn_v, bn_recip, bn_rstd, bn_mg = (sb(n, [2]) for n in (
            "lsq_sq", "lsq_gain", "bn_dev", "bn_v", "bn_recip", "bn_rstd", "bn_mg"))
        bn_a = sb("bn_a", [2])
        bn_b = sb("bn_b", [2])
        hst = sb("hst", [6])
        hmv = sb("hmv", [2])
        h_dev, h_v, h_ve_t, h_recip, h_rstd, h_gain, h_mg = (sb(n, [1]) for n in (
            "h_dev", "h_v", "h_ve_t", "h_recip", "h_rstd", "h_gain", "h_mg"))
        h_a = sb("h_a", [1])
        h_b = sb("h_b", [1])
        st2 = sb("st2", [OC, 6])
        f_mean, f_v, f_recip, f_rstd, f_mg, f_mgr = (sb(n, [OC]) for n in (
            "f_mean", "f_v", "f_recip", "f_rstd", "f_mg", "f_mgr"))
        f_dev = sb("f_dev", [OC, 2])
        f_sq = sb("f_sq", [OC, 2])
        f_a = sb("f_a", [OC])
        f_b = sb("f_b", [OC])

        att = ExitStack()

        def sa(name, shape, dt=F32):
            return att.enter_context(nc.sbuf_tensor(name, [128] + shape, dt))

        xd = sa("xd", [NB, HW])
        x12 = sa("x12", [NB - PLAIN, HW], BF16)
        x13 = sa("x13", [NB - PLAIN, HW], BF16)
        bhalf = sa("bhalf", [128 * DIRECT])
        rx = sa("rx", [HW])
        b32 = sa("b32", [HW])
        c32 = sa("c32", [HW])
        rb = sa("rb", [HW])
        rc = sa("rc", [HW])
        b11 = sa("b11", [2, HW], BF16)
        b22 = sa("b22", [2, HW], BF16)
        b31 = sa("b31", [2, HW], BF16)
        c12 = sa("c12", [2, HW], BF16)
        c13 = sa("c13", [2, HW], BF16)
        d32 = sa("d32", [2, JT, C])
        dz = sa("dz", [4, C])
        probs = sa("probs", [3, HW])
        nmax = sa("nmax", [NB * JT])
        zsum = sa("zsum", [NB * JT])
        rz = sa("rz", [NB * JT])
        wsrc = sa("wsrc", [WA_COLS - 256])
        wsp = sa("wsp", [384])
        wr = sa("wr", [384])
        whalf = sa("whalf", [384])
        w11 = sa("w11", [384], BF16)
        w22 = sa("w22", [384], BF16)
        w31 = sa("w31", [384], BF16)
        b3b = wr[:, 0:128]
        brow = sa("brow", [C])
        att.close()

        cols_blk = sb("cols_blk", [C, NB, W])
        y2 = sb("y2", [NB, HALF])
        y3 = sb("y3", [NB, HALF])
        tmp = sb("tmp", [2, HALF])
        tmpo = sb("tmpo", [2, HALF])
        x15 = sb("x15", [NB, HALF])
        q_in = sb("q_in", [2, HALF], BF16)
        xi = sb("xi", [NB, HALF], BF16)
        hs = sb("hs", [HALF])
        hblk = sb("hblk", [OC, 128])
        edge_buf = [rows_w[:].rearrange("q o n -> q (o n)")] + [box_t[:, i, :] for i in range(3)]
        xf, fo, ts = (box_t[:, i, :].rearrange("q (o n) -> q o n", o=OC) for i in range(3))

        ps = ctx.enter_context(nc.psum_tensor("ps", [128, 8, 512], F32))

        def slot(u):
            n = slot_of[u]
            return ps[:, 2 * n:2 * n + 2, :].rearrange("q a n -> q (a n)")

        y_of = (y1, y2, y3)

        def main(i, b):
            return parts[:, i, b, 0, S2:S2 + HALF]

        def side(i, b, half, skew):
            place = 2 if i == 2 else half
            q = slice(64 * half, 64 * half + 64)
            to_q = slice(64 * (1 - half), 64 * (1 - half) + 64) if i == 1 else q
            first = 0 if (skew and half) else S2
            o = parts[to_q, place, b, 1, first:first + HALF].rearrange("q (r s) -> q r s", s=S2)
            to, of = (slice(1, S2), slice(0, S2 - 1)) if half else (slice(0, S2 - 1), slice(1, S2))

            def moved(t):
                return t[q].rearrange("q (r s) -> q r s", s=S2)[:, :, of]
            return o[:, :, to], moved

        x_in = sems("x_in", NB)
        x_cast, x_top, x_res, x_mid, x_parts = (sem(n) for n in ("x_cast", "x_top", "x_res", "x_mid", "x_parts"))
        b_hi, b_res, b_mid, b_lo, b_rep = (sem(n) for n in ("b_hi", "b_res", "b_mid", "b_lo", "b_rep"))
        c_hi, c_top, c_res, c_mid, c_lo = (sem(n) for n in ("c_hi", "c_top", "c_res", "c_mid", "c_lo"))
        par_in, wa_in, cst_in, wconv_in = (sem(n) for n in ("par_in", "wa_in", "cst_in", "wconv_in"))
        w_sum, w_fold, w_parts, biases = (sem(n) for n in ("w_sum", "w_fold", "w_parts", "biases"))
        warm_zero, w_half, first_ready, first_act, bhalf_ready = (sem(n) for n in (
            "warm_zero", "w_half", "first_ready", "first_act", "bhalf_ready"))
        wsrc_in, edge_sum, edge_clip = sem("wsrc_in"), sem("edge_sum"), sem("edge_clip")
        act_step, d_done = sem("act_step"), sem("d_done")
        bc_ready, d_ready, s_ready = sem("bc_ready"), sem("d_ready"), sem("s_ready")
        max_ready, rz_ready, dz_ready, pv_done = sem("max_ready"), sem("rz_ready"), sem("dz_ready"), sem("pv_done")
        gen = sems("gen", 3)
        main_done, side_done, r_done = sems("main_done", 3), sems("side_done", 3), sem("r_done")
        conv_done = sems("conv_done", 4)
        wq_ready = sems("wq_ready", 4)
        wq_zero, borders_zero, skew_zero, hblk_zero = (sem(n) for n in (
            "wq_zero", "borders_zero", "skew_zero", "hblk_zero"))
        tanh_done, wmax_part, wmax_done = sem("tanh_done"), sem("wmax_part"), sem("wmax_done")
        rows_ready, cols_ready, cols_placed = sem("rows_ready"), sem("cols_ready"), sem("cols_placed")
        wp_ready, id_ready = sem("wp_ready"), sem("id_ready")
        ev_var, ev_sqrt, ev_ready = sem("ev_var"), sem("ev_sqrt"), sem("ev_ready")
        bn_mv, bn_avg, bn_var, bn_sqrt, bn_ready = (sems(n, 2) for n in (
            "bn_mv", "bn_avg", "bn_var", "bn_sqrt", "bn_ready"))
        sum_ready = sem("sum_ready")
        q_relu, q_int, q_ready = sem("q_relu"), sem("q_int"), sem("q_ready")
        x15_ready, xi_ready = sem("x15_ready"), sem("xi_ready")
        h_raw, h_mv, h_avg, h_var, h_vavg, h_ve, h_sqrt, h_ab, h_ready = (sem(n) for n in (
            "h_raw", "h_mv", "h_avg", "h_var", "h_vavg", "h_ve", "h_sqrt", "h_ab", "h_ready"))
        tr_ready, hblk_act, hblk_dve = sem("tr_ready"), sem("hblk_act"), sem("hblk_dve")
        t_ready, ts_act, f_ready = sem("t_ready"), sem("ts_act"), sem("f_ready")
        xt_ready, xf_ready = sem("xt_ready"), sem("xf_ready")
        f_stat, f_avg, f_sqr, f_vavg, f_ve, f_sqrt, f_bias, f_scale, f_add, f_out = (sem(n) for n in (
            "f_stat", "f_avg", "f_sqr", "f_vavg", "f_ve", "f_sqrt", "f_bias", "f_scale", "f_add", "f_out"))
        chain = sem("dve_chain")
        pchain = sem("pool_chain")
        stored, f_out_dve = sem("stored"), sem("f_out_dve")

        warm = main(0, 0)

        block = ctx.enter_context(nc.Block())

        @block.sync
        def _(sp):
            sp.dma_start(xd[0:64, 0, :], x[:, 0:HW]).then_inc(x_in[0], 16)
            sp.dma_start(xd[64:128, 0, :], x[:, 0:HW]).then_inc(x_in[0], 16)
            sp.dma_start(consts[:], cst).then_inc(cst_in, 16)
            for b in range(1, NB):
                sp.dma_start(xd[0:64, b, :], x[:, b * HW:(b + 1) * HW]).then_inc(x_in[b], 16)
                sp.dma_start(xd[64:128, b, :], x[:, b * HW:(b + 1) * HW]).then_inc(x_in[b], 16)
            sp.dma_start(wraw[:].rearrange("q k n -> q (k n)"), wconv).then_inc(wconv_in, 16)
            for g in range(4):
                by_dve_relu = sum(o < 4 * (g + 1) for o in RELU_DVE)
                sp.wait_ge(f_out, 4 * (g + 1) - by_dve_relu)
                sp.wait_ge(f_out_dve, by_dve_relu)
                sp.dma_start(out[:, 512 * g:512 * (g + 1)],
                             fo[:, 4 * g:4 * g + 4, :].rearrange("q o n -> q (o n)")).then_inc(stored, 16)
            sp.wait_ge(stored, 64)

        @block.tensor
        def _(pe):
            mm = nc.tensor.matmul

            pe.wait_ge(warm_zero, 1)
            for _ in range(WARM):
                mm(ps[:, 6, :], warm[:, 0:128], warm, start=True, stop=True)

            def project_first(kind):
                o = slot((kind, 0))
                w0 = 0 if kind == "B" else 128
                for h in range(2):
                    cols = slice(512 * h, 512 * h + 512)
                    mm(o[:, cols], whalf[:, w0:w0 + 128], xd[:, 0, cols], start=True, stop=True)\
                        .then_inc(first_ready, 1)

            def wait_slot(n):
                if n >= 3:
                    if n < 5:
                        pe.wait_ge(first_act, 2 * (n - 2))
                    elif uses[n - 3][0] == "D":
                        pe.wait_ge(d_done, by_dve[n - 3])
                    else:
                        pe.wait_ge(act_step, by_act[n - 3])

            def project(n, kind, b):
                if kind == "B" and b >= PLAIN:
                    pe.wait_ge(x_top, b - PLAIN + 1)
                    pe.wait_ge(x_parts, b - PLAIN + 1)
                    pe.wait_ge(w_parts, 4)
                elif b == 1:
                    pe.wait_ge(x_in[1], 32)
                wait_slot(n)
                o = slot((kind, b))
                if kind == "D":
                    if b == 0:
                        pe.wait_ge(w_half, 3)
                    for t in range(JT):
                        cols = slice(128 * t, 128 * t + 128)
                        v = o[:, 64 * t:64 * t + 64]
                        if b < PLAIN:
                            last = mm(v, xd[:, b, cols], whalf[:, 320:384], start=True, stop=True)
                            continue
                        mm(v, x12[:, b - PLAIN, cols], w11[:, 320:384], start=True, stop=False)
                        mm(v, x12[:, b - PLAIN, cols], w22[:, 320:384], start=False, stop=False)
                        last = mm(v, x13[:, b - PLAIN, cols], w31[:, 320:384], start=False, stop=True)
                    last.then_inc(d_ready, 1)
                    return
                w0 = 0 if kind == "B" else 128
                for h in range(2):
                    cols = slice(512 * h, 512 * h + 512)
                    if b < PLAIN:
                        last = mm(o[:, cols], whalf[:, w0:w0 + 128], xd[:, b, cols], start=True, stop=True)
                        continue
                    mm(o[:, cols], w11[:, w0:w0 + 128], x12[:, b - PLAIN, cols], start=True, stop=False)
                    mm(o[:, cols], w22[:, w0:w0 + 128], x12[:, b - PLAIN, cols], start=False, stop=False)
                    last = mm(o[:, cols], w31[:, w0:w0 + 128], x13[:, b - PLAIN, cols], start=False, stop=True)
                last.then_inc(bc_ready, 1)

            def scores(n, g):
                b, t = divmod(g, JT)
                if g == 0:
                    pe.wait_ge(first_act, 2)
                    pe.wait_ge(bhalf_ready, 1)
                elif g == DIRECT or t == 0:
                    for s in (b_hi, b_mid, b_lo, b_rep, c_top, c_hi, c_mid, c_lo):
                        pe.wait_ge(s, b + 1)
                wait_slot(n)
                if g < DIRECT:
                    for h in range(2):
                        cols = slice(512 * h, 512 * h + 512)
                        last = mm(slot(("S", g))[:, cols], bhalf[:, 128 * g:128 * g + 128], c32[:, cols],
                                  start=True, stop=True)
                    last.then_inc(s_ready, 1)
                    return
                o = slot(("S", g))
                j = slice(128 * t, 128 * t + 128)
                for w, m in ((b11, c12), (b22, c12), (b31, c13)):
                    for h in range(2):
                        last = mm(o[:, 512 * h:512 * h + 512], w[:, b % 2, j], m[:, b % 2, 512 * h:512 * h + 512],
                                  start=w is b11, stop=w is b31)
                last.then_inc(s_ready, 1)

            def values(g):
                b, t = divmod(g, JT)
                y = ps[:, 6 + b % 2, :]
                if t == 0:
                    if b >= 2:
                        pe.wait_ge(gen[0], b - 1)
                    terms = [(whalf, xd[:, b, :])] if b < PLAIN else \
                        [(w, m[:, b - PLAIN, :]) for w, m in ((w11, x12), (w22, x12), (w31, x13))]
                    for n, (w, m) in enumerate(terms):
                        for p in range(2):
                            mm(y[64 * p:64 * p + 64, :], w[:, 256:320], m[:, 512 * p:512 * p + 512],
                               start=n == 0, stop=False)
                pe.wait_ge(dz_ready, g + 1)
                for p in range(2):
                    last = mm(y[64 * p:64 * p + 64, :], dz[:, g % 4, :], probs[:, g % 3, 512 * p:512 * p + 512],
                              start=False, stop=t == JT - 1)
                last.then_inc(pv_done, 1)

            pe.wait_ge(x_in[0], 32)
            pe.wait_ge(w_half, 1)
            project_first("C")
            project_first("B")
            pe.wait_ge(w_sum, 2)
            mm(ps[:, 7, 0:64], wsrc[0:64, 0:128], wsp[0:64, 256:320], start=True, stop=True)
            mm(ps[:, 7, 64:128], b3b[0:64, :], wsp[0:64, 256:320], start=True, stop=True).then_inc(w_fold, 1)
            for n, (kind, i) in enumerate(uses):
                if n < 2:
                    continue
                if kind == "S":
                    scores(n, i)
                    if i >= LAG:
                        values(i - LAG)
                else:
                    project(n, kind, i)

            def convolve(k, b, i):
                bank = ps[:, BANKS[k % 2][b], :]
                nbw = 3 if k < 2 else 2
                last_part = 2 if k < 3 else 0
                n = NB * k + b
                if k == 3:
                    pe.wait_ge(q_ready, 3 * (b + 1))
                else:
                    pe.wait_ge(main_done[i], n + 1)
                for kh in range(3):
                    mm(bank, wq[:, k, kh, :], parts[:, i, b, 0, S2 * kh:S2 * kh + HALF],
                       start=i == 0 and kh == 0, stop=False)
                if i == 1:
                    pe.wait_ge(side_done[0], 2 * (n + 1))
                    pe.wait_ge(side_done[1], 2 * (n + 1))
                    for kh in range(nbw):
                        for half in range(2):
                            o = slice(64 * (1 - half), 64 * (1 - half) + 64)
                            mm(bank[o], wside[:, k, kh, half, :], parts[:, half, b, 1, S2 * kh:S2 * kh + HALF],
                               start=False, stop=False)
                elif i == last_part:
                    if k < 3:
                        pe.wait_ge(side_done[2], 2 * (n + 1))
                    for kh in range(nbw):
                        last = mm(bank, wq[:, k, 3 + kh, :], parts[:, 2, b, 1, S2 * kh:S2 * kh + HALF],
                                  start=False, stop=kh == nbw - 1)
                if i == last_part:
                    last.then_inc(conv_done[k], 1)

            def keep_busy(n, bank):
                for _ in range(n):
                    mm(ps[:, bank, :], ident_bf[:], wq[:, 0, 0:4, :].rearrange("q a n -> q (a n)"),
                       start=True, stop=True)

            def average(k):
                spare = BANKS[1 - k][3]
                keep_busy(4, spare)
                pe.wait_ge(bn_mv[k], 1)
                mm(ps[:, BANKS[1 - k][0], 0:2], consts[:, K_AVG2:K_AVG2 + 128], mv[:, k, :],
                   start=True, stop=True).then_inc(bn_avg[k], 1)
                keep_busy((9, 15)[k], spare)

            pe.wait_ge(wq_ready[0], 9)
            pe.wait_ge(borders_zero, 1)
            pe.wait_ge(id_ready, 1)
            pe.wait_ge(gen[0], NB - 1)
            convolve(0, 0, 0)
            convolve(0, 0, 1)
            values(NB * JT - 2)
            convolve(0, 0, 2)
            values(NB * JT - 1)
            pe.wait_ge(act_step, act_after[("S", NB * JT - 1)])
            for b in range(1, NB):
                for i in range(3):
                    convolve(0, b, i)
            average(0)
            pe.wait_ge(wq_ready[1], 9)
            for b, i in ORDER_1:
                convolve(1, b, i)
            average(1)
            pe.wait_ge(wq_ready[2], 11)
            pe.wait_ge(wq_ready[3], 7)
            pe.wait_ge(skew_zero, 2)
            for k, b, i in ORDER_2:
                convolve(k, b, i)

            pe.wait_ge(wp_ready, 1)
            pe.wait_ge(id_ready, 1)

            def residual(b, s):
                col = xi[:, b, :].rearrange("q (r s) -> q r s", s=S2)[:, :, s]
                pick = ident_bf[:].rearrange("q (p o x) -> q p o x", p=2, x=BOX)
                for x_ in range(BOX):
                    last = mm(ps[32 * x_:32 * x_ + 32, BANKS[1][b], 32 * s:32 * s + 32], col, pick[:, :, :, x_],
                              start=True, stop=True)
                return last

            def bottleneck(b):
                pe.wait_ge(xi_ready, b + 1)
                for i in range(3):
                    last = mm(ps[32 * b:32 * b + 32, H_BANK, :], wp[:, i, :], xi[:, b, :], start=i == 0, stop=i == 2)
                return last

            def residuals(b, h):
                for s in range(8 * h, 8 * h + 8):
                    last = residual(b, s)
                last.then_inc(xt_ready, 1)

            bottleneck(0)
            convolve(3, 2, 0)
            residuals(0, 0)
            convolve(3, 3, 0)
            residuals(0, 1)
            bottleneck(1)
            bottleneck(2)
            keep_busy(5, BANKS[0][3])
            bottleneck(3).then_inc(h_raw, 1)
            residuals(1, 0)
            residuals(1, 1)
            pe.wait_ge(h_mv, 1)
            mm(ps[:, AVG_BANK, 0:2], consts[:, K_AVG8:K_AVG8 + 128], hmv[:], start=True, stop=True).then_inc(h_avg, 1)
            keep_busy(3, BANKS[0][3])
            pe.wait_ge(h_var, 1)
            mm(ps[:, HT_BANK, 0:1], consts[:, K_AVG8:K_AVG8 + 128], h_v[:], start=True, stop=True).then_inc(h_vavg, 1)
            residuals(2, 0)
            residuals(2, 1)
            keep_busy(3, BANKS[0][3])
            pe.wait_ge(h_ready, 1)
            for sq in range(4):
                cols = slice(128 * sq, 128 * sq + 128)
                last = mm(ps[:, HT_BANK, cols], hs[:, cols], consts[:, K_ID:K_ID + 128], start=True, stop=True)
            last.then_inc(tr_ready, 1)
            residuals(3, 0)
            residuals(3, 1)
            keep_busy(2, BANKS[0][3])
            pe.wait_ge(hblk_act, 2)
            pe.wait_ge(hblk_dve, 2)
            pe.wait_ge(rows_ready, 1)
            pe.wait_ge(cols_placed, NB)

            def box_rows(g):
                pe.wait_ge(xf_ready, g + 1)
                for o in range(4 * g, 4 * g + 4):
                    last = mm(ps[:, BANKS[1][g], 128 * (o % 4):128 * (o % 4) + 128], hblk[:, o, :], rows_w[:, o, :],
                              start=True, stop=True)
                last.then_inc(t_ready, 1)

            def box_columns(g):
                pe.wait_ge(ts_act, g + 1)
                for o in range(4 * g, 4 * g + 4):
                    for x_ in range(BOX):
                        last = mm(ps[32 * x_:32 * x_ + 32, BANKS[0][g], 128 * (o % 4):128 * (o % 4) + 128],
                                  ts[:, o, 32 * x_:32 * x_ + 32],
                                  cols_blk[:, BOX * o + x_].rearrange("q b j -> q (b j)"), start=True, stop=True)
                last.then_inc(f_ready, 1)

            box_rows(0)
            box_rows(1)
            box_columns(0)
            box_rows(2)
            box_columns(1)
            box_rows(3)
            box_columns(2)
            box_columns(3)
            pe.wait_ge(f_stat, 1)
            avg, means, variances = consts[:, K_AVGQ:K_AVGQ + 128], ps[:, BANKS[1][0], 0:OC], ps[:, BANKS[1][1], 0:OC]
            mm(means, avg, st2[:, :, 1], start=True, stop=False)
            mm(means, avg, st2[:, :, 4], start=False, stop=True).then_inc(f_avg, 1)
            mm(variances, avg, st2[:, :, 2], start=True, stop=False)
            mm(variances, avg, st2[:, :, 5], start=False, stop=False)
            pe.wait_ge(f_sqr, 1)
            mm(variances, avg, f_sq[:, :, 0], start=False, stop=False)
            mm(variances, avg, f_sq[:, :, 1], start=False, stop=True).then_inc(f_vavg, 1)

        @block.scalar
        def _(act):
            act.dma_start(wsp[:, 0:256], wa[:, 0:256]).then_inc(wa_in, 16)
            act.dma_start(parm[:], par).then_inc(par_in, 16)
            act.dma_start(wsrc[:], wa[:, 256:512]).then_inc(wsrc_in, 16)

            def run(o, i, f, **kw):
                return nc.scalar.activation(o, i, f, **kw)

            def x_first(b):
                act.wait_ge(x_in[b], 32)
                run(x13[:, b - PLAIN, :], xd[:, b, :], ACT.Copy).then_inc(x_cast, 1)

            def first_out(kind, h):
                cols = slice(512 * h, 512 * h + 512)
                act.wait_ge(first_ready, 1 + h + 2 * (kind == "B"))
                o = slot((kind, 0))[:, cols]
                if kind == "C":
                    act.wait_ge(biases, 2)
                    run(c32[:, cols], o, ACT.Identity, bias=nb2[:], scale=-1.0).then_inc(first_act, 1)
                else:
                    run(b32[:, cols], o, ACT.Identity, bias=parm[:, P_B1:P_B1 + 1]).then_inc(first_act, 1)

            def b_out(b):
                act.wait_ge(b_res, b)
                act.wait_ge(bc_ready, 2 * b - 1)
                run(b32[:], slot(("B", b)), ACT.Identity, bias=parm[:, P_B1:P_B1 + 1]).then_inc(act_step, 1)
                act.wait_ge(act_step, act_after[("B", b)])
                run(b11[:, b % 2, :], b32[:], ACT.Copy).then_inc(b_hi, 1)

            def b_repeat(b):
                run(b31[64:128, b % 2, :], b32[64:128, :], ACT.Copy).then_inc(b_rep, 1)

            def c_out(b):
                act.wait_ge(c_res, b)
                act.wait_ge(bc_ready, 2 * b)
                run(c32[:], slot(("C", b)), ACT.Identity, bias=nb2[:], scale=-1.0).then_inc(act_step, 1)

            def c_repeat(b):
                act.wait_ge(act_step, act_after[("C", b)])
                run(c12[0:64, b % 2, :], c32[0:64, :], ACT.Copy).then_inc(c_top, 1)

            def exponentials(g):
                act.wait_ge(max_ready, g + 1)
                if g >= 3:
                    act.wait_ge(pv_done, g - 2)
                run(probs[:, g % 3, :], slot(("S", g)), ACT.Exp, bias=nmax[:, g:g + 1], scale=-1.0,
                    accum_out=zsum[:, g:g + 1]).then_inc(act_step, 1)

            def image_out(k, b, src, func, **kw):
                run(main(0, b), src, func, **kw).then_inc(main_done[0], 1)
                run(y_of[k][:, b, :], src, func, **kw).then_inc(gen[k], 1)

            def block0_out(b):
                act.wait_ge(pv_done, JT * (b + 1))
                image_out(0, b, ps[:, 6 + b % 2, :], ACT.Identity, bias=bd[:])

            act.wait_ge(warm_zero, 1)
            run(zsum[:, 0:1], warm[:, 0:1], ACT.Exp)
            act.wait_ge(par_in, 16)
            first_out("C", 0)
            first_out("C", 1)
            first_out("B", 0)
            first_out("B", 1)
            act.wait_ge(first_act, 4)
            run(c12[0:64, 0, :], c32[0:64, :], ACT.Copy).then_inc(c_top, 1)
            run(b11[:, 0, :], b32[:], ACT.Copy).then_inc(b_hi, 1)
            run(b31[64:128, 0, :], b32[64:128, :], ACT.Copy).then_inc(b_rep, 1)
            for kind, i in uses:
                if kind != "S":
                    continue
                b, t = divmod(i, JT)
                if t == (3 if b == 0 else 0) and b + 2 < NB:
                    x_first(b + 2)
                exponentials(i)
                if b + 1 < NB:
                    if t == b_after(b):
                        b_out(b + 1)
                    if t == c_after(b):
                        c_out(b + 1)
                        b_repeat(b + 1)
                    if t == c_after(b) + 1:
                        c_repeat(b + 1)
                if t == 4 and b >= 1:
                    block0_out(b - 1)
                if i == NB * JT - 3:
                    act.wait_ge(wconv_in, 16)
                    run(wraw[:, 2:4, 0:512], wraw[:, 2:4, 0:512], ACT.Tanh).then_inc(tanh_done, 1)
            block0_out(NB - 1)
            act.wait_ge(ev_var, 1)
            run(ev_rstd[:], ev_var_r[:], ACT.Sqrt).then_inc(ev_sqrt, 1)

            act.wait_ge(bn_var[0], 1)
            run(bn_rstd[:, 0:1], bn_recip[:, 0:1], ACT.Sqrt).then_inc(bn_sqrt[0], 1)
            act.wait_ge(bn_ready[0], 2)
            for b in range(NB):
                image_out(1, b, ps[:, BANKS[0][b], :], ACT.Relu, bias=bn_b[:, 0:1], scale=bn_a[:, 0:1])
            act.wait_ge(cols_ready, 1)
            for b in range(NB):
                run(cols_blk[:, :, b, :], box_t[:, 2, :].rearrange("q (k j) -> q k j", j=W), ACT.Copy,
                    scale=consts[:, K_MASK + b:K_MASK + b + 1]).then_inc(cols_placed, 1)
            act.wait_ge(bn_var[1], 1)
            run(bn_rstd[:, 1:2], bn_recip[:, 1:2], ACT.Sqrt).then_inc(bn_sqrt[1], 1)
            act.wait_ge(bn_ready[1], 2)
            act.wait_ge(ev_ready, 1)

            def inner(b):
                act.wait_ge(conv_done[2], b + 1)
                if b < 2:
                    act.wait_ge(gen[2], b + 3)
                else:
                    act.wait_ge(q_ready, 3 * (b - 1))
                run(tmp[:, b % 2, :], ps[:, BANKS[0][b], :], ACT.Relu, bias=ev_bias[:, 0:1], scale=ev_scale[:, 0:1])\
                    .then_inc(q_relu, 1)

            def outer_out(b):
                act.wait_ge(sum_ready, b + 1)
                image_out(2, b, tmp[:, b % 2, :], ACT.Relu, bias=bn_b[:, 1:2])
                act.wait_ge(main_done[0], 2 * NB + b + 1)
                for half in range(2):
                    o, moved = side(0, b, half, True)
                    run(o, moved(main(0, b)), ACT.Copy).then_inc(side_done[0], 1)

            def third_sides(b):
                act.wait_ge(main_done[2], 2 * NB + b + 1)
                for half in range(2):
                    o, moved = side(2, b, half, True)
                    run(o, moved(main(2, b)), ACT.Copy).then_inc(side_done[2], 1)

            def scaled(b):
                act.wait_ge(gen[2], b + 1)
                run(x15[:, b, :], y3[:, b, :], ACT.Identity, bias=ev_bias[:, 1:2], scale=LEVELS)\
                    .then_inc(x15_ready, 1)

            outer_out(0)
            outer_out(1)
            outer_out(2)
            scaled(0)
            inner(0)
            outer_out(3)
            scaled(1)
            scaled(2)
            third_sides(2)
            inner(1)
            scaled(3)
            third_sides(3)
            inner(2)
            inner(3)

            def x_out(b):
                act.wait_ge(xt_ready, 2 * (b + 1))
                run(xf[:, :, 32 * b:32 * b + 32], ps[:, BANKS[1][b], :].rearrange("q (j o) -> q o j", o=OC), ACT.Copy,
                    scale=1.0 / LEVELS).then_inc(xf_ready, 1)

            def rows_out(g):
                act.wait_ge(t_ready, g + 1)
                run(ts[:, 4 * g:4 * g + 4, :].rearrange("q o n -> q (o n)"), ps[:, BANKS[1][g], :], ACT.Copy)\
                    .then_inc(ts_act, 1)

            x_out(0)
            x_out(1)
            act.wait_ge(h_ve, 1)
            run(h_rstd[:], h_recip[:], ACT.Sqrt).then_inc(h_sqrt, 1)
            act.wait_ge(h_ab, 2)
            run(hs[:].rearrange("q (s r) -> q r s", r=H), ps[:, H_BANK, :].rearrange("q (r s) -> q r s", s=S2),
                ACT.Relu, bias=h_b[:], scale=h_a[:]).then_inc(h_ready, 1)
            x_out(2)
            act.wait_ge(hblk_zero, 1)
            act.wait_ge(tr_ready, 1)
            for q in range(2):
                rows = slice(32 * q, 32 * q + 32)
                run(hblk[rows, :, rows], ps[rows, HT_BANK, :].rearrange("q (m o) -> q o m", o=OC), ACT.Copy)\
                    .then_inc(hblk_act, 1)
            x_out(3)
            for g in range(4):
                rows_out(g)
            act.wait_ge(f_ve, 1)
            run(f_rstd[:], f_recip[:], ACT.Sqrt).then_inc(f_sqrt, 1)
            act.wait_ge(f_bias, 1)
            for o in range(OC):
                if o not in RELU_DVE:
                    act.wait_ge(f_add, o + 1)
                    run(fo[:, o, :], fo[:, o, :], ACT.Relu, bias=f_b[:, o:o + 1]).then_inc(f_out, 1)

        @block.vector
        def _(dve):
            V = nc.vector
            links = [0]

            def link(ins):
                links[0] += 1
                ins.then_inc(chain, 1)
                dve.wait_ge(chain, links[0])

            V.memset(warm, 0.0).then_inc(warm_zero, 1)
            images = parts[:].rearrange("q i b a n -> q (i b a) n")
            shadows = parts[:, :, :, 1, :].rearrange("q i b (r s) -> q i b r s", s=S2)
            dve.wait_ge(warm_zero, 1)
            link(V.memset(images[:, :, 0:S2], 0.0))
            link(V.memset(images[:, :, PAD - S2:PAD], 0.0))
            link(V.memset(shadows[:, 0, :, :, S2 - 1], 0.0))
            link(V.memset(shadows[:, 1, :, :, 0], 0.0))
            link(V.memset(shadows[0:64, 2, :, :, S2 - 1], 0.0))
            V.memset(shadows[64:128, 2, :, :, 0], 0.0).then_inc(borders_zero, 1)
            dve.wait_ge(wa_in, 16)
            V.tensor_scalar(whalf[:, 0:256], wsp[:, 0:256], 0.5, None, ALU.mult).then_inc(w_half, 1)
            dve.wait_ge(par_in, 16)
            V.tensor_scalar(nb2[:], parm[:, P_B2:P_B2 + 1], -1.0, None, ALU.mult).then_inc(biases, 1)
            V.tensor_tensor(bd[:], parm[:, P_BD1:P_BD1 + 1], parm[:, P_BD2:P_BD2 + 1], ALU.add).then_inc(biases, 1)
            V.tensor_copy(b3b, parm[:, P_B3:P_B3 + 1].to_broadcast([128, 128])).then_inc(w_sum, 1)
            dve.wait_ge(wsrc_in, 16)
            V.tensor_tensor(wsp[:, 256:320], wsrc[:, 128:192], wsrc[:, 192:256], ALU.add).then_inc(w_sum, 1)
            dve.wait_ge(w_sum, 2)
            V.tensor_scalar(whalf[:, 256:320], wsp[:, 256:320], 0.5, None, ALU.mult).then_inc(w_half, 1)

            def x_top_copy(b):
                dve.wait_ge(x_in[b], 32)
                V.tensor_copy(x12[0:64, b - PLAIN, :], xd[0:64, b, :]).then_inc(x_top, 1)

            def x_middle(b):
                dve.wait_ge(x_res, b - PLAIN + 1)
                V.tensor_copy(x12[64:128, b - PLAIN, :], rx[64:128, :]).then_inc(x_mid, 1)

            def weight_parts():
                dve.wait_ge(w_fold, 1)
                alpha = parm[:, P_ALPHA:P_ALPHA + 1]
                link(V.tensor_scalar(wsp[:, 320:384], ps[:, 7, 0:64], alpha, None, ALU.mult))
                link(V.tensor_scalar(brow[:], ps[:, 7, 64:128], alpha, None, ALU.mult))
                V.tensor_scalar(whalf[:, 320:384], wsp[:, 320:384], 0.5, None, ALU.mult).then_inc(w_half, 1)
                V.tensor_copy(w11[:], wsp[:]).then_inc(w_parts, 1)
                dve.wait_ge(w_parts, 1)
                link(V.tensor_tensor(wr[:], wsp[:], w11[:], ALU.subtract))
                V.tensor_copy(w22[:], wr[:]).then_inc(w_parts, 1)
                dve.wait_ge(w_parts, 2)
                V.tensor_tensor(w31[0:64, :], wr[0:64, :], w22[0:64, :], ALU.subtract).then_inc(w_parts, 1)
                V.tensor_copy(w31[64:128, :], wsp[64:128, :]).then_inc(w_parts, 1)

            def b_middle(b):
                dve.wait_ge(b_res, b + 1)
                V.tensor_copy(b22[:, b % 2, :], rb[:]).then_inc(b_mid, 1)

            def c_first(b):
                if b:
                    dve.wait_ge(act_step, act_after[("C", b)])
                else:
                    dve.wait_ge(first_act, 2)
                V.tensor_copy(c13[:, b % 2, :], c32[:]).then_inc(c_hi, 1)

            def c_middle(b):
                dve.wait_ge(c_res, b + 1)
                V.tensor_copy(c12[64:128, b % 2, :], rc[64:128, :]).then_inc(c_mid, 1)

            def d_out(b):
                dve.wait_ge(d_ready, b + 1)
                if b >= 2:
                    dve.wait_ge(dz_ready, JT * (b - 1))
                V.tensor_tensor(d32[:, b % 2], slot(("D", b))[:, 0:512].rearrange("q (t c) -> q t c", c=C),
                                brow[:].unsqueeze(1).to_broadcast([128, JT, C]), ALU.add).then_inc(d_done, 1)

            def normalise(g):
                b, t = divmod(g, JT)
                dve.wait_ge(act_step, act_after[("S", g)])
                V.reciprocal(rz[:, g:g + 1], zsum[:, g:g + 1]).then_inc(rz_ready, 1)
                dve.wait_ge(rz_ready, g + 1)
                if t == 0:
                    dve.wait_ge(d_done, b + 1)
                if g >= 4:
                    dve.wait_ge(pv_done, g - 3)
                V.tensor_scalar(dz[:, g % 4, :], d32[:, b % 2, t, :], rz[:, g:g + 1], None, ALU.mult)\
                    .then_inc(dz_ready, 1)

            def side_copies(k, b, i):
                dve.wait_ge(main_done[i], NB * k + b + 1)
                for half in range(2):
                    o, moved = side(i, b, half, k == 2)
                    V.tensor_copy(o, moved(main(i, b))).then_inc(side_done[i], 1)

            def split_residual(k, b):
                n = NB * k + b
                dve.wait_ge(main_done[0], n + 1)
                dve.wait_ge(gen[k], b + 1)
                if n >= 2:
                    dve.wait_ge(side_done[2], 2 * (n - 1))
                V.tensor_tensor(res[:, b % 2, :], y_of[k][:, b, :], main(0, b), ALU.subtract).then_inc(r_done, 1)

            def split_second(k, b):
                dve.wait_ge(r_done, NB * k + b + 1)
                V.tensor_copy(main(1, b), res[:, b % 2, :]).then_inc(main_done[1], 1)
                side_copies(k, b, 1)

            def place_b(k, src, nbw):
                for half in range(2):
                    q = slice(64 * half, 64 * half + 64)
                    o = slice(64 * (1 - half), 64 * (1 - half) + 64)
                    yield wq[q, k, 3:3 + nbw, o], src[q, NA:NA + 64 * nbw].rearrange("q (a n) -> q a n", n=64)

            def side_weights(k):
                dve.wait_ge(wq_ready[k], 5)
                for half in range(2):
                    q, o = slice(64 * half, 64 * half + 64), slice(64 * (1 - half), 64 * (1 - half) + 64)
                    for to in (q, o):
                        V.tensor_copy(wside[to, k, :, half, :], wq[q, k, 3:6, o]).then_inc(wq_ready[k], 1)

            def lsq_scales():
                la = parm[:, P_LA:P_LA + 2]
                link(V.tensor_scalar(lsq_t[:], la, LSQ_G, None, ALU.mult))
                link(V.tensor_tensor(lsq[:], la, lsq_t[:], ALU.subtract))
                link(V.tensor_tensor(lsq[:], lsq_t[:], lsq[:], ALU.add))
                link(V.reciprocal(lsq_r[:], lsq[:]))
                link(V.tensor_tensor(lsq_sq[:], lsq[:], lsq[:], ALU.mult))
                link(V.tensor_tensor(lsq_gain[:], lsq[:], parm[:, P_L1G:P_L1G + 2], ALU.mult))
                link(V.tensor_scalar(ev_add[:], parm[:, P_L2V:P_L2V + 2], EPS, None, ALU.add))
                V.reciprocal(ev_var_r[:], ev_add[:]).then_inc(ev_var, 1)

            def lsq_round(k):
                dve.wait_ge(wconv_in, 16)
                dve.wait_ge(wq_zero, 1)
                w = wtmp[:, k, :]
                link(V.tensor_scalar(w, wraw[:, k, :], lsq_r[:, k:k + 1], QP, ALU.mult, ALU.min))
                link(V.tensor_scalar(w, w, QN, MAGIC, ALU.max, ALU.add))
                V.tensor_scalar(wq[:, k, 0:3, :], w[:, 0:NA].rearrange("q (a n) -> q a n", n=128), MAGIC, None,
                                ALU.subtract).then_inc(wq_ready[k], 3)

            def lsq_side(k):
                for o, i in place_b(k, wtmp[:, k, :], 3):
                    V.tensor_scalar(o, i, MAGIC, None, ALU.subtract).then_inc(wq_ready[k], 1)
                side_weights(k)

            def tanh_max():
                dve.wait_ge(tanh_done, 1)
                V.tensor_reduce(wmax[:], wraw[:, 2:4, 0:NA], AX.X, ALU.max, apply_absolute_value=True)\
                    .then_inc(wmax_part, 1)

            def tanh_scale():
                dve.wait_ge(wmax_done, 1)
                link(V.tensor_scalar(wden[:], wmax_all[:], 2.0, None, ALU.mult))
                link(V.reciprocal(wden[:], wden[:]))

            def tanh_weights(k):
                n = NA + 128
                w = wtmp[:, k - 2, 0:n]
                dve.wait_ge(wq_ready[k - 2], 5)
                link(V.tensor_scalar(w, wraw[:, k, 0:n], wden[:, k - 2:k - 1], 0.5, ALU.mult, ALU.add))
                link(V.tensor_scalar(w, w, LEVELS, MAGIC, ALU.mult, ALU.add))
                V.tensor_scalar(wq[:, k, 0:3, :], w[:, 0:NA].rearrange("q (a n) -> q a n", n=128), MAGIC,
                                LEVELS / 2, ALU.subtract, ALU.subtract).then_inc(wq_ready[k], 3)
                for o, i in place_b(k, w, 2):
                    V.tensor_scalar(o, i, MAGIC, LEVELS / 2, ALU.subtract, ALU.subtract).then_inc(wq_ready[k], 1)
                dve.wait_ge(wq_ready[k], 5)
                V.memset(wq[0:64, k, 0, 64:128], 0.0).then_inc(wq_ready[k], 1)
                V.memset(wq[64:128, k, 2, 0:64], 0.0).then_inc(wq_ready[k], 1)
                if k == 2:
                    side_weights(k)

            def clip_edges(i):
                v = edge_buf[i]
                dve.wait_ge(edge_sum, i + 1)
                V.tensor_scalar(v, v, 0.0, 1.0, ALU.max, ALU.min).then_inc(edge_clip, 1)

            def half_of_b():
                dve.wait_ge(first_act, 3)
                V.tensor_scalar(bhalf[:], b32[:, 0:128 * DIRECT], 0.5, None, ALU.mult).then_inc(bhalf_ready, 1)

            half_of_b()
            c_first(0)
            weight_parts()
            for kind, i in uses:
                if kind == "D":
                    d_out(i)
                if kind != "S":
                    continue
                b, t = divmod(i, JT)
                dve.wait_ge(s_ready, i + 1)
                V.tensor_reduce(nmax[:, i:i + 1], slot(("S", i)), AX.X, ALU.min).then_inc(max_ready, 1)
                if i >= 1:
                    normalise(i - 1)
                if i == 0:
                    c_middle(0)
                if i == 1:
                    b_middle(0)
                if b + 1 < NB:
                    if t == c_after(b) + 1:
                        c_first(b + 1)
                    if t == (3 if b == 0 else 2):
                        b_middle(b + 1)
                    if t == (5 if b == 0 else c_after(b) + 3):
                        c_middle(b + 1)
                if b + 2 < NB:
                    if t == (5 if b == 0 else 0):
                        x_top_copy(b + 2)
                    elif t == (6 if b == 0 else 1):
                        x_middle(b + 2)
                if b >= 1:
                    if t == 5:
                        side_copies(0, b - 1, 0)
                    elif t == 6:
                        split_residual(0, b - 1)
                    elif t == 7:
                        split_second(0, b - 1)
                if i == 8:
                    lsq_scales()
                if i == 16:
                    lsq_round(0)
                if i == 16:
                    lsq_side(0)
                if i == 25:
                    lsq_round(1)
                if i == 26:
                    lsq_side(1)
                if i >= NB * JT - 4:
                    clip_edges(i - (NB * JT - 4))
            normalise(NB * JT - 1)
            side_copies(0, NB - 1, 0)
            split_residual(0, NB - 1)
            split_second(0, NB - 1)
            tanh_max()
            side_copies(0, NB - 1, 2)
            tanh_scale()
            tanh_weights(2)

            def normalisation(k):
                c = slice(k, k + 1)
                avg = ps[:, BANKS[1 - k][0], 0:2]
                V.bn_aggr(mv[:, k, :], st[:, k].rearrange("q b n -> q (b n)")).then_inc(bn_mv[k], 1)
                dve.wait_ge(bn_avg[k], 1)
                dve.wait_ge(bn_mv[k], 1)
                link(V.tensor_tensor(bn_dev[:, c], mv[:, k, 0:1], avg[:, 0:1], ALU.subtract))
                link(V.scalar_tensor_tensor(bn_v[:, c], bn_dev[:, c], bn_dev[:, c], avg[:, 1:2], ALU.mult, ALU.add))
                link(V.tensor_scalar(bn_v[:, c], bn_v[:, c], lsq_sq[:, c], EPS, ALU.mult, ALU.add))
                V.reciprocal(bn_recip[:, c], bn_v[:, c]).then_inc(bn_var[k], 1)
                link(V.scalar_tensor_tensor(bn_mg[:, c], avg[:, 0:1], -1.0, lsq_gain[:, c], ALU.mult, ALU.mult))
                dve.wait_ge(bn_sqrt[k], 1)
                V.tensor_tensor(bn_a[:, c], bn_rstd[:, c], lsq_gain[:, c], ALU.mult).then_inc(bn_ready[k], 1)
                V.scalar_tensor_tensor(bn_b[:, c], bn_mg[:, c], bn_rstd[:, c], parm[:, P_L1B + k:P_L1B + k + 1],
                                       ALU.mult, ALU.add).then_inc(bn_ready[k], 1)
                dve.wait_ge(bn_ready[k], 2)

            def inner_normalisation():
                eg, eb, em = (parm[:, p:p + 2] for p in (P_L2G, P_L2B, P_L2M))
                dve.wait_ge(ev_sqrt, 1)
                link(V.tensor_tensor(ev_gain[:], ev_rstd[:], eg, ALU.mult))
                link(V.tensor_tensor(ev_shift[:], em, ev_gain[:], ALU.mult))
                link(V.tensor_tensor(ev_add[:], eb, ev_shift[:], ALU.subtract))
                link(V.tensor_scalar(ev_bias[:], ev_add[:], LEVELS, None, ALU.mult))
                link(V.tensor_scalar(ev_scale[:, 0:1], ev_gain[:, 0:1], 2.0, None, ALU.mult))
                V.tensor_scalar(ev_scale[:, 1:2], ev_gain[:, 1:2], 2.0 / LEVELS, None, ALU.mult).then_inc(ev_ready, 1)
                dve.wait_ge(ev_ready, 1)

            def link_stats(k, b):
                dve.wait_ge(conv_done[k], b + 1)
                link(V.bn_stats(st[:, k, b, :], ps[:, BANKS[k][b], :]))

            for b in range(NB - 1):
                link_stats(0, b)
            inner_normalisation()
            link_stats(0, 3)
            normalisation(0)
            for b in range(NB):
                side_copies(1, b, 0)
                split_residual(1, b)
                split_second(1, b)
                if b:
                    side_copies(1, b - 1, 2)
            side_copies(1, NB - 1, 2)
            tanh_weights(3)
            link_stats(1, 0)
            link_stats(1, 1)
            link_stats(1, 2)
            link_stats(1, 3)
            V.memset(shadows[:, 1, :, RP - 2, :], 0.0).then_inc(skew_zero, 1)
            V.memset(shadows[64:128, 2, :, RP - 2, :], 0.0).then_inc(skew_zero, 1)
            normalisation(1)

            def add_residual(b):
                if b >= 2:
                    dve.wait_ge(gen[2], b - 1)
                V.scalar_tensor_tensor(tmp[:, b % 2, :], ps[:, BANKS[1][b], :], bn_a[:, 1:2], y1[:, b, :],
                                       ALU.mult, ALU.add).then_inc(sum_ready, 1)

            def round_inner(b):
                v = tmp[:, b % 2, :]
                dve.wait_ge(q_relu, b + 1)
                V.tensor_scalar(q_in[:, b % 2, :], v, MAGIC, MAGIC, ALU.add, ALU.subtract).then_inc(q_int, 1)
                dve.wait_ge(q_int, b + 1)
                v = q_in[:, b % 2, :]
                V.tensor_scalar(main(0, b), v, LEVELS, None, ALU.min).then_inc(q_ready, 1)
                for half in range(2):
                    o, moved = side(2, b, half, True)
                    V.tensor_scalar(o, moved(v), LEVELS, None, ALU.min).then_inc(q_ready, 1)

            def outer(b):
                v = tmpo[:, b % 2, :]
                dve.wait_ge(conv_done[3], b + 1)
                dve.wait_ge(x15_ready, b + 1)
                link(V.scalar_tensor_tensor(v, ps[:, BANKS[1][b], :], ev_scale[:, 1:2], x15[:, b, :],
                                            ALU.mult, ALU.add))
                link(V.tensor_scalar(xi[:, b, :], v, MAGIC, MAGIC, ALU.add, ALU.subtract))
                V.tensor_scalar(xi[:, b, :], xi[:, b, :], 0.0, LEVELS, ALU.max, ALU.min).then_inc(xi_ready, 1)

            def split_two(b):
                split_residual(2, b)
                split_second(2, b)

            add_residual(0)
            add_residual(1)
            split_two(0)
            add_residual(2)
            split_two(1)
            add_residual(3)
            split_two(2)
            round_inner(0)
            split_two(3)
            round_inner(1)
            outer(0)
            round_inner(2)
            outer(1)
            round_inner(3)
            outer(2)
            outer(3)

            dve.wait_ge(h_raw, 1)
            link(V.bn_stats(hst[:], ps[:, H_BANK, :]))
            V.bn_aggr(hmv[:], hst[:]).then_inc(h_mv, 1)
            dve.wait_ge(h_avg, 1)
            dve.wait_ge(h_mv, 1)
            link(V.tensor_tensor(h_dev[:], hmv[:, 0:1], ps[:, AVG_BANK, 0:1], ALU.subtract))
            V.scalar_tensor_tensor(h_v[:], h_dev[:], h_dev[:], hmv[:, 1:2], ALU.mult, ALU.add).then_inc(h_var, 1)
            link(V.tensor_scalar(h_gain[:], parm[:, P_G1:P_G1 + 1], 1.0 / LEVELS, None, ALU.mult))
            link(V.scalar_tensor_tensor(h_mg[:], ps[:, AVG_BANK, 0:1], -1.0, h_gain[:], ALU.mult, ALU.mult))
            dve.wait_ge(h_vavg, 1)
            link(V.tensor_scalar(h_ve_t[:], ps[:, HT_BANK, 0:1], LEVELS ** -2, EPS, ALU.mult, ALU.add))
            V.reciprocal(h_recip[:], h_ve_t[:]).then_inc(h_ve, 1)
            dve.wait_ge(h_sqrt, 1)
            V.tensor_tensor(h_a[:], h_rstd[:], h_gain[:], ALU.mult).then_inc(h_ab, 1)
            V.scalar_tensor_tensor(h_b[:], h_mg[:], h_rstd[:], parm[:, P_BT1:P_BT1 + 1], ALU.mult, ALU.add)\
                .then_inc(h_ab, 1)
            dve.wait_ge(hblk_zero, 1)
            dve.wait_ge(tr_ready, 1)
            for q in range(2, 4):
                rows = slice(32 * q, 32 * q + 32)
                V.tensor_copy(hblk[rows, :, rows], ps[rows, HT_BANK, :].rearrange("q (m o) -> q o m", o=OC))\
                    .then_inc(hblk_dve, 1)
            for o in range(OC):
                if o % 4 == 0:
                    dve.wait_ge(f_ready, o // 4 + 1)
                last = V.bn_stats(st2[:, o, :], ps[:, BANKS[0][o // 4], 128 * (o % 4):128 * (o % 4) + 128])
            last.then_inc(f_stat, 1)
            dve.wait_ge(f_avg, 1)
            dve.wait_ge(f_stat, 1)
            link(V.tensor_copy(f_mean[:], ps[:, BANKS[1][0], 0:OC]))
            link(V.tensor_tensor(f_dev[:], st2[:, :, 1:5:3], f_mean[:].unsqueeze(2).to_broadcast([128, OC, 2]),
                                 ALU.subtract))
            V.scalar_tensor_tensor(f_sq[:], f_dev[:], 64.0, f_dev[:], ALU.mult, ALU.mult).then_inc(f_sqr, 1)
            link(V.scalar_tensor_tensor(f_mg[:], f_mean[:], -1.0, parm[:, P_G2:P_G2 + OC], ALU.mult, ALU.mult))
            dve.wait_ge(f_vavg, 1)
            link(V.tensor_scalar(f_v[:], ps[:, BANKS[1][1], 0:OC], 1.0 / 64, EPS, ALU.mult, ALU.add))
            V.reciprocal(f_recip[:], f_v[:]).then_inc(f_ve, 1)
            dve.wait_ge(f_sqrt, 1)
            V.tensor_tensor(f_a[:], f_rstd[:], parm[:, P_G2:P_G2 + OC], ALU.mult).then_inc(f_scale, 1)
            V.tensor_tensor(f_mgr[:], f_mg[:], f_rstd[:], ALU.mult).then_inc(f_scale, 1)
            dve.wait_ge(f_scale, 2)
            dve.wait_ge(xf_ready, NB)
            for o in range(OC):
                V.scalar_tensor_tensor(fo[:, o, :], ps[:, BANKS[0][o // 4], 128 * (o % 4):128 * (o % 4) + 128],
                                       f_a[:, o:o + 1], xf[:, o, :], ALU.mult, ALU.add).then_inc(f_add, 1)
                if o == 0:
                    V.tensor_tensor(f_b[:], f_mgr[:], parm[:, P_BT2:P_BT2 + OC], ALU.add).then_inc(f_bias, 1)
                if o - 1 in RELU_DVE:
                    dve.wait_ge(f_bias, 1)
                    dve.wait_ge(f_add, o)
                    V.tensor_scalar(fo[:, o - 1, :], fo[:, o - 1, :], f_b[:, o - 1:o], 0.0, ALU.add, ALU.max)\
                        .then_inc(f_out_dve, 1)

        @block.gpsimd
        def _(pool):
            G = nc.gpsimd
            links = [0]

            def link(ins):
                links[0] += 1
                ins.then_inc(pchain, 1)
                pool.wait_ge(pchain, links[0])

            G.memset(wq[:], 0.0).then_inc(wq_zero, 1)
            pool.wait_ge(wq_zero, 1)
            pool.wait_ge(cst_in, 16)
            G.tensor_copy(ident_bf[:], consts[:, K_ID:K_ID + 128]).then_inc(id_ready, 1)
            pool.wait_ge(id_ready, 1)

            def x_residual(b):
                pool.wait_ge(x_cast, b - PLAIN + 1)
                G.tensor_tensor(rx[64:128, :], xd[64:128, b, :], x13[64:128, b - PLAIN, :], ALU.subtract)\
                    .then_inc(x_res, 1)
                pool.wait_ge(x_res, b - PLAIN + 1)

            def x_third(b):
                pool.wait_ge(x_mid, b - PLAIN + 1)
                G.tensor_tensor(x13[64:128, b - PLAIN, :], rx[64:128, :], x12[64:128, b - PLAIN, :], ALU.subtract)\
                    .then_inc(x_parts, 1)
                pool.wait_ge(x_parts, b - PLAIN + 1)

            def b_residual(b):
                pool.wait_ge(b_hi, b + 1)
                G.tensor_tensor(rb[:], b32[:], b11[:, b % 2, :], ALU.subtract).then_inc(b_res, 1)
                pool.wait_ge(b_res, b + 1)

            def b_third(b):
                pool.wait_ge(b_mid, b + 1)
                G.tensor_tensor(b31[0:64, b % 2, :], rb[0:64, :], b22[0:64, b % 2, :], ALU.subtract)\
                    .then_inc(b_lo, 1)
                pool.wait_ge(b_lo, b + 1)

            def c_residual(b):
                pool.wait_ge(c_hi, b + 1)
                G.tensor_tensor(rc[64:128, :], c32[64:128, :], c13[64:128, b % 2, :], ALU.subtract)\
                    .then_inc(c_res, 1)
                pool.wait_ge(c_res, b + 1)

            def c_third(b):
                pool.wait_ge(c_mid, b + 1)
                G.tensor_tensor(c13[64:128, b % 2, :], rc[64:128, :], c12[64:128, b % 2, :], ALU.subtract)\
                    .then_inc(c_lo, 1)
                pool.wait_ge(c_lo, b + 1)

            def third_part(k, b):
                n = NB * k + b
                pool.wait_ge(main_done[1], n + 1)
                G.tensor_tensor(main(2, b), res[:, b % 2, :], main(1, b), ALU.subtract).then_inc(main_done[2], 1)
                pool.wait_ge(main_done[2], n + 1)
                for half in range(2 if gpsimd_sides(k, b) else 0):
                    o, moved = side(2, b, half, k == 2)
                    G.tensor_tensor(o, moved(res[:, b % 2, :]), moved(main(1, b)), ALU.subtract)\
                        .then_inc(side_done[2], 1)
                    pool.wait_ge(side_done[2], 2 * n + 1 + half)

            def edge(i, offset, table):
                G.tensor_tensor(edge_buf[i].rearrange("q (k j) -> q k j", j=W),
                                parm[:, offset:offset + C].unsqueeze(2).to_broadcast([128, C, W]),
                                consts[:, table:table + W].unsqueeze(1).to_broadcast([128, C, W]), ALU.add)\
                    .then_inc(edge_sum, 1)
                pool.wait_ge(edge_sum, i + 1)

            c_residual(0)
            b_residual(0)
            c_third(0)
            b_third(0)
            pool.wait_ge(par_in, 16)
            w1 = parm[:, P_W1:P_W1 + OC]
            link(G.memset(wp[:], 0.0))
            link(G.tensor_copy(w1p[:, 0, :], w1))
            link(G.tensor_tensor(w1f[:], w1, w1p[:, 0, :], ALU.subtract))
            link(G.tensor_copy(w1p[:, 1, :], w1f[:]))
            link(G.tensor_tensor(w1p[:, 2, :], w1f[:], w1p[:, 1, :], ALU.subtract))
            link(G.tensor_copy(wp[0:64, :, 0:OC], w1p[0:64]))
            G.tensor_copy(wp[64:128, :, OC:2 * OC], w1p[64:128]).then_inc(wp_ready, 1)
            pool.wait_ge(wp_ready, 1)

            b_residual(1)
            b_third(1)
            c_residual(1)
            x_residual(2)
            c_third(1)
            x_third(2)
            x_residual(3)
            b_residual(2)
            x_third(3)
            b_third(2)
            c_residual(2)
            c_third(2)
            third_part(0, 0)
            b_residual(3)
            b_third(3)
            c_residual(3)
            c_third(3)
            third_part(0, 1)
            edge(0, P_XMAX, K_IR1)
            edge(1, P_XMIN, K_IR)
            edge(2, P_YMAX, K_JW1)
            edge(3, P_YMIN, K_JW)
            third_part(0, 2)
            third_part(0, 3)
            pool.wait_ge(wmax_part, 1)
            G.partition_all_reduce(wmax_all[:], wmax[:], 128, bass.bass_isa.ReduceOp.max).then_inc(wmax_done, 1)
            pool.wait_ge(wmax_done, 1)
            pool.wait_ge(edge_clip, 2)
            G.tensor_tensor(edge_buf[0], edge_buf[0], edge_buf[1], ALU.subtract).then_inc(rows_ready, 1)
            pool.wait_ge(rows_ready, 1)
            pool.wait_ge(edge_clip, 4)
            G.tensor_tensor(edge_buf[3], edge_buf[2], edge_buf[3], ALU.subtract).then_inc(cols_ready, 1)
            pool.wait_ge(cols_ready, 1)
            pool.wait_ge(pv_done, NB * JT)
            G.memset(hblk[:], 0.0).then_inc(hblk_zero, 1)
            pool.wait_ge(hblk_zero, 1)
            for k in (1, 2):
                for b in range(NB):
                    third_part(k, b)


def constants():
    import numpy as np

    k = np.zeros((128, K_COLS), np.float32)
    q = np.arange(128)
    k[:, K_ID:K_ID + 128] = np.eye(128)
    k[:, K_AVG2:K_AVG2 + 128] = (q[:, None] % 64 == q[None] % 64) / 2
    k[:, K_AVG8:K_AVG8 + 128] = (q[:, None] % 16 == q[None] % 16) / 8
    k[:, K_AVGQ:K_AVGQ + 128] = (q[:, None] // 32 == q[None] // 32) / 64
    n = np.arange(32)
    r = q % 32
    w = 8 * (q // 8 % 4) + 2 * (q // 32) + q % 2
    k[:, K_IR:K_IR + 32] = n - r[:, None]
    k[:, K_IR1:K_IR1 + 32] = n - r[:, None] + 1
    k[:, K_JW:K_JW + 32] = n - w[:, None]
    k[:, K_JW1:K_JW1 + 32] = n - w[:, None] + 1
    k[:, K_MASK:K_MASK + 4] = (q[:, None] // 2 % 4) == np.arange(4)
    return k


def kernel(**inputs):
    import numpy as np
    import concourse.bacc as bacc
    from concourse.bass_utils import run_bass_kernel_spmd

    a = {n: np.asarray(v) for n, v in inputs.items()}
    x = a["x"].reshape(NB, C, H, S2, 2).transpose(1, 0, 4, 2, 3).reshape(C, NB * HW)

    def twice(m, axis=0):
        return np.concatenate([m, m], axis=axis)

    l0 = {n: a["L0_conv_" + n] for n in ("w1", "w2", "w3", "wd1", "wd2")}
    wa = np.concatenate([twice(twice(l0["w1"].T), 1), twice(twice(l0["w2"].T), 1), twice(twice(l0["w3"]), 1),
                         twice(l0["wd1"].T), twice(l0["wd2"].T)], axis=1)

    def taps(w, picks):
        t = w.transpose(1, 2, 3, 0)
        return np.concatenate([np.concatenate([t[:, kh, kw, :] for kh, kw in picks[p]], axis=1) for p in range(2)])

    col = {(0, 0): 1, (1, 0): 2, (0, 1): 0, (1, 1): 1}
    main = [[(kh, col[i, o]) for kh in range(3) for o in range(2)] for i in range(2)]
    side1 = [[(kh, 2) for kh in range(3)], [(kh, 0) for kh in range(3)]]
    side2 = [[(0, 2), (1, 2), (2, 2)], [(1, 0), (2, 0), (0, 0)]]
    wconv = np.concatenate([taps(a[n], [m + s for m, s in zip(main, side)]) for n, side in (
        ("L1_conv_w1", side1), ("L1_conv_w2", side1), ("L2_conv_w1", side2), ("L2_conv_w2", side2))], axis=1)

    def column(v, n=1):
        return np.tile(np.ravel(v), n)[:, None]

    def everywhere(v):
        return np.broadcast_to(np.ravel(v)[None], (128, np.size(v)))

    cols = [column(a["L0_conv_" + n], 2) for n in ("b1", "b2", "b3", "bd1", "bd2")]
    cols += [column(a[n], 128) for n in ("L0_conv_alpha", "L1_conv_alpha1", "L1_conv_alpha2")]
    cols += [column(a["L1_conv_" + n], 2) for n in ("gamma1", "gamma2", "beta1", "beta2")]
    cols += [column(a["L2_conv_" + n], 2) for n in (
        "gamma1", "gamma2", "beta1", "beta2", "mean1", "mean2", "var1", "var2")]
    cols += [column(a["L3_conv_" + n], 8) for n in ("g1", "b1")]
    cols += [np.repeat(a["L3_conv_" + n].reshape(OC, BOX).T, 32, axis=0) for n in ("g2", "b2")]
    cols += [everywhere(a["L3_conv_" + n]) for n in ("x_max", "x_min", "y_max", "y_min")]
    cols.append(twice(a["L3_conv_w1"].T))
    par = np.concatenate(cols, axis=1)

    sent = {"x": x, "wa": wa, "wconv": wconv, "par": par, "cst": constants()}
    sent = {n: np.ascontiguousarray(v) for n, v in sent.items()}
    nc = bacc.Bacc("TRN2", target_bir_lowering=False, num_devices=1)
    args = [nc.dram_tensor(n, v.shape, mybir.dt.from_np(v.dtype), kind="ExternalInput").ap() for n, v in sent.items()]
    args.append(nc.dram_tensor("out", (128, OC * 128), F32, kind="ExternalOutput").ap())
    build(nc, *args)
    r = run_bass_kernel_spmd(nc, [sent], core_ids=[0])
    got = r.results[0]["out"].reshape(BOX, H, OC, NB, W)
    return np.ascontiguousarray(got.transpose(3, 2, 0, 1, 4)).reshape(NB, C, H, W)
```
